# Optimizing a Trainium2 kernel written in Bass

```python
import numpy as np
import jax
import jax.numpy as jnp

def _softmax(x, axis=-1):
    return jax.nn.softmax(x, axis=axis)

def _gelu(x):
    return jax.nn.gelu(x, approximate=True)

def _silu(x):
    return jax.nn.silu(x)

def _sigmoid(x):
    return jax.nn.sigmoid(x)

def _layernorm(x, axis=-1, eps=1e-05):
    m = jnp.mean(x, axis=axis, keepdims=True)
    v = jnp.var(x, axis=axis, keepdims=True)
    return (x - m) / jnp.sqrt(v + eps)

def _scatter_add(tgt, idx, src, axis=0):
    return tgt.at[idx].add(src)

def _segment_sum(src, seg, n):
    return jax.ops.segment_sum(src, seg, n)
kernel_name = 'mk_perceiver_d1_seqx_r2_65d88d'

def setup_inputs(seed: int=0):
    np.random.seed(seed)
    _w = jnp.asarray

    def _rec_inputs():
        import jax
        import jax.numpy as jnp
        _rk = jax.random.key(seed)
        x = -0.0002928 + 1 * jax.random.normal(jax.random.fold_in(_rk, 1), (1, 512, 512), jnp.float32)
        _lenS = 512 - jax.random.randint(jax.random.fold_in(_rk, 7), (1,), 0, max(1, 512 // 4) + 1, jnp.int32)
        _lenS2 = 8192 - jax.random.randint(jax.random.fold_in(_rk, 8), (1,), 0, max(1, 8192 // 4) + 1, jnp.int32)
        _ctx_1024P = jax.random.normal(jax.random.fold_in(_rk, 11), (1, 16, 512), jnp.float32)
        _ctx_1024c = jax.random.dirichlet(jax.random.fold_in(_rk, 511), 0.3 * jnp.ones((16,), jnp.float32), (1, 8192))
        _ctx_1024t = jnp.einsum('bsk,bkd->bsd', _ctx_1024c, _ctx_1024P)
        _ctx_1024t = _ctx_1024t * jax.lax.rsqrt(jnp.mean(jnp.square(_ctx_1024t)) + 1e-12) * 0.953939
        ctx_1024 = -1.39393e-06 + 0.999914 * (_ctx_1024t + 0.3 * jax.random.normal(jax.random.fold_in(_rk, 611), (1, 8192, 512), jnp.float32))
        return (x, ctx_1024)
    x, ctx_1024 = _rec_inputs()

    def _L0_xattn_setup():
        import jax, jax.numpy as jnp
        import numpy as np
        EMB = 512
        DM = 64
        NH = 16
        key = jax.random.key(seed)
        ks = jax.random.split(key, 11)
        bs, slen = (2, 1024)
        s = 1.0 / np.sqrt(EMB)
        inp = {'Q': jax.random.normal(ks[0], (bs, slen, EMB), jnp.float32), 'K': jax.random.normal(ks[1], (bs, slen, EMB), jnp.float32), 'V': jax.random.normal(ks[2], (bs, slen, EMB), jnp.float32), 'Wq': jax.random.normal(ks[3], (EMB, DM * NH), jnp.float32) * s, 'bq': jnp.zeros((DM * NH,), jnp.float32), 'Wk': jax.random.normal(ks[4], (EMB, DM * NH), jnp.float32) * s, 'bk': jnp.zeros((DM * NH,), jnp.float32), 'Wv': jax.random.normal(ks[5], (EMB, DM * NH), jnp.float32) * s, 'bv': jnp.zeros((DM * NH,), jnp.float32), 'Wo': jax.random.normal(ks[6], (DM * NH, EMB), jnp.float32) * (1.0 / np.sqrt(DM * NH)), 'bo': jnp.zeros((EMB,), jnp.float32)}
        return inp
    _L0_xattn_all = _L0_xattn_setup()
    _L0_xattn_in = {k: v for k, v in _L0_xattn_all.items() if k in ('Wq', 'bq', 'Wk', 'bk', 'Wv', 'bv', 'Wo', 'bo')}
    del _L0_xattn_all

    def _L0_attn_setup():
        import jax, jax.numpy as jnp
        import numpy as np
        EPS = 1e-06
        D_MODEL = 512
        D_STATE = 16
        D_CONV = 4
        BATCH = 2
        SEQ = 1024
        D_INNER = 2 * D_MODEL
        DT_RANK = D_MODEL // 16
        D_FF = 4 * D_MODEL

        def rmsnorm(x, w):
            return x * w * jax.lax.rsqrt(jnp.mean(x * x, axis=-1, keepdims=True) + EPS)

        def _ssm(h, in_proj_w, conv_w, conv_b, x_proj_w, dt_proj_w, dt_proj_b, A_log, D, out_proj_w):
            d_inner, d_state = A_log.shape
            dt_rank = dt_proj_w.shape[1]
            d_conv = conv_w.shape[-1]
            bsz = h.shape[0]
            xz = jnp.einsum('bld,ed->ble', h, in_proj_w)
            xin, z = jnp.split(xz, 2, axis=-1)
            xc = jnp.swapaxes(xin, 1, 2)
            xc = jax.lax.conv_general_dilated(xc, conv_w, (1,), [(d_conv - 1, 0)], feature_group_count=d_inner)
            xin = jax.nn.silu(jnp.swapaxes(xc + conv_b[:, None], 1, 2))
            x_dbl = jnp.einsum('bld,ed->ble', xin, x_proj_w)
            dt, Bm, Cm = jnp.split(x_dbl, [dt_rank, dt_rank + d_state], axis=-1)
            delta = jax.nn.softplus(jnp.einsum('blr,dr->bld', dt, dt_proj_w) + dt_proj_b)
            A = -jnp.exp(A_log)

            def step(hstate, t):
                delta_t, B_t, C_t, x_t = t
                dA = jnp.exp(delta_t[..., None] * A)
                dBx = (delta_t * x_t)[..., None] * B_t[:, None, :]
                hstate = dA * hstate + dBx
                y = jnp.einsum('bdn,bn->bd', hstate, C_t)
                return (hstate, y)
            tm = lambda a: jnp.swapaxes(a, 0, 1)
            h0 = jnp.zeros((bsz, d_inner, d_state), h.dtype)
            _, ys = jax.lax.scan(step, h0, (tm(delta), tm(Bm), tm(Cm), tm(xin)))
            y = jnp.swapaxes(ys, 0, 1) + xin * D
            return jnp.einsum('bld,ed->ble', y * jax.nn.silu(z), out_proj_w)
        key = jax.random.key(seed)
        ks = jax.random.split(key, 12)
        s = lambda k, shape, scale=0.02: jax.random.normal(k, shape, jnp.float32) * scale
        A_log = jnp.log(jnp.broadcast_to(jnp.arange(1, D_STATE + 1, dtype=jnp.float32), (D_INNER, D_STATE)))
        return {'x': jax.random.normal(ks[0], (BATCH, SEQ, D_MODEL), jnp.float32), 'norm1_w': jnp.ones((D_MODEL,), jnp.float32), 'norm2_w': jnp.ones((D_MODEL,), jnp.float32), 'in_proj_w': s(ks[1], (2 * D_INNER, D_MODEL)), 'conv_w': s(ks[2], (D_INNER, 1, D_CONV), 0.2), 'conv_b': jnp.zeros((D_INNER,), jnp.float32), 'x_proj_w': s(ks[3], (DT_RANK + 2 * D_STATE, D_INNER)), 'dt_proj_w': s(ks[4], (D_INNER, DT_RANK), 0.1), 'dt_proj_b': jax.random.uniform(ks[5], (D_INNER,), jnp.float32, -4.0, -3.0), 'A_log': A_log, 'D': jnp.ones((D_INNER,), jnp.float32), 'out_proj_w': s(ks[6], (D_MODEL, D_INNER)), 'w1': s(ks[7], (D_FF, D_MODEL)), 'w3': s(ks[8], (D_FF, D_MODEL)), 'w2': s(ks[9], (D_MODEL, D_FF))}
    _L0_attn_all = _L0_attn_setup()
    _L0_attn_in = {k: v for k, v in _L0_attn_all.items() if k in ('norm1_w', 'norm2_w', 'in_proj_w', 'conv_w', 'conv_b', 'x_proj_w', 'dt_proj_w', 'dt_proj_b', 'A_log', 'D', 'out_proj_w', 'w1', 'w3', 'w2')}
    del _L0_attn_all

    def _L0_ffn_setup():
        import jax, jax.numpy as jnp
        import numpy as np
        D_MODEL = 512
        N_EXPERTS = 16
        TOP_K = 2
        EXPERT_DIM = 512
        SHARED_DIM = 1024
        B, T = (2, 512)
        key = jax.random.key(seed)
        ks = jax.random.split(key, 7)
        std = 0.02
        return {'x': jax.random.normal(ks[0], (B, T, D_MODEL), dtype=jnp.float32), 'router_w': jax.random.normal(ks[1], (N_EXPERTS, D_MODEL), dtype=jnp.float32) * std, 'gate_up_w': jax.random.normal(ks[2], (N_EXPERTS, D_MODEL, 2 * EXPERT_DIM), dtype=jnp.float32) * std, 'down_w': jax.random.normal(ks[3], (N_EXPERTS, EXPERT_DIM, D_MODEL), dtype=jnp.float32) * std, 'shared_gate_w': jax.random.normal(ks[4], (SHARED_DIM, D_MODEL), dtype=jnp.float32) * std, 'shared_up_w': jax.random.normal(ks[5], (SHARED_DIM, D_MODEL), dtype=jnp.float32) * std, 'shared_down_w': jax.random.normal(ks[6], (D_MODEL, SHARED_DIM), dtype=jnp.float32) * std}
    _L0_ffn_all = _L0_ffn_setup()
    _L0_ffn_in = {k: v for k, v in _L0_ffn_all.items() if k in ('router_w', 'gate_up_w', 'down_w', 'shared_gate_w', 'shared_up_w', 'shared_down_w')}
    del _L0_ffn_all
    return {'x': x, 'ctx_1024': ctx_1024, 'L0_xattn_Wq': _L0_xattn_in['Wq'], 'L0_xattn_bq': _L0_xattn_in['bq'], 'L0_xattn_Wk': _L0_xattn_in['Wk'], 'L0_xattn_bk': _L0_xattn_in['bk'], 'L0_xattn_Wv': _L0_xattn_in['Wv'], 'L0_xattn_bv': _L0_xattn_in['bv'], 'L0_xattn_Wo': _L0_xattn_in['Wo'], 'L0_xattn_bo': _L0_xattn_in['bo'], 'L0_attn_norm1_w': _L0_attn_in['norm1_w'], 'L0_attn_norm2_w': _L0_attn_in['norm2_w'], 'L0_attn_in_proj_w': _L0_attn_in['in_proj_w'], 'L0_attn_conv_w': _L0_attn_in['conv_w'], 'L0_attn_conv_b': _L0_attn_in['conv_b'], 'L0_attn_x_proj_w': _L0_attn_in['x_proj_w'], 'L0_attn_dt_proj_w': _L0_attn_in['dt_proj_w'], 'L0_attn_dt_proj_b': _L0_attn_in['dt_proj_b'], 'L0_attn_A_log': _L0_attn_in['A_log'], 'L0_attn_D': _L0_attn_in['D'], 'L0_attn_out_proj_w': _L0_attn_in['out_proj_w'], 'L0_attn_w1': _L0_attn_in['w1'], 'L0_attn_w3': _L0_attn_in['w3'], 'L0_attn_w2': _L0_attn_in['w2'], 'L0_ffn_router_w': _L0_ffn_in['router_w'], 'L0_ffn_gate_up_w': _L0_ffn_in['gate_up_w'], 'L0_ffn_down_w': _L0_ffn_in['down_w'], 'L0_ffn_shared_gate_w': _L0_ffn_in['shared_gate_w'], 'L0_ffn_shared_up_w': _L0_ffn_in['shared_up_w'], 'L0_ffn_shared_down_w': _L0_ffn_in['shared_down_w']}

def reference(x, ctx_1024, L0_xattn_Wq, L0_xattn_bq, L0_xattn_Wk, L0_xattn_bk, L0_xattn_Wv, L0_xattn_bv, L0_xattn_Wo, L0_xattn_bo, L0_attn_norm1_w, L0_attn_norm2_w, L0_attn_in_proj_w, L0_attn_conv_w, L0_attn_conv_b, L0_attn_x_proj_w, L0_attn_dt_proj_w, L0_attn_dt_proj_b, L0_attn_A_log, L0_attn_D, L0_attn_out_proj_w, L0_attn_w1, L0_attn_w3, L0_attn_w2, L0_ffn_router_w, L0_ffn_gate_up_w, L0_ffn_down_w, L0_ffn_shared_gate_w, L0_ffn_shared_up_w, L0_ffn_shared_down_w):
    import jax
    import jax.numpy as jnp

    def _L0_xattn_ref(Q, K, V, Wq, bq, Wk, bk, Wv, bv, Wo, bo):
        import jax, jax.numpy as jnp
        import numpy as np
        EMB = 512
        DM = 64
        NH = 16
        bs, q_len, _ = Q.shape
        kv_len = K.shape[1]
        scale = 1.0 / np.sqrt(DM)
        q = (scale * (Q @ Wq + bq)).reshape(bs, q_len, NH, DM)
        k = (K @ Wk + bk).reshape(bs, kv_len, NH, DM)
        v = (V @ Wv + bv).reshape(bs, kv_len, NH, DM)
        qk = jnp.einsum('nlhd,nshd->nhls', q, k)
        a = jax.nn.softmax(qk, axis=-1)
        o = jnp.einsum('nhls,nshd->nlhd', a, v).reshape(bs, q_len, NH * DM)
        return o @ Wo + bo

    def _L0_attn_ref(x, norm1_w, norm2_w, in_proj_w, conv_w, conv_b, x_proj_w, dt_proj_w, dt_proj_b, A_log, D, out_proj_w, w1, w3, w2):
        import jax, jax.numpy as jnp
        import numpy as np
        EPS = 1e-06
        D_MODEL = 512
        D_STATE = 16
        D_CONV = 4
        BATCH = 2
        SEQ = 1024
        D_INNER = 2 * D_MODEL
        DT_RANK = D_MODEL // 16
        D_FF = 4 * D_MODEL

        def rmsnorm(x, w):
            return x * w * jax.lax.rsqrt(jnp.mean(x * x, axis=-1, keepdims=True) + EPS)

        def _ssm(h, in_proj_w, conv_w, conv_b, x_proj_w, dt_proj_w, dt_proj_b, A_log, D, out_proj_w):
            d_inner, d_state = A_log.shape
            dt_rank = dt_proj_w.shape[1]
            d_conv = conv_w.shape[-1]
            bsz = h.shape[0]
            xz = jnp.einsum('bld,ed->ble', h, in_proj_w)
            xin, z = jnp.split(xz, 2, axis=-1)
            xc = jnp.swapaxes(xin, 1, 2)
            xc = jax.lax.conv_general_dilated(xc, conv_w, (1,), [(d_conv - 1, 0)], feature_group_count=d_inner)
            xin = jax.nn.silu(jnp.swapaxes(xc + conv_b[:, None], 1, 2))
            x_dbl = jnp.einsum('bld,ed->ble', xin, x_proj_w)
            dt, Bm, Cm = jnp.split(x_dbl, [dt_rank, dt_rank + d_state], axis=-1)
            delta = jax.nn.softplus(jnp.einsum('blr,dr->bld', dt, dt_proj_w) + dt_proj_b)
            A = -jnp.exp(A_log)

            def step(hstate, t):
                delta_t, B_t, C_t, x_t = t
                dA = jnp.exp(delta_t[..., None] * A)
                dBx = (delta_t * x_t)[..., None] * B_t[:, None, :]
                hstate = dA * hstate + dBx
                y = jnp.einsum('bdn,bn->bd', hstate, C_t)
                return (hstate, y)
            tm = lambda a: jnp.swapaxes(a, 0, 1)
            h0 = jnp.zeros((bsz, d_inner, d_state), h.dtype)
            _, ys = jax.lax.scan(step, h0, (tm(delta), tm(Bm), tm(Cm), tm(xin)))
            y = jnp.swapaxes(ys, 0, 1) + xin * D
            return jnp.einsum('bld,ed->ble', y * jax.nn.silu(z), out_proj_w)
        x = x + _ssm(rmsnorm(x, norm1_w), in_proj_w, conv_w, conv_b, x_proj_w, dt_proj_w, dt_proj_b, A_log, D, out_proj_w)
        h = rmsnorm(x, norm2_w)
        mlp = jnp.einsum('blf,df->bld', jax.nn.silu(jnp.einsum('bld,fd->blf', h, w1)) * jnp.einsum('bld,fd->blf', h, w3), w2)
        return x + mlp

    def _L0_ffn_ref(x, router_w, gate_up_w, down_w, shared_gate_w, shared_up_w, shared_down_w):
        import jax, jax.numpy as jnp
        import numpy as np
        D_MODEL = 512
        N_EXPERTS = 16
        TOP_K = 2
        EXPERT_DIM = 512
        SHARED_DIM = 1024
        B, T = (2, 512)
        Bb, Tt, C = x.shape
        N = Bb * Tt
        E = gate_up_w.shape[0]
        logits = jnp.einsum('btc,ec->bte', x, router_w)
        top_vals, top_idx = jax.lax.top_k(logits, TOP_K)
        gates = jax.nn.sigmoid(top_vals)
        xf = x.reshape(N, C)
        sel = top_idx.reshape(N, TOP_K)
        gw = gates.reshape(N, TOP_K)
        w_full = jnp.zeros((N, E), dtype=x.dtype).at[jnp.arange(N)[:, None], sel].add(gw)
        gu = jnp.einsum('nc,ech->neh', xf, gate_up_w)
        gate, up = jnp.split(gu, 2, axis=-1)
        h = jax.nn.silu(gate) * up
        out_all = jnp.einsum('neh,ehc->nec', h, down_w)
        moe = jnp.einsum('ne,nec->nc', w_full, out_all).reshape(Bb, Tt, C)
        sg = jnp.einsum('btc,sc->bts', x, shared_gate_w)
        su = jnp.einsum('btc,sc->bts', x, shared_up_w)
        shared = jnp.einsum('bts,cs->btc', jax.nn.silu(sg) * su, shared_down_w)
        return moe + shared
    x = x + _L0_xattn_ref(_layernorm(x, axis=-1), ctx_1024, ctx_1024, L0_xattn_Wq, L0_xattn_bq, L0_xattn_Wk, L0_xattn_bk, L0_xattn_Wv, L0_xattn_bv, L0_xattn_Wo, L0_xattn_bo)
    x = x + _L0_attn_ref(_layernorm(x, axis=-1), L0_attn_norm1_w, L0_attn_norm2_w, L0_attn_in_proj_w, L0_attn_conv_w, L0_attn_conv_b, L0_attn_x_proj_w, L0_attn_dt_proj_w, L0_attn_dt_proj_b, L0_attn_A_log, L0_attn_D, L0_attn_out_proj_w, L0_attn_w1, L0_attn_w3, L0_attn_w2)
    x = x + _L0_ffn_ref(_layernorm(x, axis=-1), L0_ffn_router_w, L0_ffn_gate_up_w, L0_ffn_down_w, L0_ffn_shared_gate_w, L0_ffn_shared_up_w, L0_ffn_shared_down_w)
    return x

_drawn_inputs = setup_inputs


def setup_inputs(seed=0):
    import zlib

    import numpy as np

    out = dict(_drawn_inputs(seed))
    spreads = {'L0_xattn_bq': (0.0, 0.1),
     'L0_xattn_bk': (0.0, 0.1),
     'L0_xattn_bv': (0.0, 0.1),
     'L0_xattn_bo': (0.0, 0.1),
     'L0_attn_norm1_w': (1.0, 0.2),
     'L0_attn_norm2_w': (1.0, 0.2),
     'L0_attn_conv_b': (0.0, 0.1),
     'L0_attn_D': (1.0, 0.2)}
    factors = {}
    for name, (base, spread) in spreads.items():
        noise = np.random.default_rng([zlib.crc32(name.encode()), seed]).standard_normal(out[name].shape)
        drawn = base * np.exp(spread * noise) if base else spread * noise
        out[name] = jnp.asarray(drawn.astype(out[name].dtype))
    for name, factor in factors.items():
        out[name] = (out[name] * factor).astype(out[name].dtype)
    return out
```

```python
import math

import numpy as np

import concourse.bass as bass
from concourse import mybir
from contextlib import ExitStack

F32 = mybir.dt.float32
F16 = mybir.dt.float16
ALU = mybir.AluOpType
ACT = mybir.ActivationFunctionType
AX = mybir.AxisListType

P = 128
T = 512
D = 512
TT = T // P
DC = D // P
SA = 16.0
SW = 256.0


class Chain:

    def __init__(self, eng, sem):
        self.eng, self.sem, self.n = eng, sem, 0

    def inc(self, ins):
        self.n += 1
        return ins.then_inc(self.sem, 1)

    def wait(self):
        self.eng.wait_ge(self.sem, self.n)

    def done(self, ins):
        self.inc(ins)
        self.wait()


class Space:

    def __init__(self, nc, ctx, prefix):
        self.nc, self.ctx, self.prefix, self.sems = nc, ctx, prefix, []
        ctx.callback(self.clear)

    def clear(self):
        if self.sems:
            self.nc.clear_and_free_semaphores(self.sems)
            self.nc.all_engine_barrier()

    def sb(self, name, shape, dt=F32):
        return self.ctx.enter_context(self.nc.sbuf_tensor(f"{self.prefix}_{name}", shape, dt))

    def ps(self, name, shape, dt=F32):
        return self.ctx.enter_context(self.nc.psum_tensor(f"{self.prefix}_{name}", shape, dt))

    def sem(self, name):
        self.sems.append(self.nc.alloc_semaphore(f"{self.prefix}_{name}"))
        return self.sems[-1]


def identity(nc, pool, tile, made):
    nc.gpsimd.memset(tile[:, :], 0.0).then_inc(made, 1)
    pool.wait_ge(made, 1)
    nc.gpsimd.affine_select(out=tile[:, :], in_=tile[:, :], compare_op=ALU.not_equal, fill=1.0,
                            base=0, pattern=[[-1, P]], channel_multiplier=1).then_inc(made, 1)


def norm_factor(nc, dve, act_in, act_out, own, var, sd, r, t):
    dve.wait_ge(act_out, 1)
    own.done(nc.vector.reciprocal(r, sd))
    own.done(nc.vector.tensor_tensor(t, r, r, ALU.mult))
    own.done(nc.vector.tensor_tensor(t, t, var, ALU.mult))
    own.done(nc.vector.tensor_scalar(t, t, -0.5, 1.5, ALU.mult, ALU.add))
    own.done(nc.vector.tensor_tensor(r, r, t, ALU.mult))


NH = 16
DH = 64
S = 8192
CK = 512
NCK = S // CK
PAIRS = NH // 2
KT = S // P
WC = 2048
WT = 2 * (NCK - 2)


def latent_queries(nc, x, wq, bq, q_dram):
    with ExitStack() as ctx:
        m = Space(nc, ctx, "lq")
        xs = m.sb("xs", [P, TT, D])
        st = m.sb("st", [P, TT, 6])
        mv = m.sb("mv", [P, TT, 2])
        ve = m.sb("ve", [P, TT])
        sd = m.sb("sd", [P, TT])
        rs = m.sb("rs", [P, TT])
        tmp = m.sb("tmp", [P, TT])
        xn = m.sb("xn", [P, TT, D])
        xh = m.sb("xh", [P, DC, T], F16)
        xl = m.sb("xl", [P, DC, T], F16)
        wf = m.sb("wf", [P, DC, NH * DH])
        wh = m.sb("wh", [P, DC, NH * DH], F16)
        wl = m.sb("wl", [P, DC, NH * DH], F16)
        bqc = m.sb("bqc", [P, PAIRS])
        bqs = m.sb("bqs", [P, PAIRS])
        qf = m.sb("qf", [P, PAIRS, T])
        qh = m.sb("qh", [P, PAIRS, T], F16)
        ql = m.sb("ql", [P, PAIRS, T], F16)
        ident = m.sb("ident", [P, P])
        xT = m.ps("xT", [P, DC, T])
        qp = m.ps("qp", [P, 4, T])
        x_in, w_in, b_in, made = m.sem("x_in"), m.sem("w_in"), m.sem("b_in"), m.sem("made")
        var_ready, sd_ready, xn_ready = m.sem("var_ready"), m.sem("sd_ready"), m.sem("xn_ready")
        xT_ready, xh_ready, xl_ready = m.sem("xT_ready"), m.sem("xh_ready"), m.sem("xl_ready")
        wh_ready, wl_ready, own_dve = m.sem("wh_ready"), m.sem("wl_ready"), m.sem("own_dve")
        b_ready, q_ready, qf_ready = m.sem("b_ready"), m.sem("q_ready"), m.sem("qf_ready")
        qh_ready, ql_ready, q_out = m.sem("qh_ready"), m.sem("ql_ready"), m.sem("q_out")
        block = ctx.enter_context(nc.Block())

        @block.sync
        def _(sp):
            sp.dma_start(xs[:, :, :], x.rearrange("(t p) d -> p t d", p=P)).then_inc(x_in, 16)
            sp.dma_start(wf[:, :, :], wq.rearrange("(c p) n -> p c n", p=P)).then_inc(w_in, 16)
            sp.dma_start(bqc[:, :], bq).then_inc(b_in, 16)
            sp.wait_ge(qh_ready, PAIRS)
            sp.dma_start(q_dram[0].rearrange("(j p) t -> p j t", p=P), qh[:, :, :]).then_inc(q_out, 16)
            sp.wait_ge(ql_ready, PAIRS)
            sp.dma_start(q_dram[1].rearrange("(j p) t -> p j t", p=P), ql[:, :, :]).then_inc(q_out, 16)
            sp.wait_ge(q_out, 32)

        @block.gpsimd
        def _(pool):
            identity(nc, pool, ident, made)

        @block.scalar
        def _(act):
            act.wait_ge(var_ready, 1)
            nc.scalar.activation(sd[:, :], ve[:, :], ACT.Sqrt).then_inc(sd_ready, 1)
            act.wait_ge(w_in, 16)
            nc.scalar.activation(wh[:, :, :], wf[:, :, :], ACT.Copy, scale=SW).then_inc(wh_ready, 1)
            for c in range(DC):
                act.wait_ge(xT_ready, c + 1)
                nc.scalar.activation(xh[:, c, :], xT[:, c, :], ACT.Copy, scale=SA).then_inc(xh_ready, 1)
            act.wait_ge(b_ready, 1)
            for j in range(PAIRS):
                act.wait_ge(q_ready, j + 1)
                nc.scalar.activation(qf[:, j, :], qp[:, j % 4, :], ACT.Identity, bias=bqs[:, j:j + 1],
                                     scale=1.0 / SW).then_inc(qf_ready, 1)
                act.wait_ge(qf_ready, j + 1)
                nc.scalar.activation(qh[:, j, :], qf[:, j, :], ACT.Copy).then_inc(qh_ready, 1)

        @block.vector
        def _(dve):
            own = Chain(dve, own_dve)
            dve.wait_ge(x_in, 16)
            for t in range(TT):
                own.inc(nc.vector.bn_stats(st[:, t, :], xs[:, t, :]))
            own.wait()
            for t in range(TT):
                own.inc(nc.vector.bn_aggr(mv[:, t, :], st[:, t, :]))
            own.wait()
            nc.vector.tensor_scalar(ve[:, :], mv[:, :, 1], 1e-5, None, ALU.add).then_inc(var_ready, 1)
            dve.wait_ge(var_ready, 1)
            norm_factor(nc, dve, var_ready, sd_ready, own, ve[:, :], sd[:, :], rs[:, :], tmp[:, :])
            for t in range(TT):
                nc.vector.tensor_scalar(xn[:, t, :], xs[:, t, :], mv[:, t, 0:1], rs[:, t:t + 1],
                                        ALU.subtract, ALU.mult).then_inc(xn_ready, 1)
            dve.wait_ge(b_in, 16)
            nc.vector.tensor_scalar(bqs[:, :], bqc[:, :], SA, None, ALU.mult).then_inc(b_ready, 1)
            dve.wait_ge(wh_ready, 1)
            nc.vector.scalar_tensor_tensor(wl[:, :, :], wf[:, :, :], SW, wh[:, :, :], ALU.mult,
                                           ALU.subtract).then_inc(wl_ready, 1)
            for c in range(DC):
                dve.wait_ge(xh_ready, c + 1)
                nc.vector.scalar_tensor_tensor(xl[:, c, :], xT[:, c, :], SA, xh[:, c, :], ALU.mult,
                                               ALU.subtract).then_inc(xl_ready, 1)
            for j in range(PAIRS):
                dve.wait_ge(qh_ready, j + 1)
                nc.vector.tensor_tensor(ql[:, j, :], qf[:, j, :], qh[:, j, :],
                                        ALU.subtract).then_inc(ql_ready, 1)

        @block.tensor
        def _(pe):
            pe.wait_ge(made, 2)
            pe.wait_ge(xn_ready, TT)
            for c in range(DC):
                for t in range(TT):
                    last = nc.tensor.transpose(xT[:, c, t * P:(t + 1) * P],
                                               xn[:, t, c * P:(c + 1) * P], ident[:, :])
                last.then_inc(xT_ready, 1)
            pe.wait_ge(wh_ready, 1)
            pe.wait_ge(wl_ready, 1)
            pe.wait_ge(xl_ready, DC)
            for j in range(PAIRS):
                if j >= 4:
                    pe.wait_ge(qf_ready, j - 3)
                cols = slice(j * P, (j + 1) * P)
                for c in range(DC):
                    for n, (w, a) in enumerate(((wh, xh), (wh, xl), (wl, xh))):
                        last = nc.tensor.matmul(qp[:, j % 4, :], w[:, c, cols], a[:, c, :],
                                                start=(c == 0 and n == 0),
                                                stop=(c == DC - 1 and n == 2))
                last.then_inc(q_ready, 1)


def context_keys_values(nc, ctxT, wk, bk, wv, kd, vd, wpack, wsplit):
    with ExitStack() as ctx:
        m = Space(nc, ctx, "kv")
        N = NH * DH
        cf = [m.sb(f"cf{i}", [P, DC, CK]) for i in range(2)]
        ch = [m.sb(f"ch{i}", [P, DC, CK], F16) for i in range(2)]
        cl = [m.sb(f"cl{i}", [P, DC, CK], F16) for i in range(2)]
        wkh, wkl = m.sb("wkh", [P, DC, N], F16), m.sb("wkl", [P, DC, N], F16)
        wvh, wvl = m.sb("wvh", [P, DC, N], F16), m.sb("wvl", [P, DC, N], F16)
        wf = [m.sb(f"wf{i}", [P, DC, N // 2]) for i in range(2)]
        bkc, bks = m.sb("bkc", [P, PAIRS]), m.sb("bks", [P, PAIRS])
        kf = m.sb("kf", [P, 4, CK])
        ksh = [m.sb(f"ksh{i}", [P, PAIRS, CK], F16) for i in range(2)]
        ksl = [m.sb(f"ksl{i}", [P, PAIRS, CK], F16) for i in range(2)]
        vs = [m.sb(f"vs{i}", [P, NH, CK // P, 2 * DH], F16) for i in range(2)]
        tf = [m.sb(f"tf{i}", [P, WC]) for i in range(2)]
        th = [m.sb(f"th{i}", [P, WC], F16) for i in range(2)]
        tl = [m.sb(f"tl{i}", [P, WC], F16) for i in range(2)]
        t_in = [m.sem(f"t_in{i}") for i in range(2)]
        t_out = [m.sem(f"t_out{i}") for i in range(2)]
        th_ready, tl_ready = m.sem("th_ready"), m.sem("tl_ready")
        kp = m.ps("kp", [P, 4, CK])
        vp = m.ps("vp", [P, 4, CK])
        w_in = [m.sem(f"w_in{i}") for i in range(2)]
        b_in, b_ready = m.sem("b_in"), m.sem("b_ready")
        c_in = [m.sem(f"c_in{i}") for i in range(2)]
        wh_ready, wl_ready = m.sem("wh_ready"), m.sem("wl_ready")
        ch_ready, cl_ready = m.sem("ch_ready"), m.sem("cl_ready")
        k_ready, v_ready = m.sem("k_ready"), m.sem("v_ready")
        kf_ready, kl_ready, vl_ready = m.sem("kf_ready"), m.sem("kl_ready"), m.sem("vl_ready")
        kh_ready, vh_ready = m.sem("kh_ready"), m.sem("vh_ready")
        k_out = [m.sem(f"k_out{i}") for i in range(2)]
        v_out = [m.sem(f"v_out{i}") for i in range(2)]
        block = ctx.enter_context(nc.Block())
        VT = 2 * (CK // P)
        ctx_v = ctxT.rearrange("(c p) s -> p c s", p=P)
        wk_v, wv_v = (w.rearrange("(c p) n -> p c n", p=P) for w in (wk, wv))
        halves = [(w, slice(h * N // 2, (h + 1) * N // 2)) for w in (0, 1) for h in (0, 1)]

        @block.sync
        def _(sp):
            for n, (w, cols) in enumerate(halves):
                if n >= 2:
                    sp.wait_ge(wl_ready, n - 1)
                sp.dma_start(wf[n % 2][:, :, :], (wk_v, wv_v)[w][:, :, cols]).then_inc(w_in[n % 2], 16)
                if n < 2:
                    sp.dma_start(cf[n][:, :, :], ctx_v[:, :, n * CK:(n + 1) * CK]).then_inc(c_in[n], 16)
                if n == 0:
                    sp.dma_start(bkc[:, :], bk).then_inc(b_in, 16)

            def chunk(g, par, at):
                if True:
                    sp.wait_ge(tl_ready, 2 * g)
                    for e in range(2):
                        sp.dma_start(tf[e][:, :], wpack[bass.ds(g * 2 + e, 1), :, :]
                                     .rearrange("o p n -> (o p) n")).then_inc(t_in[e], 16)
                    sp.wait_ge(ch_ready, g + 1)
                    sp.wait_ge(cl_ready, g + 1)
                    sp.dma_start(cf[par][:, :, :], ctx_v[:, :, bass.ds(at + 2 * CK, CK)]).then_inc(c_in[par], 16)

            with sp.Fori(0, NCK // 2 - 1) as i:
                for par in range(2):
                    chunk(i * 2 + par, par, i * (2 * CK) + par * CK)
            for par in range(2):
                sp.wait_ge(t_out[par], 32 * (NCK - 2))
                sp.wait_ge(k_out[par], 64 * (NCK // 2 + 1))
                sp.wait_ge(v_out[par], 16 * (NCK // 2 + 1))

        @block.scalar
        def _(act):
            for n, (w, cols) in enumerate(halves):
                act.wait_ge(w_in[n % 2], 16 * (n // 2 + 1))
                nc.scalar.activation((wkh, wvh)[w][:, :, cols], wf[n % 2][:, :, :], ACT.Copy,
                                     scale=SW).then_inc(wh_ready, 1)
                if n == 0:
                    act.wait_ge(c_in[0], 16)
                    nc.scalar.activation(ch[0][:, :, :], cf[0][:, :, :], ACT.Copy, scale=SA).then_inc(ch_ready, 1)
            act.wait_ge(b_ready, 1)

            def chunk(g, par, i, more, weights):
                if more:
                    nxt = 1 - par
                    act.wait_ge(c_in[nxt], 16 * (i + 1) + 16 * par)
                    act.wait_ge(v_ready, VT * g)
                    nc.scalar.activation(ch[nxt][:, :, :], cf[nxt][:, :, :], ACT.Copy,
                                         scale=SA).then_inc(ch_ready, 1)
                act.wait_ge(k_out[par], 64 * (i + 1))
                act.wait_ge(v_out[par], 16 * (i + 1))
                for n in range(8):
                    act.wait_ge(k_ready, PAIRS * g + n + 1)
                    act.wait_ge(kl_ready, PAIRS * g + n + 1)
                    nc.scalar.activation(kf[:, n % 4, :], kp[:, n % 4, :], ACT.Identity,
                                         bias=bks[:, n:n + 1], scale=1.0 / SW).then_inc(kf_ready, 1)
                    act.wait_ge(v_ready, VT * g + n + 1)
                    kt, half = n // 2, n % 2
                    nc.scalar.activation(
                        vs[par][:, half * 8:(half + 1) * 8, kt, 0:DH],
                        vp[:, n % 4, :].rearrange("p (h d) -> p h d", d=DH), ACT.Copy,
                        scale=1.0 / SW).then_inc(vh_ready, 1)
                    act.wait_ge(kf_ready, PAIRS * g + n + 1 + 4)
                    nc.scalar.activation(ksh[par][:, n, :], kf[:, n % 4, :], ACT.Copy).then_inc(kh_ready, 1)
                    if weights and n % 4 == 3:
                        e = n // 4
                        act.wait_ge(t_in[e], 16 * (g + 1))
                        act.wait_ge(t_out[e], 32 * g)
                        nc.scalar.activation(th[e][:, :], tf[e][:, :], ACT.Copy, scale=SW).then_inc(th_ready, 1)

                act.wait_ge(kl_ready, PAIRS * (g + 1) + 4)
                for s, ks in enumerate((ksh, ksl)):
                    for hd in range(2):
                        act.dma_start(kd[s].rearrange("d (j e) n -> d j e n", e=2)[:, :, hd, bass.ds(g * CK, CK)],
                                      ks[par][hd * DH:(hd + 1) * DH, :, :]).then_inc(k_out[par], 16)
                act.wait_ge(vl_ready, VT * (g + 1) + 4)
                act.dma_start(vd.rearrange("h p s -> p h s")[:, :, bass.ds(g * CK, CK)],
                              vs[par].rearrange("p h t c -> p h (t c)")).then_inc(v_out[par], 16)
                if weights:
                    act.wait_ge(tl_ready, 2 * g + 2)
                    for e in range(2):
                        for s, t in enumerate((th, tl)):
                            act.dma_start(wsplit[s].rearrange("p w n -> p (w n)")[:, bass.ds(g * (2 * WC) + e * WC, WC)],
                                          t[e][:, :]).then_inc(t_out[e], 16)

            with act.Fori(0, NCK // 2 - 1) as i:
                for par in range(2):
                    chunk(i * 2 + par, par, i, True, True)
            for par in range(2):
                chunk(NCK - 2 + par, par, NCK // 2 - 1, par == 0, False)

        @block.vector
        def _(dve):
            dve.sem_inc(kl_ready, 4)
            dve.sem_inc(kf_ready, 4)
            dve.sem_inc(vl_ready, 4)
            for par in range(2):
                dve.sem_inc(k_out[par], 64)
                dve.sem_inc(v_out[par], 16)
            for n, (w, cols) in enumerate(halves):
                dve.wait_ge(wh_ready, n + 1)
                nc.vector.scalar_tensor_tensor((wkl, wvl)[w][:, :, cols], wf[n % 2][:, :, :], SW,
                                               (wkh, wvh)[w][:, :, cols], ALU.mult,
                                               ALU.subtract).then_inc(wl_ready, 1)
                if n == 0:
                    dve.wait_ge(ch_ready, 1)
                    nc.vector.scalar_tensor_tensor(cl[0][:, :, :], cf[0][:, :, :], SA, ch[0][:, :, :],
                                                   ALU.mult, ALU.subtract).then_inc(cl_ready, 1)
                    dve.wait_ge(b_in, 16)
                    nc.vector.tensor_scalar(bks[:, :], bkc[:, :], SA, None, ALU.mult).then_inc(b_ready, 1)

            def chunk(g, par, i, more, weights):
                if more:
                    dve.wait_ge(ch_ready, g + 2)
                    nxt = 1 - par
                    nc.vector.scalar_tensor_tensor(cl[nxt][:, :, :], cf[nxt][:, :, :], SA,
                                                   ch[nxt][:, :, :], ALU.mult,
                                                   ALU.subtract).then_inc(cl_ready, 1)
                for n in range(8):
                    dve.wait_ge(vh_ready, VT * g + n + 1)
                    kt, half = n // 2, n % 2
                    hs = slice(half * 8, (half + 1) * 8)
                    nc.vector.scalar_tensor_tensor(
                        vs[par][:, hs, kt, DH:2 * DH], vp[:, n % 4, :].rearrange("p (h d) -> p h d", d=DH),
                        1.0 / SW, vs[par][:, hs, kt, 0:DH], ALU.mult, ALU.subtract).then_inc(vl_ready, 1)
                    dve.wait_ge(kh_ready, PAIRS * g + n + 1)
                    nc.vector.tensor_tensor(ksl[par][:, n, :], kf[:, n % 4, :], ksh[par][:, n, :],
                                            ALU.subtract).then_inc(kl_ready, 1)
                    if weights and n % 4 == 3:
                        e = n // 4
                        dve.wait_ge(th_ready, 2 * g + e + 1)
                        nc.vector.scalar_tensor_tensor(tl[e][:, :], tf[e][:, :], SW, th[e][:, :], ALU.mult,
                                                       ALU.subtract).then_inc(tl_ready, 1)

            with dve.Fori(0, NCK // 2 - 1) as i:
                for par in range(2):
                    chunk(i * 2 + par, par, i, True, True)
            for par in range(2):
                chunk(NCK - 2 + par, par, NCK // 2 - 1, par == 0, False)

        @block.tensor
        def _(pe):
            pe.wait_ge(wh_ready, 4)
            pe.wait_ge(wl_ready, 4)

            def chunk(g, par):
                pe.wait_ge(ch_ready, g + 1)
                pe.wait_ge(cl_ready, g + 1)
                for n in range(8):
                    pe.wait_ge(kf_ready, PAIRS * g + n + 1)
                    cols = slice(n * P, (n + 1) * P)
                    for c in range(DC):
                        for e, (w, a) in enumerate(((wkh, ch), (wkh, cl), (wkl, ch))):
                            last = nc.tensor.matmul(kp[:, n % 4, :], w[:, c, cols], a[par][:, c, :],
                                                    start=(c == 0 and e == 0),
                                                    stop=(c == DC - 1 and e == 2))
                    last.then_inc(k_ready, 1)
                    pe.wait_ge(vl_ready, VT * g + n + 1)
                    kt, half = n // 2, n % 2
                    for c in range(DC):
                        for e, (a, w) in enumerate(((ch, wvh), (ch, wvl), (cl, wvh))):
                            last = nc.tensor.matmul(vp[:, n % 4, :], a[par][:, c, kt * P:(kt + 1) * P],
                                                    w[:, c, half * 512:(half + 1) * 512],
                                                    start=(c == 0 and e == 0),
                                                    stop=(c == DC - 1 and e == 2))
                    last.then_inc(v_ready, 1)

            with pe.Fori(0, NCK // 2) as i:
                for par in range(2):
                    chunk(i * 2 + par, par)


RING = 8
LAG = 3
ONE_K = 256.0
SCORE = 1.0 / (SA * SA * 8)
P_MAX = 1024.0
PARTS = (slice(0, P), slice(DH, P), slice(0, P))
NQ = 4


def attention(nc, q_dram, kd, vd, o_parts):
    with ExitStack() as ctx:
        m = Space(nc, ctx, "at")
        qh = m.sb("qh", [P, NH * T], F16)
        ql = m.sb("ql", [P, NH * T], F16)
        k_next = m.sb("k_next", [P, S], F16)
        k_cur = m.sb("k_cur", [P, S], F16)
        k_one = m.sb("k_one", [P, S], F16)
        vs = m.sb("vs", [P, KT, P], F16)
        ones = m.sb("ones", [P, 32], F16)
        pf = m.sb("pf", [P, RING, T])
        ph = m.sb("ph", [P, RING, T], F16)
        pl = m.sb("pl", [P, RING, T], F16)
        mx = m.sb("mx", [P, TT, NCK])
        mr = m.sb("mr", [P, TT])
        negm = m.sb("negm", [P, TT])
        parts = m.sb("parts", [P, 3, T])
        ident = m.sb("ident", [P, P])
        s1 = m.ps("s1", [P, 2, T])
        st = m.ps("st", [P, 2, T])
        acc = m.ps("acc", [P, 3, T])
        mt = m.ps("mt", [1, T])

        made, q_in, const_ready = m.sem("made"), m.sem("q_in"), m.sem("const_ready")
        kn_in = [m.sem(f"kn_in{i}") for i in range(NQ)]
        k_in = [m.sem(f"k_in{i}") for i in range(NQ)]
        v_in = [m.sem(f"v_in{i}") for i in range(NQ)]
        s1_ready = m.sem("s1_ready")
        s1_free = m.sem("s1_free")
        mr_ready, negm_ready = m.sem("mr_ready"), m.sem("negm_ready")
        mt_ready, m_row = m.sem("mt_ready"), m.sem("m_row")
        st_ready = m.sem("st_ready")
        pf_ready = m.sem("pf_ready")
        ph_ready = m.sem("ph_ready")
        pl_ready = m.sem("pl_ready")
        pv_done = m.sem("pv_done")
        acc_free, o_out = m.sem("acc_free"), m.sem("o_out")
        block = ctx.enter_context(nc.Block())

        STEPS = KT
        QS = STEPS // NQ
        QK = S // NQ
        EARLY = 56
        ends = [min(64, (s + 1) * 64 // EARLY) for s in range(STEPS)]
        items = [range(ends[s - 1] if s else 0, ends[s]) for s in range(STEPS)]

        @block.sync
        def _(sp):
            for s, q in enumerate((qh, ql)):
                src = q_dram[s].rearrange("(h d) t -> d h t", d=DH)
                sp.dma_start(q[0:DH, :].rearrange("d (h t) -> d h t", t=T), src).then_inc(q_in, 16)
            sp.dma_start(qh[DH:P, :].rearrange("d (h t) -> d h t", t=T),
                         q_dram[0].rearrange("(h d) t -> d h t", d=DH)).then_inc(q_in, 16)

            def load_next(n, q):
                cols = slice(q * QK, (q + 1) * QK)
                for s in range(2):
                    sp.dma_start(k_next[s * DH:(s + 1) * DH, cols],
                                 kd[s].rearrange("d h n -> d (h n)")[:, bass.ds(n * S + q * QK, QK)]).then_inc(kn_in[q], 16)

            def load_keys(n, q):
                cols = slice(q * QK, (q + 1) * QK)
                for k, s, at in ((k_cur, 0, 0), (k_cur, 1, DH), (k_one, 0, 0)):
                    sp.dma_start(k[at:at + DH, cols],
                                 kd[s].rearrange("d h n -> d (h n)")[:, bass.ds(n * S + q * QK, QK)]).then_inc(k_in[q], 16)

            def load_values(n, q):
                sp.dma_start(vs[:, q * QS:(q + 1) * QS, :].rearrange("p k c -> p (k c)"),
                             vd.rearrange("h p s -> p h s")[:, bass.ds(n, 1), q * QK:(q + 1) * QK]
                             .rearrange("p h s -> p (h s)")).then_inc(v_in[q], 16)

            for q in range(NQ):
                load_next(0, q)
            for q in range(NQ):
                load_keys(0, q)
            for q in range(NQ):
                load_values(0, q)
            for q in range(NQ):
                sp.wait_ge(s1_ready, 16 * (q + 1))
                load_next(1, q)

            def head(h, more):
                for q in range(NQ):
                    if more:
                        sp.wait_ge(s1_ready, h * 64 + 64 + 16 * (q + 1))
                        load_next(h + 2, q)
                    sp.wait_ge(st_ready, h * STEPS + QS * (q + 1))
                    load_keys(h + 1, q)
                    sp.wait_ge(pv_done, h * (STEPS // 2) + QS // 2 * (q + 1) + RING // 2)
                    load_values(h + 1, q)

            with sp.Fori(0, NH - 2) as h:
                head(h, True)
            head(NH - 2, False)
            sp.wait_ge(o_out, 48 * NH)

        @block.gpsimd
        def _(pool):
            identity(nc, pool, ident, made)
            own = Chain(pool, const_ready)
            pool.wait_ge(made, 2)
            own.done(nc.gpsimd.memset(ones[:, :], 1.0))
            own.done(nc.gpsimd.memset(k_one[DH:P, :], 0.0))
            own.done(nc.gpsimd.memset(ql[DH:P, :], 0.0))
            own.done(nc.gpsimd.memset(k_one[DH:DH + 1, :], ONE_K))

        @block.scalar
        def _(act):
            def row(n):
                act.wait_ge(mt_ready, n + 1)
                nc.scalar.activation(ql[DH:DH + 1, bass.ds(n * T, T)], mt[0:1, :],
                                     ACT.Copy).then_inc(m_row, 1)

            def hi(h, s):
                g = h * STEPS + s
                act.wait_ge(pf_ready, g + 3)
                if s % 2 == 0:
                    act.wait_ge(pv_done, h * (STEPS // 2) + s // 2 + 1)
                nc.scalar.activation(ph[:, s % RING, :], pf[:, s % RING, :], ACT.Copy).then_inc(ph_ready, 1)

            def head(h, more):
                for s in range(STEPS):
                    g = h * STEPS + s
                    act.wait_ge(st_ready, g + 1)
                    act.wait_ge(pl_ready, g + 1)
                    nc.scalar.activation(pf[:, s % RING, :], st[:, s % 2, :], ACT.Exp,
                                         scale=SCORE).then_inc(pf_ready, 1)
                    if s:
                        hi(h, s - 1)
                    if more and s == STEPS - 2:
                        row(h + 1)
                hi(h, STEPS - 1)
                act.wait_ge(pv_done, (h + 1) * (STEPS // 2) + RING // 2)
                act.wait_ge(o_out, h * 48)
                for n, rows in enumerate(PARTS):
                    nc.scalar.activation(parts[rows, n, :], acc[rows, n, :], ACT.Copy).then_inc(acc_free, 1)
                act.wait_ge(acc_free, h * 3 + 3)
                for n, rows in enumerate(PARTS):
                    act.dma_start(o_parts[n][rows, bass.ds(h * T, T)],
                                  parts[rows, n, :]).then_inc(o_out, 16)

            act.wait_ge(const_ready, 4)
            row(0)
            with act.Fori(0, NH - 1) as h:
                head(h, True)
            head(NH - 1, False)

        @block.vector
        def _(dve):
            dve.sem_inc(s1_free, 2)
            dve.sem_inc(pf_ready, 2)
            dve.sem_inc(pl_ready, RING)
            dve.sem_inc(pv_done, RING // 2)

            def tile_max(n, k):
                dve.wait_ge(s1_ready, n * 64 + k + 1)
                nc.vector.reduce_max(mx[:, k % 4, k // 4:k // 4 + 1], s1[:, k % 2, :],
                                     AX.X).then_inc(s1_free, 1)

            def head_max(n):
                dve.wait_ge(s1_free, n * 64 + 64 + 2)
                nc.vector.reduce_max(mr[:, :], mx[:, :, :], AX.X).then_inc(mr_ready, 1)
                dve.wait_ge(mr_ready, n + 1)
                dve.wait_ge(mt_ready, n)
                nc.vector.tensor_scalar(negm[:, :], mr[:, :], -1.0 / ONE_K,
                                        math.log(P_MAX) / SCORE / ONE_K, ALU.mult,
                                        ALU.add).then_inc(negm_ready, 1)

            def head(h, more):
                for s in range(STEPS):
                    g = h * STEPS + s
                    if more:
                        for k in items[s]:
                            tile_max(h + 1, k)
                        if s == EARLY:
                            head_max(h + 1)
                    dve.wait_ge(ph_ready, g + 1)
                    nc.vector.tensor_tensor(pl[:, s % RING, :], pf[:, s % RING, :], ph[:, s % RING, :],
                                            ALU.subtract).then_inc(pl_ready, 1)

            for k in range(64):
                tile_max(0, k)
            head_max(0)
            with dve.Fori(0, NH - 1) as h:
                head(h, True)
            head(NH - 1, False)

        @block.tensor
        def _(pe):
            def scores(n, k):
                chunk, t = k // 4, k % 4
                pe.wait_ge(s1_free, n * 64 + k + 1)
                if k % 16 == 0:
                    pe.wait_ge(kn_in[k // 16], 32 * n + 32)
                if k == 0:
                    pe.wait_ge(m_row, n)
                nc.tensor.matmul(s1[:, k % 2, :], qh[:, bass.ds(n * T + t * P, P)],
                                 k_next[:, chunk * CK:(chunk + 1) * CK], start=True,
                                 stop=True).then_inc(s1_ready, 1)

            def transpose_max(n):
                pe.wait_ge(negm_ready, n + 1)
                for t in range(TT):
                    last = nc.tensor.matmul(mt[0:1, t * P:(t + 1) * P], negm[:, t:t + 1], ident[:, :],
                                            start=True, stop=True)
                last.then_inc(mt_ready, 1)

            def values(h, s):
                g = h * STEPS + s
                if s % QS == 0:
                    pe.wait_ge(v_in[s // QS], 16 * (h + 1))
                if s == 0:
                    pe.wait_ge(acc_free, h * 3)
                first, final = s == 0, s == STEPS - 1
                pe.wait_ge(ph_ready, g + 1)
                if s % 2:
                    pair = (s - 1, s)
                    pe.wait_ge(pl_ready, g + 1 + RING)
                    nc.tensor.matmul(acc[0:DH, 0, :], vs[:, s - 1, 0:DH], pl[:, (s - 1) % RING, :],
                                     start=False, stop=False)
                    nc.tensor.matmul(acc[DH:P, 1, :], vs[:, s, 0:DH], pl[:, s % RING, :],
                                     start=(s == 1), stop=final)
                    for e, (p, r) in enumerate((p, r) for p in (ph, pl) for r in pair):
                        nc.tensor.matmul(acc[e * 32:(e + 1) * 32, 2, :], ones[:, :], p[:, r % RING, :],
                                         start=(s == 1), stop=final, tile_position=(0, e * 32))
                return nc.tensor.matmul(acc[:, 0, :], vs[:, s, :], ph[:, s % RING, :], start=first,
                                        stop=final)

            def head(h, more):
                for s in range(STEPS + LAG):
                    if s < STEPS:
                        g = h * STEPS + s
                        if s == 0:
                            pe.wait_ge(m_row, h + 1)
                        if s % QS == 0:
                            pe.wait_ge(k_in[s // QS], 48 * (h + 1))
                        pe.wait_ge(pf_ready, g + 1)
                        tile = slice(s * P, (s + 1) * P)
                        nc.tensor.matmul(st[:, s % 2, :], k_cur[:, tile], qh[:, bass.ds(h * T, T)],
                                         start=True, stop=False)
                        nc.tensor.matmul(st[:, s % 2, :], k_one[:, tile], ql[:, bass.ds(h * T, T)],
                                         start=False, stop=True).then_inc(st_ready, 1)
                        if more:
                            for k in items[s]:
                                scores(h + 1, k)
                            if s == EARLY + 3:
                                transpose_max(h + 1)
                    if s >= LAG:
                        last = values(h, s - LAG)
                        if (s - LAG) % 2:
                            last.then_inc(pv_done, 1)

            pe.wait_ge(made, 2)
            pe.wait_ge(q_in, 48)
            pe.wait_ge(const_ready, 4)
            for k in range(64):
                scores(0, k)
            transpose_max(0)
            with pe.Fori(0, NH - 1) as h:
                head(h, True)
            head(NH - 1, False)


class W:
    O = (0, 2)
    IN = (2, 4)
    W1 = (6, 4)
    W3 = (10, 4)
    W2 = (14, 4)
    OUT = (18, 2)
    SMALL = (20, 1)


def load_split(eng, wsplit, where, hi, lo, sem):
    at, n = where
    for s, t in enumerate((hi, lo)):
        eng.dma_start(t, wsplit[s][:, at:at + n, :].rearrange("p w n -> p (w n)")).then_inc(sem, 16)


UNSCALE = 1.0 / (SA * SW)


def row_factor(nc, dve, own, src, st, mv, var, sd, rs, tmp, var_ready, sd_ready, n, eps, rms):
    for t in range(TT):
        own.inc(nc.vector.bn_stats(st[:, t, :], src[:, t, :]))
    own.wait()
    for t in range(TT):
        own.inc(nc.vector.bn_aggr(mv[:, t, :], st[:, t, :]))
    own.wait()
    if rms:
        own.done(nc.vector.tensor_tensor(tmp[:, :], mv[:, :, 0], mv[:, :, 0], ALU.mult))
        own.done(nc.vector.tensor_tensor(tmp[:, :], tmp[:, :], mv[:, :, 1], ALU.add))
        nc.vector.tensor_scalar(var[:, :], tmp[:, :], eps, None, ALU.add).then_inc(var_ready, 1)
    else:
        nc.vector.tensor_scalar(var[:, :], mv[:, :, 1], eps, None, ALU.add).then_inc(var_ready, 1)
    dve.wait_ge(var_ready, n)
    dve.wait_ge(sd_ready, n)
    own.done(nc.vector.reciprocal(rs[:, :], sd[:, :]))
    own.done(nc.vector.tensor_tensor(tmp[:, :], rs[:, :], rs[:, :], ALU.mult))
    own.done(nc.vector.tensor_tensor(tmp[:, :], tmp[:, :], var[:, :], ALU.mult))
    own.done(nc.vector.tensor_scalar(tmp[:, :], tmp[:, :], -0.5, 1.5, ALU.mult, ALU.add))
    own.done(nc.vector.tensor_tensor(rs[:, :], rs[:, :], tmp[:, :], ALU.mult))


class Rows:

    def __init__(self, m):
        self.st, self.mv = m.sb("st", [P, TT, 6]), m.sb("mv", [P, TT, 2])
        self.var, self.sd, self.rs, self.tmp = (m.sb(n, [P, TT]) for n in ("var", "sd", "rs", "tmp"))
        self.all = (self.st, self.mv, self.var, self.sd, self.rs, self.tmp)


def transpose_rows(nc, src, dst, ident, ready):
    for c in range(DC):
        for t in range(TT):
            last = nc.tensor.transpose(dst[:, c, t * P:(t + 1) * P], src[:, t, c * P:(c + 1) * P], ident[:, :])
        last.then_inc(ready, 1)


def product(nc, out, pairs):
    for n, (a, b) in enumerate(pairs):
        last = nc.tensor.matmul(out, a, b, start=(n == 0), stop=(n == len(pairs) - 1))
    return last


def three(ah, al, bh, bl):
    return [(ah, bh), (ah, bl), (al, bh)]


def project_attention(nc, keep, x, o_parts, r_dram, bv, bo, n1w, wsplit):
    with ExitStack() as ctx:
        m = Space(nc, ctx, "pa")
        a0, a1, a2 = (m.sb(f"a{i}", [P, PAIRS, T]) for i in range(3))
        rb = m.sb("rb", [P, PAIRS, T])
        dn = m.sb("dn", [P, 4, DH])
        oh, ol = (m.sb(n, [P, PAIRS, T], F16) for n in ("oh", "ol"))
        woh, wol = (m.sb(n, [P, PAIRS, D], F16) for n in ("woh", "wol"))
        bvc, bvs, nw, nws = (m.sb(n, [P, k]) for n, k in (("bvc", PAIRS), ("bvs", PAIRS), ("nw", DC), ("nws", DC)))
        bob, xs, h = m.sb("bob", [P, D]), m.sb("xs", [P, TT, D]), m.sb("h", [P, TT, D])
        rows = Rows(m)
        ident = m.sb("ident", [P, P])
        yp = m.ps("yp", [P, TT, D])
        hT = m.ps("hT", [P, DC, T])
        parts_in, den_in, small_in, w_in = m.sem("parts_in"), m.sem("den_in"), m.sem("small_in"), m.sem("w_in")
        r_ready, r_out, rb_in, own_dve = m.sem("r_ready"), m.sem("r_out"), m.sem("rb_in"), m.sem("own_dve")
        s_ready, oh_ready, ol_ready, y_ready = m.sem("s_ready"), m.sem("oh_ready"), m.sem("ol_ready"), m.sem("y_ready")
        var_ready, sd_ready, h_ready = m.sem("var_ready"), m.sem("sd_ready"), m.sem("h_ready")
        hT_ready, hh_ready, hl_ready, made = m.sem("hT_ready"), m.sem("hh_ready"), m.sem("hl_ready"), m.sem("made")
        block = ctx.enter_context(nc.Block())

        @block.sync
        def _(sp):
            for e in range(4):
                sp.dma_start(dn[:, e, :], o_parts[2][e * 32].rearrange("(p c) -> p c", p=P)).then_inc(den_in, 16)
            for hd in range(2):
                for n, (dst, rows_) in enumerate(((a0, 0), (a1, DH), (a2, DH))):
                    src = o_parts[n // 2][rows_:rows_ + DH, :].rearrange("p (j e t) -> p j e t", e=2, t=T)
                    sp.dma_start(dst[hd * DH:(hd + 1) * DH, :, :], src[:, :, hd, :]).then_inc(parts_in, 16)
            sp.dma_start(xs[:, :, :], x.rearrange("(t p) d -> p t d", p=P)).then_inc(small_in, 16)
            sp.dma_start(bob[:, :], bo.partition_broadcast(P)).then_inc(small_in, 16)
            sp.dma_start(bvc[:, :], bv).then_inc(small_in, 16)
            sp.dma_start(nw[:, :], n1w).then_inc(small_in, 16)
            load_split(sp, wsplit, W.O, woh.rearrange("p j d -> p (j d)"), wol.rearrange("p j d -> p (j d)"), w_in)
            sp.wait_ge(r_ready, 1)
            sp.dma_start(r_dram.rearrange("(p c) -> p c", p=P), dn[:, 0, :]).then_inc(r_out, 16)
            sp.wait_ge(r_out, 16)
            for hd in range(2):
                src = r_dram.rearrange("(j e t) -> j e t", e=2, t=T)[:, hd, :].partition_broadcast(DH)
                sp.dma_start(rb[hd * DH:(hd + 1) * DH, :, :], src).then_inc(rb_in, 16)
            sp.wait_ge(rb_in, 32)

        @block.gpsimd
        def _(pool):
            identity(nc, pool, ident, made)

        @block.scalar
        def _(act):
            for j in range(PAIRS):
                act.wait_ge(s_ready, j + 1)
                nc.scalar.activation(oh[:, j, :], a0[:, j, :], ACT.Copy).then_inc(oh_ready, 1)
            for n in range(2):
                act.wait_ge(var_ready, n + 1)
                nc.scalar.activation(rows.sd[:, :], rows.var[:, :], ACT.Sqrt).then_inc(sd_ready, 1)
            act.wait_ge(small_in, 64)
            for c in range(DC):
                act.wait_ge(hT_ready, c + 1)
                nc.scalar.activation(keep.hh[:, c, :], hT[:, c, :], ACT.Copy, scale=nws[:, c:c + 1]).then_inc(hh_ready, 1)

        @block.vector
        def _(dve):
            own = Chain(dve, own_dve)
            dve.wait_ge(den_in, 64)
            for e in range(1, 4):
                own.done(nc.vector.tensor_tensor(dn[:, 0, :], dn[:, 0, :], dn[:, e, :], ALU.add))
            nc.vector.reciprocal(dn[:, 0, :], dn[:, 0, :]).then_inc(r_ready, 1)
            dve.wait_ge(parts_in, 96)
            own.done(nc.vector.tensor_tensor(a0[:, :, :], a0[:, :, :], a1[:, :, :], ALU.add))
            own.done(nc.vector.tensor_tensor(a0[:, :, :], a0[:, :, :], a2[:, :, :], ALU.add))
            dve.wait_ge(small_in, 64)
            for t in range(TT):
                own.inc(nc.vector.tensor_tensor(xs[:, t, :], xs[:, t, :], bob[:, :], ALU.add))
            own.inc(nc.vector.tensor_scalar(bvs[:, :], bvc[:, :], SA, None, ALU.mult))
            own.inc(nc.vector.tensor_scalar(nws[:, :], nw[:, :], SA, None, ALU.mult))
            dve.wait_ge(rb_in, 32)
            own.done(nc.vector.tensor_tensor(a0[:, :, :], a0[:, :, :], rb[:, :, :], ALU.mult))
            for j in range(PAIRS):
                nc.vector.tensor_scalar(a0[:, j, :], a0[:, j, :], bvs[:, j:j + 1], None, ALU.add).then_inc(s_ready, 1)
            for j in range(PAIRS):
                dve.wait_ge(oh_ready, j + 1)
                nc.vector.tensor_tensor(ol[:, j, :], a0[:, j, :], oh[:, j, :], ALU.subtract).then_inc(ol_ready, 1)
            for t in range(TT):
                dve.wait_ge(y_ready, t + 1)
                own.inc(nc.vector.scalar_tensor_tensor(keep.x1[:, t, :], yp[:, t, :], UNSCALE, xs[:, t, :],
                                                       ALU.mult, ALU.add))
            own.wait()
            row_factor(nc, dve, own, keep.x1, *rows.all, var_ready, sd_ready, 1, 1e-5, False)
            for t in range(TT):
                own.inc(nc.vector.tensor_scalar(keep.a[:, t, :], keep.x1[:, t, :], rows.mv[:, t, 0:1],
                                                rows.rs[:, t:t + 1], ALU.subtract, ALU.mult))
            own.wait()
            row_factor(nc, dve, own, keep.a, *rows.all, var_ready, sd_ready, 2, 1e-6, True)
            for t in range(TT):
                nc.vector.tensor_scalar(h[:, t, :], keep.a[:, t, :], rows.rs[:, t:t + 1], None,
                                        ALU.mult).then_inc(h_ready, 1)
            for c in range(DC):
                dve.wait_ge(hh_ready, c + 1)
                nc.vector.scalar_tensor_tensor(keep.hl[:, c, :], hT[:, c, :], nws[:, c:c + 1], keep.hh[:, c, :],
                                               ALU.mult, ALU.subtract).then_inc(hl_ready, 1)

        @block.tensor
        def _(pe):
            pe.wait_ge(made, 2)
            pe.wait_ge(w_in, 32)
            pe.wait_ge(ol_ready, PAIRS)
            for t in range(TT):
                tok = slice(t * P, (t + 1) * P)
                product(nc, yp[:, t, :], [p for j in range(PAIRS)
                                          for p in three(oh[:, j, tok], ol[:, j, tok], woh[:, j, :], wol[:, j, :])]
                        ).then_inc(y_ready, 1)
            pe.wait_ge(h_ready, TT)
            transpose_rows(nc, h, hT, ident, hT_ready)


DI = 1024
DIC = DI // P
DS = 16
DR = 32


def mamba_inputs(nc, keep, convw, convb, dtb, xd_dram, wsplit):
    with ExitStack() as ctx:
        m = Space(nc, ctx, "mi")
        wh, wl = (m.sb(n, [P, DC, 2 * DI], F16) for n in ("wh", "wl"))
        sh, sl = (m.sb(n, [P, WC], F16) for n in ("sh", "sl"))
        xp = m.sb("xp", [P, DIC, T + 3])
        cw, cb, db = m.sb("cw", [P, DIC, 4]), m.sb("cb", [P, DIC]), m.sb("db", [P, DIC])
        xih, xil = (m.sb(n, [P, DIC, T], F16) for n in ("xih", "xil"))
        xd = m.sb("xd", [2 * DS + DR, T])
        dh, dl = (m.sb(n, [DR, T], F16) for n in ("dh", "dl"))
        pre, soft = m.sb("pre", [P, DIC, T]), m.sb("soft", [P, DIC, T])
        zp = m.ps("zp", [P, 4, T])
        xdp = m.ps("xdp", [2 * DS + DR, T])
        dp = m.ps("dp", [P, 2, T])
        w_in, small_in, pad, own_dve = m.sem("w_in"), m.sem("small_in"), m.sem("pad"), m.sem("own_dve")
        p_ready, p_read = m.sem("p_ready"), m.sem("p_read")
        conv_ready, xin_ready, xih_ready, xil_ready = (m.sem(n) for n in ("conv_ready", "xin_ready", "xih_ready", "xil_ready"))
        xd_ready, xd_read, xd_out, dh_ready, dl_ready = (m.sem(n) for n in ("xd_ready", "xd_read", "xd_out", "dh_ready", "dl_ready"))
        d_ready, pre_ready, abs_ready, ln_ready = (m.sem(n) for n in ("d_ready", "pre_ready", "abs_ready", "ln_ready"))
        block = ctx.enter_context(nc.Block())
        xpw = [s[:, 0:DIC * 64].rearrange("p (c n) -> p c n", c=DIC) for s in (sh, sl)]
        dtw = [s[0:DR, DIC * 64 + 64:DIC * 64 + 64 + DI] for s in (sh, sl)]

        @block.sync
        def _(sp):
            load_split(sp, wsplit, W.IN, wh.rearrange("p c n -> p (c n)"), wl.rearrange("p c n -> p (c n)"), w_in)
            sp.dma_start(cw[:, :, :], convw).then_inc(small_in, 16)
            sp.dma_start(cb[:, :], convb).then_inc(small_in, 16)
            sp.dma_start(db[:, :], dtb).then_inc(small_in, 16)
            load_split(sp, wsplit, W.SMALL, sh[:, :], sl[:, :], small_in)
            sp.wait_ge(xd_read, 1)
            sp.dma_start(xd_dram, xd[DR:DR + 2 * DS, :]).then_inc(xd_out, 16)
            sp.wait_ge(xd_out, 16)

        @block.gpsimd
        def _(pool):
            nc.gpsimd.memset(xp[:, :, 0:3], 0.0).then_inc(pad, 1)

        @block.scalar
        def _(act):
            for f in range(2 * DIC):
                act.wait_ge(p_ready, f + 1)
                if f < DIC:
                    nc.scalar.activation(xp[:, f, 3:], zp[:, f % 4, :], ACT.Copy, scale=UNSCALE).then_inc(p_read, 1)
                else:
                    nc.scalar.activation(keep.zs[:, f - DIC, :], zp[:, f % 4, :], ACT.Silu,
                                         scale=UNSCALE).then_inc(p_read, 1)
            act.wait_ge(small_in, 80)
            for f in range(DIC):
                act.wait_ge(conv_ready, f + 1)
                nc.scalar.activation(keep.xin[:, f, :], soft[:, f, :], ACT.Silu, bias=cb[:, f:f + 1]).then_inc(xin_ready, 1)
                act.wait_ge(xin_ready, f + 1)
                nc.scalar.activation(xih[:, f, :], keep.xin[:, f, :], ACT.Copy, scale=SA).then_inc(xih_ready, 1)
            act.wait_ge(xd_ready, 1)
            nc.scalar.activation(xd[:, :], xdp[:, :], ACT.Copy, scale=UNSCALE).then_inc(xd_read, 1)
            act.wait_ge(xd_read, 1)
            nc.scalar.activation(dh[:, :], xd[0:DR, :], ACT.Copy, scale=SA).then_inc(dh_ready, 1)
            for f in range(DIC):
                act.wait_ge(d_ready, f + 1)
                nc.scalar.activation(pre[:, f, :], dp[:, f % 2, :], ACT.Identity, bias=db[:, f:f + 1],
                                     scale=UNSCALE).then_inc(pre_ready, 1)
            act.wait_ge(pre_ready, DIC)
            act.wait_ge(xin_ready, DIC)
            nc.scalar.activation(soft[:, :, :], pre[:, :, :], ACT.Abs).then_inc(abs_ready, 1)
            act.wait_ge(abs_ready, 1)
            nc.scalar.activation(soft[:, :, :], soft[:, :, :], ACT.Exp, scale=-1.0).then_inc(ln_ready, 1)
            act.wait_ge(ln_ready, 1)
            nc.scalar.activation(soft[:, :, :], soft[:, :, :], ACT.Ln, bias=1.0).then_inc(ln_ready, 1)

        @block.vector
        def _(dve):
            own = Chain(dve, own_dve)
            dve.wait_ge(small_in, 80)
            dve.wait_ge(pad, 1)
            for f in range(DIC):
                dve.wait_ge(p_read, f + 1)
                c = soft[:, f, :]
                own.done(nc.vector.tensor_scalar(c, xp[:, f, 0:T], cw[:, f, 0:1], None, ALU.mult))
                for k in range(1, 4):
                    ins = nc.vector.scalar_tensor_tensor(c, xp[:, f, k:k + T], cw[:, f, k:k + 1], c, ALU.mult, ALU.add)
                    if k < 3:
                        own.done(ins)
                ins.then_inc(conv_ready, 1)
            for f in range(DIC):
                dve.wait_ge(xih_ready, f + 1)
                nc.vector.scalar_tensor_tensor(xil[:, f, :], keep.xin[:, f, :], SA, xih[:, f, :], ALU.mult,
                                               ALU.subtract).then_inc(xil_ready, 1)
            dve.wait_ge(dh_ready, 1)
            nc.vector.scalar_tensor_tensor(dl[:, :], xd[0:DR, :], SA, dh[:, :], ALU.mult, ALU.subtract).then_inc(dl_ready, 1)
            dve.wait_ge(abs_ready, 1)
            own.done(nc.vector.tensor_scalar(pre[:, :, :], pre[:, :, :], 0.0, None, ALU.max))
            dve.wait_ge(ln_ready, 2)
            own.inc(nc.vector.tensor_tensor(keep.delta[:, :, :], pre[:, :, :], soft[:, :, :], ALU.add))

        @block.tensor
        def _(pe):
            pe.wait_ge(w_in, 32)
            for f in range(2 * DIC):
                if f >= 4:
                    pe.wait_ge(p_read, f - 3)
                cols = slice(f * P, (f + 1) * P)
                product(nc, zp[:, f % 4, :], [p for c in range(DC) for p in
                                              three(wh[:, c, cols], wl[:, c, cols], keep.hh[:, c, :], keep.hl[:, c, :])]
                        ).then_inc(p_ready, 1)
            pe.wait_ge(small_in, 80)
            pe.wait_ge(xil_ready, DIC)
            product(nc, xdp[:, :], [p for c in range(DIC) for p in
                                    three(xpw[0][:, c, :], xpw[1][:, c, :], xih[:, c, :], xil[:, c, :])]
                    ).then_inc(xd_ready, 1)
            pe.wait_ge(dl_ready, 1)
            for f in range(DIC):
                if f >= 2:
                    pe.wait_ge(pre_ready, f - 1)
                cols = slice(f * P, (f + 1) * P)
                product(nc, dp[:, f % 2, :], three(dtw[0][:, cols], dtw[1][:, cols], dh[:, :], dl[:, :])
                        ).then_inc(d_ready, 1)


def mamba_scan(nc, keep, a_log, dskip, xd_dram):
    HN = 4
    PASSES = DS // HN
    with ExitStack() as ctx:
        m = Space(nc, ctx, "ms")
        bb, cc = (m.sb(n, [P, DS, T]) for n in ("bb", "cc"))
        al, aneg, dk = m.sb("al", [P, DIC, DS]), m.sb("aneg", [P, DIC, DS]), m.sb("dk", [P, DIC])
        da = [m.sb(f"da{i}", [P, HN, T]) for i in range(2)]
        hs = [m.sb(f"hs{i}", [P, HN, T]) for i in range(2)]
        u = m.sb("u", [P, T])
        y = m.sb("y", [P, 2, T])
        ident = m.sb("ident", [P, P])
        yp = m.ps("yp", [P, 2, T])
        in_sem, made, a_ready, zero_ready = m.sem("in_sem"), m.sem("made"), m.sem("a_ready"), m.sem("zero_ready")
        da_ready, scanned, hc_ready, summed = (m.sem(n) for n in ("da_ready", "scanned", "hc_ready", "summed"))
        own_dve, y_ready, yh_ready, yl_ready = (m.sem(n) for n in ("own_dve", "y_ready", "yh_ready", "yl_ready"))
        block = ctx.enter_context(nc.Block())
        passes = [(f, q) for f in range(DIC) for q in range(PASSES)]

        @block.sync
        def _(sp):
            sp.dma_start(al[:, :, :], a_log).then_inc(in_sem, 16)
            sp.dma_start(dk[:, :], dskip).then_inc(in_sem, 16)
            sp.dma_start(bb[:, :, :], xd_dram[0:DS, :].partition_broadcast(P)).then_inc(in_sem, 16)
            sp.dma_start(cc[:, :, :], xd_dram[DS:2 * DS, :].partition_broadcast(P)).then_inc(in_sem, 16)

        @block.gpsimd
        def _(pool):
            identity(nc, pool, ident, made)
            for i in range(2):
                nc.gpsimd.memset(da[i][:, :, 0:1], 0.0).then_inc(zero_ready, 1)

        @block.scalar
        def _(act):
            def high(f):
                act.wait_ge(y_ready, f + 1)
                nc.scalar.activation(keep.yh[:, f, :], y[:, f % 2, :], ACT.Copy, scale=SA).then_inc(yh_ready, 1)

            act.wait_ge(in_sem, 64)
            nc.scalar.activation(aneg[:, :, :], al[:, :, :], ACT.Exp).then_inc(a_ready, 1)
            act.wait_ge(a_ready, 2)
            act.wait_ge(zero_ready, 2)
            for i, (f, q) in enumerate(passes):
                if i >= 2:
                    act.wait_ge(scanned, i - 1)
                for n in range(HN):
                    s = q * HN + n
                    last = nc.scalar.activation(da[i % 2][:, n, 1:], keep.delta[:, f, 1:], ACT.Exp,
                                                scale=aneg[:, f, s:s + 1])
                last.then_inc(da_ready, 1)
                if q == 2 and f:
                    high(f - 1)
            high(DIC - 1)

        @block.vector
        def _(dve):
            own = Chain(dve, own_dve)
            dve.wait_ge(a_ready, 1)
            nc.vector.tensor_scalar(aneg[:, :, :], aneg[:, :, :], -1.0, None, ALU.mult).then_inc(a_ready, 1)

            def gate(f):
                dve.wait_ge(summed, PASSES * (f + 1))
                if f >= 2:
                    dve.wait_ge(yl_ready, f - 1)
                own.done(nc.vector.scalar_tensor_tensor(y[:, f % 2, :], keep.xin[:, f, :], dk[:, f:f + 1],
                                                        yp[:, f % 2, :], ALU.mult, ALU.add))
                nc.vector.tensor_tensor(y[:, f % 2, :], y[:, f % 2, :], keep.zs[:, f, :], ALU.mult).then_inc(y_ready, 1)

            def low(f):
                dve.wait_ge(yh_ready, f + 1)
                nc.vector.scalar_tensor_tensor(keep.yl[:, f, :], y[:, f % 2, :], SA, keep.yh[:, f, :], ALU.mult,
                                               ALU.subtract).then_inc(yl_ready, 1)

            for i, (f, q) in enumerate(passes):
                st = slice(q * HN, (q + 1) * HN)
                b = hs[i % 2]
                if q == 0:
                    own.done(nc.vector.tensor_tensor(u[:, :], keep.delta[:, f, :], keep.xin[:, f, :], ALU.mult))
                if i >= 2:
                    dve.wait_ge(summed, i - 1)
                own.done(nc.vector.tensor_tensor(b[:, :, :], u[:, :].unsqueeze(1).to_broadcast([P, HN, T]),
                                                 bb[:, st, :], ALU.mult))
                dve.wait_ge(da_ready, i + 1)
                flat = b.rearrange("p n t -> p (n t)")
                nc.vector.tensor_tensor_scan(flat, da[i % 2].rearrange("p n t -> p (n t)"), flat, 0.0,
                                             ALU.mult, ALU.add).then_inc(scanned, 1)
                dve.wait_ge(scanned, i + 1)
                nc.vector.tensor_tensor(b[:, :, :], b[:, :, :], cc[:, st, :], ALU.mult).then_inc(hc_ready, 1)
                if q == 1 and f:
                    gate(f - 1)
                if q == 3 and f:
                    low(f - 1)
            gate(DIC - 1)
            low(DIC - 1)

        @block.tensor
        def _(pe):
            pe.wait_ge(made, 2)
            for i, (f, q) in enumerate(passes):
                pe.wait_ge(hc_ready, i + 1)
                if q == 0 and f >= 2:
                    pe.wait_ge(y_ready, f - 1)
                for n in range(HN):
                    last = nc.tensor.matmul(yp[:, f % 2, :], ident[:, :], hs[i % 2][:, n, :],
                                            start=(q == 0 and n == 0), stop=(q == PASSES - 1 and n == HN - 1))
                last.then_inc(summed, 1)


def mamba_output(nc, keep, n2w, wsplit):
    with ExitStack() as ctx:
        m = Space(nc, ctx, "mo")
        wh, wl = (m.sb(n, [P, DIC, D], F16) for n in ("wh", "wl"))
        nw, nws, h = m.sb("nw", [P, DC]), m.sb("nws", [P, DC]), m.sb("h", [P, TT, D])
        rows = Rows(m)
        ident = m.sb("ident", [P, P])
        op = m.ps("op", [P, TT, D])
        hT = m.ps("hT", [P, DC, T])
        w_in, n_in, own_dve, o_ready, made = (m.sem(n) for n in ("w_in", "n_in", "own_dve", "o_ready", "made"))
        var_ready, sd_ready, h_ready = m.sem("var_ready"), m.sem("sd_ready"), m.sem("h_ready")
        hT_ready, hh_ready, hl_ready = m.sem("hT_ready"), m.sem("hh_ready"), m.sem("hl_ready")
        nws_ready = m.sem("nws_ready")
        block = ctx.enter_context(nc.Block())

        @block.sync
        def _(sp):
            load_split(sp, wsplit, W.OUT, wh.rearrange("p c n -> p (c n)"), wl.rearrange("p c n -> p (c n)"), w_in)
            sp.dma_start(nw[:, :], n2w).then_inc(n_in, 16)

        @block.gpsimd
        def _(pool):
            identity(nc, pool, ident, made)

        @block.scalar
        def _(act):
            act.wait_ge(var_ready, 1)
            nc.scalar.activation(rows.sd[:, :], rows.var[:, :], ACT.Sqrt).then_inc(sd_ready, 1)
            act.wait_ge(nws_ready, 1)
            for c in range(DC):
                act.wait_ge(hT_ready, c + 1)
                nc.scalar.activation(keep.hh[:, c, :], hT[:, c, :], ACT.Copy, scale=nws[:, c:c + 1]).then_inc(hh_ready, 1)

        @block.vector
        def _(dve):
            own = Chain(dve, own_dve)
            dve.wait_ge(n_in, 16)
            nc.vector.tensor_scalar(nws[:, :], nw[:, :], SA, None, ALU.mult).then_inc(nws_ready, 1)
            dve.wait_ge(nws_ready, 1)
            for t in range(TT):
                dve.wait_ge(o_ready, t + 1)
                own.inc(nc.vector.scalar_tensor_tensor(keep.a[:, t, :], op[:, t, :], UNSCALE, keep.a[:, t, :],
                                                       ALU.mult, ALU.add))
            own.wait()
            row_factor(nc, dve, own, keep.a, *rows.all, var_ready, sd_ready, 1, 1e-6, True)
            for t in range(TT):
                nc.vector.tensor_scalar(h[:, t, :], keep.a[:, t, :], rows.rs[:, t:t + 1], None,
                                        ALU.mult).then_inc(h_ready, 1)
            for c in range(DC):
                dve.wait_ge(hh_ready, c + 1)
                nc.vector.scalar_tensor_tensor(keep.hl[:, c, :], hT[:, c, :], nws[:, c:c + 1], keep.hh[:, c, :],
                                               ALU.mult, ALU.subtract).then_inc(hl_ready, 1)

        @block.tensor
        def _(pe):
            pe.wait_ge(made, 2)
            pe.wait_ge(w_in, 32)
            for t in range(TT):
                tok = slice(t * P, (t + 1) * P)
                product(nc, op[:, t, :], [p for j in range(DIC) for p in
                                          three(keep.yh[:, j, tok], keep.yl[:, j, tok], wh[:, j, :], wl[:, j, :])]
                        ).then_inc(o_ready, 1)
            pe.wait_ge(h_ready, TT)
            transpose_rows(nc, h, hT, ident, hT_ready)


DF = 2048
DFC = DF // P


def gated_mlp(nc, keep, wsplit):
    with ExitStack() as ctx:
        m = Space(nc, ctx, "gm")
        w1h, w1l, w3h, w3l = (m.sb(n, [P, DC, DF], F16) for n in ("w1h", "w1l", "w3h", "w3l"))
        w2h, w2l = (m.sb(n, [P, DFC, D], F16) for n in ("w2h", "w2l"))
        sg, mf = m.sb("sg", [P, 2, T]), m.sb("mf", [P, 2, T])
        mh, ml = (m.sb(n, [P, DFC, T], F16) for n in ("mh", "ml"))
        rows = Rows(m)
        gp, up = m.ps("gp", [P, 2, T]), m.ps("up", [P, 2, T])
        op = m.ps("op", [P, TT, D])
        w_in, w2_in, own_dve = m.sem("w_in"), m.sem("w2_in"), m.sem("own_dve")
        g_ready, u_ready, sg_ready, mf_ready, mh_ready, ml_ready = (
            m.sem(n) for n in ("g_ready", "u_ready", "sg_ready", "mf_ready", "mh_ready", "ml_ready"))
        o_ready, var_ready, sd_ready = m.sem("o_ready"), m.sem("var_ready"), m.sem("sd_ready")
        block = ctx.enter_context(nc.Block())

        @block.sync
        def _(sp):
            load_split(sp, wsplit, W.W1, w1h.rearrange("p c n -> p (c n)"), w1l.rearrange("p c n -> p (c n)"), w_in)
            load_split(sp, wsplit, W.W3, w3h.rearrange("p c n -> p (c n)"), w3l.rearrange("p c n -> p (c n)"), w_in)
            load_split(sp, wsplit, W.W2, w2h.rearrange("p c n -> p (c n)"), w2l.rearrange("p c n -> p (c n)"), w2_in)

        @block.scalar
        def _(act):
            for f in range(DFC):
                act.wait_ge(g_ready, f + 1)
                if f >= 2:
                    act.wait_ge(mf_ready, f - 1)
                nc.scalar.activation(sg[:, f % 2, :], gp[:, f % 2, :], ACT.Silu, scale=UNSCALE).then_inc(sg_ready, 1)
                if f:
                    act.wait_ge(mf_ready, f)
                    nc.scalar.activation(mh[:, f - 1, :], mf[:, (f - 1) % 2, :], ACT.Copy).then_inc(mh_ready, 1)
            act.wait_ge(mf_ready, DFC)
            nc.scalar.activation(mh[:, DFC - 1, :], mf[:, (DFC - 1) % 2, :], ACT.Copy).then_inc(mh_ready, 1)
            act.wait_ge(var_ready, 1)
            nc.scalar.activation(rows.sd[:, :], rows.var[:, :], ACT.Sqrt).then_inc(sd_ready, 1)

        @block.vector
        def _(dve):
            own = Chain(dve, own_dve)

            def low(f):
                dve.wait_ge(mh_ready, f + 1)
                nc.vector.tensor_tensor(ml[:, f, :], mf[:, f % 2, :], mh[:, f, :], ALU.subtract).then_inc(ml_ready, 1)

            for f in range(DFC):
                if f >= 2:
                    low(f - 2)
                    dve.wait_ge(ml_ready, f - 1)
                dve.wait_ge(u_ready, f + 1)
                dve.wait_ge(sg_ready, f + 1)
                nc.vector.scalar_tensor_tensor(mf[:, f % 2, :], up[:, f % 2, :], SA * UNSCALE, sg[:, f % 2, :],
                                               ALU.mult, ALU.mult).then_inc(mf_ready, 1)
            for t in range(TT):
                own.inc(nc.vector.tensor_tensor(keep.x1[:, t, :], keep.x1[:, t, :], keep.a[:, t, :], ALU.add))
            low(DFC - 2)
            low(DFC - 1)
            own.wait()
            for t in range(TT):
                dve.wait_ge(o_ready, t + 1)
                own.inc(nc.vector.scalar_tensor_tensor(keep.x1[:, t, :], op[:, t, :], UNSCALE, keep.x1[:, t, :],
                                                       ALU.mult, ALU.add))
            own.wait()
            row_factor(nc, dve, own, keep.x1, *rows.all, var_ready, sd_ready, 1, 1e-5, False)
            for t in range(TT):
                own.inc(nc.vector.tensor_scalar(keep.a[:, t, :], keep.x1[:, t, :], rows.mv[:, t, 0:1],
                                                rows.rs[:, t:t + 1], ALU.subtract, ALU.mult))

        @block.tensor
        def _(pe):
            pe.wait_ge(w_in, 64)
            for f in range(DFC):
                cols = slice(f * P, (f + 1) * P)
                if f >= 2:
                    pe.wait_ge(sg_ready, f - 1)
                product(nc, gp[:, f % 2, :], [p for c in range(DC) for p in
                                              three(w1h[:, c, cols], w1l[:, c, cols], keep.hh[:, c, :], keep.hl[:, c, :])]
                        ).then_inc(g_ready, 1)
                if f >= 2:
                    pe.wait_ge(mf_ready, f - 1)
                product(nc, up[:, f % 2, :], [p for c in range(DC) for p in
                                              three(w3h[:, c, cols], w3l[:, c, cols], keep.hh[:, c, :], keep.hl[:, c, :])]
                        ).then_inc(u_ready, 1)
            pe.wait_ge(w2_in, 32)
            pe.wait_ge(ml_ready, DFC)
            for t in range(TT):
                tok = slice(t * P, (t + 1) * P)
                product(nc, op[:, t, :], [p for j in range(DFC) for p in
                                          three(mh[:, j, tok], ml[:, j, tok], w2h[:, j, :], w2l[:, j, :])]
                        ).then_inc(o_ready, 1)


NE = 16
NX = NE + 2
EH = 512
EHC = EH // P


def route(nc, keep, gates, wsplit):
    with ExitStack() as ctx:
        m = Space(nc, ctx, "ro")
        rh, rl = (m.sb(n, [P, DC, NE], F16) for n in ("rh", "rl"))
        ident = m.sb("ident", [P, P])
        shape = [P, TT, NE]
        lg, rank, eq, one, two, sig = (m.sb(n, shape) for n in ("lg", "rank", "eq", "one", "two", "sig"))
        top, first = m.sb("top", [P, TT]), m.sb("first", [P, TT])
        hT = m.ps("hT", [P, DC, T])
        lp = m.ps("lp", [P, TT, T])
        w_in, made, rank_ready, own_dve = m.sem("w_in"), m.sem("made"), m.sem("rank_ready"), m.sem("own_dve")
        hT_ready, hh_ready, hl_ready, l_ready = (m.sem(n) for n in ("hT_ready", "hh_ready", "hl_ready", "l_ready"))
        lg_ready, sig_ready = m.sem("lg_ready"), m.sem("sig_ready")
        block = ctx.enter_context(nc.Block())

        @block.sync
        def _(sp):
            at = DIC * 64
            for s, r in enumerate((rh, rl)):
                sp.dma_start(r.rearrange("p c n -> p (c n)"), wsplit[s][:, W.SMALL[0], at:at + DC * NE]).then_inc(w_in, 16)

        @block.gpsimd
        def _(pool):
            identity(nc, pool, ident, made)
            for e in range(NE):
                nc.gpsimd.memset(rank[:, :, e:e + 1], float(NE - e)).then_inc(rank_ready, 1)
            nc.gpsimd.memset(gates[:, :, NE:NX], UNSCALE).then_inc(rank_ready, 1)

        @block.scalar
        def _(act):
            for c in range(DC):
                act.wait_ge(hT_ready, c + 1)
                nc.scalar.activation(keep.hh[:, c, :], hT[:, c, :], ACT.Copy, scale=SA).then_inc(hh_ready, 1)
            act.wait_ge(lg_ready, TT)
            nc.scalar.activation(sig[:, :, :], lg[:, :, :], ACT.Sigmoid).then_inc(sig_ready, 1)

        @block.vector
        def _(dve):
            own = Chain(dve, own_dve)
            for c in range(DC):
                dve.wait_ge(hh_ready, c + 1)
                nc.vector.scalar_tensor_tensor(keep.hl[:, c, :], hT[:, c, :], SA, keep.hh[:, c, :],
                                               ALU.mult, ALU.subtract).then_inc(hl_ready, 1)
            for t in range(TT):
                dve.wait_ge(l_ready, t + 1)
                nc.vector.tensor_scalar(lg[:, t, :], lp[:, t, 0:NE], UNSCALE, None, ALU.mult).then_inc(lg_ready, 1)
            dve.wait_ge(lg_ready, TT)
            dve.wait_ge(rank_ready, NE + 1)

            def pick(src, dst):
                own.done(nc.vector.reduce_max(top[:, :], src[:, :, :], AX.X))
                own.done(nc.vector.tensor_tensor(eq[:, :, :], src[:, :, :], top[:, :].unsqueeze(2).to_broadcast(shape),
                                                 ALU.is_equal))
                own.done(nc.vector.tensor_tensor(eq[:, :, :], eq[:, :, :], rank[:, :, :], ALU.mult))
                own.done(nc.vector.reduce_max(first[:, :], eq[:, :, :], AX.X))
                own.done(nc.vector.tensor_tensor(dst[:, :, :], eq[:, :, :], first[:, :].unsqueeze(2).to_broadcast(shape),
                                                 ALU.is_equal))

            pick(lg, one)
            own.done(nc.vector.scalar_tensor_tensor(two[:, :, :], one[:, :, :], -1e30, lg[:, :, :], ALU.mult, ALU.add))
            pick(two, two)
            own.done(nc.vector.tensor_tensor(one[:, :, :], one[:, :, :], two[:, :, :], ALU.add))
            own.done(nc.vector.tensor_scalar(one[:, :, :], one[:, :, :], UNSCALE, None, ALU.mult))
            dve.wait_ge(sig_ready, 1)
            own.inc(nc.vector.tensor_tensor(gates[:, :, 0:NE], one[:, :, :], sig[:, :, :], ALU.mult))

        @block.tensor
        def _(pe):
            pe.wait_ge(made, 2)
            transpose_rows(nc, keep.a, hT, ident, hT_ready)
            pe.wait_ge(w_in, 32)
            pe.wait_ge(hl_ready, DC)
            for t in range(TT):
                tok = slice(t * P, (t + 1) * P)
                product(nc, lp[:, t, 0:NE], [p for c in range(DC) for p in
                                             three(keep.hh[:, c, tok], keep.hl[:, c, tok], rh[:, c, :], rl[:, c, :])]
                        ).then_inc(l_ready, 1)


def experts(nc, keep, gates, gate_up, down, out):
    with ExitStack() as ctx:
        m = Space(nc, ctx, "ex")
        gf = [m.sb(f"gf{i}", [P, DC, 2 * EH]) for i in range(2)]
        df = [m.sb(f"df{i}", [P, EHC, D]) for i in range(2)]
        gh, gl = ([m.sb(f"{n}{i}", [P, DC, 2 * EH], F16) for i in range(2)] for n in ("gh", "gl"))
        dh, dl = ([m.sb(f"{n}{i}", [P, EHC, D], F16) for i in range(2)] for n in ("dh", "dl"))
        sg, mf = m.sb("sg", [P, EHC, T]), m.sb("mf", [P, EHC, T])
        mh, ml = ([m.sb(f"{n}{i}", [P, EHC, T], F16) for i in range(2)] for n in ("mh", "ml"))
        gp, up = m.ps("gp", [P, 2, T]), m.ps("up", [P, 2, T])
        op = m.ps("op", [P, TT, D])
        w_in = [m.sem(f"w_in{i}") for i in range(2)]
        wh_ready, wl_ready = m.sem("wh_ready"), m.sem("wl_ready")
        g_ready, u_ready = m.sem("g_ready"), m.sem("u_ready")
        sg_ready, mf_ready, o_read = m.sem("sg_ready"), m.sem("mf_ready"), m.sem("o_read")
        mh_ready, ml_ready, o_ready, y_out = (m.sem(n) for n in ("mh_ready", "ml_ready", "o_ready", "y_out"))
        block = ctx.enter_context(nc.Block())

        @block.sync
        def _(sp):
            def load(e, par):
                sp.dma_start(gf[par][:, :, :], gate_up.rearrange("(e c p) n -> p e c n", p=P, c=DC)[:, bass.ds(e, 1), :, :]
                             .rearrange("p o c n -> p (o c) n")).then_inc(w_in[par], 16)
                sp.dma_start(df[par][:, :, :], down.rearrange("(e c p) n -> p e c n", p=P, c=EHC)[:, bass.ds(e, 1), :, :]
                             .rearrange("p o c n -> p (o c) n")).then_inc(w_in[par], 16)

            load(0, 0)
            load(1, 1)
            with sp.Fori(0, NX // 2 - 1) as i:
                for par in range(2):
                    sp.wait_ge(wl_ready, i * 4 + 2 * par + 2)
                    load(i * 2 + par + 2, par)
            sp.wait_ge(y_out, 16)

        def loop(eng, body):
            body(0, 0, 0, "first")
            with eng.Fori(0, NX // 2 - 1) as i:
                body(i * 2 + 1, 1, i, "inner")
                body(i * 2 + 2, 0, i + 1, "inner")
            body(NX - 1, 1, NX // 2 - 1, "last")

        @block.scalar
        def _(act):
            def split(e, par, turn):
                act.wait_ge(w_in[par], (turn + 1) * 32)
                nc.scalar.activation(gh[par][:, :, :], gf[par][:, :, :], ACT.Copy, scale=SW).then_inc(wh_ready, 1)
                nc.scalar.activation(dh[par][:, :, :], df[par][:, :, :], ACT.Copy, scale=SW).then_inc(wh_ready, 1)

            def high(e, par, j):
                act.wait_ge(mf_ready, e * EHC + j + 1 + 2)
                nc.scalar.activation(mh[par][:, j, :], mf[:, j, :], ACT.Copy).then_inc(mh_ready, 1)

            def body(e, par, turn, kind):
                for j in range(EHC):
                    act.wait_ge(g_ready, e * EHC + j + 1)
                    nc.scalar.activation(sg[:, j, :], gp[:, j % 2, :], ACT.Silu, scale=UNSCALE).then_inc(sg_ready, 1)
                    if j:
                        high(e, par, j - 1)
                    if j == 2 and kind != "last":
                        if kind != "first":
                            act.wait_ge(o_ready, e * TT)
                        split(e + 1, 1 - par, turn + par)
                high(e, par, EHC - 1)

            split(0, 0, 0)
            loop(act, body)

        @block.vector
        def _(dve):
            dve.sem_inc(sg_ready, 2)
            dve.sem_inc(mf_ready, 2)
            dve.sem_inc(o_read, TT)

            def split(e, par):
                dve.wait_ge(wh_ready, e * 2 + 2)
                nc.vector.scalar_tensor_tensor(gl[par][:, :, :], gf[par][:, :, :], SW, gh[par][:, :, :], ALU.mult,
                                               ALU.subtract).then_inc(wl_ready, 1)
                nc.vector.scalar_tensor_tensor(dl[par][:, :, :], df[par][:, :, :], SW, dh[par][:, :, :], ALU.mult,
                                               ALU.subtract).then_inc(wl_ready, 1)

            def low(e, par, j):
                dve.wait_ge(mh_ready, e * EHC + j + 1)
                nc.vector.tensor_tensor(ml[par][:, j, :], mf[:, j, :], mh[par][:, j, :], ALU.subtract).then_inc(ml_ready, 1)

            def add(e):
                for t in range(TT):
                    dve.wait_ge(o_ready, e * TT + t + 1)
                    dve.wait_ge(o_read, e * TT + t + 1)
                    nc.vector.scalar_tensor_tensor(keep.x1[:, t, :], op[:, t, :], gates[:, t, bass.ds(e, 1)],
                                                   keep.x1[:, t, :], ALU.mult, ALU.add).then_inc(o_read, 1)

            def body(e, par, turn, kind):
                for j in range(EHC):
                    dve.wait_ge(u_ready, e * EHC + j + 1)
                    dve.wait_ge(sg_ready, e * EHC + j + 1 + 2)
                    dve.wait_ge(ml_ready, e * EHC) if kind != "first" else None
                    nc.vector.scalar_tensor_tensor(mf[:, j, :], up[:, j % 2, :], SA * UNSCALE, sg[:, j, :], ALU.mult,
                                                   ALU.mult).then_inc(mf_ready, 1)
                    if j:
                        low(e, par, j - 1)
                    if j == 2:
                        if kind != "first":
                            add(e - 1)
                        if kind != "last":
                            split(e + 1, 1 - par)
                low(e, par, EHC - 1)

            split(0, 0)
            loop(dve, body)
            add(NX - 1)

        @block.tensor
        def _(pe):
            def down_proj(e, par):
                pe.wait_ge(ml_ready, e * EHC + EHC)
                for t in range(TT):
                    tok = slice(t * P, (t + 1) * P)
                    pe.wait_ge(o_read, e * TT + t + 1)
                    product(nc, op[:, t, :], [p for j in range(EHC) for p in
                                              three(mh[par][:, j, tok], ml[par][:, j, tok], dh[par][:, j, :], dl[par][:, j, :])]
                            ).then_inc(o_ready, 1)

            def body(e, par, turn, kind):
                pe.wait_ge(wl_ready, e * 2 + 2)
                for j in range(EHC):
                    for half, bank, free, ready in ((0, gp, sg_ready, g_ready), (1, up, mf_ready, u_ready)):
                        cols = slice(half * EH + j * P, half * EH + (j + 1) * P)
                        pe.wait_ge(free, e * EHC + j + 1)
                        product(nc, bank[:, j % 2, :], [p for c in range(DC) for p in
                                                        three(gh[par][:, c, cols], gl[par][:, c, cols],
                                                              keep.hh[:, c, :], keep.hl[:, c, :])]
                                ).then_inc(ready, 1)
                    if j == 1 and kind != "first":
                        down_proj(e - 1, 1 - par)

            loop(pe, body)
            down_proj(NX - 1, 1)

        @block.gpsimd
        def _(pool):
            pool.wait_ge(o_read, NX * TT + TT)
            pool.dma_start(out.rearrange("(t p) d -> p t d", p=P), keep.x1[:, :, :]).then_inc(y_out, 16)


class Keep:
    pass


def program(nc, x, ctxT, wq, bq, wk, bk, wv, bv, bo, n1w, n2w, convw, convb, dtb, a_log, dskip, wpack, gate_up,
            down, out):
    def scratch(name, shape, dt=F32):
        return nc.dram_tensor(name, shape, dt).ap()

    q_dram = scratch("q_dram", [2, NH * DH, T], F16)
    kd = scratch("kd", [2, DH, NH, S], F16)
    vd = scratch("vd", [NH, P, S], F16)
    wsplit = scratch("wsplit", [2, P, WT, WC], F16)
    o_parts = scratch("o_parts", [3, P, NH * T])
    r_dram = scratch("r_dram", [NH * T])
    xd_dram = scratch("xd_dram", [2 * DS, T])

    latent_queries(nc, x, wq, bq, q_dram)
    context_keys_values(nc, ctxT, wk, bk, wv, kd, vd, wpack, wsplit)
    attention(nc, q_dram, kd, vd, o_parts)
    with ExitStack() as outer:
        m = Space(nc, outer, "keep")
        keep = Keep()
        keep.x1, keep.a = m.sb("x1", [P, TT, D]), m.sb("a", [P, TT, D])
        keep.hh, keep.hl = m.sb("hh", [P, DC, T], F16), m.sb("hl", [P, DC, T], F16)
        gates = m.sb("gates", [P, TT, NX])
        project_attention(nc, keep, x, o_parts, r_dram, bv, bo, n1w, wsplit)
        with ExitStack() as inner:
            m = Space(nc, inner, "mamba")
            keep.xin, keep.zs, keep.delta = (m.sb(n, [P, DIC, T]) for n in ("xin", "zs", "delta"))
            keep.yh, keep.yl = (m.sb(n, [P, DIC, T], F16) for n in ("yh", "yl"))
            mamba_inputs(nc, keep, convw, convb, dtb, xd_dram, wsplit)
            mamba_scan(nc, keep, a_log, dskip, xd_dram)
            mamba_output(nc, keep, n2w, wsplit)
        gated_mlp(nc, keep, wsplit)
        route(nc, keep, gates, wsplit)
        experts(nc, keep, gates, gate_up, down, out)


def columns(v):
    return v.reshape(-1, P).T


def layout(inputs):
    a = {k: np.asarray(v) for k, v in inputs.items()}
    g = lambda n: a["L0_xattn_" + n]
    b = lambda n: a["L0_attn_" + n]
    f = lambda n: a["L0_ffn_" + n]

    def rows(w):
        return w.reshape(-1, P, w.shape[1]).transpose(1, 0, 2).reshape(P, -1)

    dtw = np.concatenate([b("dt_proj_w").T, np.zeros((P - DR, DI), np.float32)])
    small = np.concatenate([rows(b("x_proj_w").T), rows(f("router_w").T), dtw], axis=1)
    small = np.concatenate([small, np.zeros((P, WC - small.shape[1]), np.float32)], axis=1)
    packed = np.concatenate([rows(g("Wo")), rows(b("in_proj_w").T), rows(b("w1").T), rows(b("w3").T),
                             rows(b("w2").T), rows(b("out_proj_w").T), small], axis=1)
    packed = np.concatenate([packed, np.zeros((P, WT * WC - packed.shape[1]), np.float32)], axis=1)
    sg, su, sd = f("shared_gate_w").T, f("shared_up_w").T, f("shared_down_w").T
    shared = [np.concatenate([sg[:, h * EH:(h + 1) * EH], su[:, h * EH:(h + 1) * EH]], axis=1) for h in range(2)]
    gate_up = np.concatenate([f("gate_up_w").reshape(NE * D, 2 * EH)] + shared)
    down = np.concatenate([f("down_w").reshape(NE * EH, D), sd])
    out = dict(
        x=a["x"][0], ctxT=a["ctx_1024"][0].T, wq=g("Wq"), bq=columns(g("bq")), wk=g("Wk"), bk=columns(g("bk")),
        wv=g("Wv"), bv=columns(g("bv")), bo=g("bo"), n1w=columns(b("norm1_w")), n2w=columns(b("norm2_w")),
        convw=b("conv_w").reshape(DIC, P, 4).transpose(1, 0, 2), convb=columns(b("conv_b")),
        dtb=columns(b("dt_proj_b")), a_log=b("A_log").reshape(DIC, P, DS).transpose(1, 0, 2), dskip=columns(b("D")),
        wpack=packed.reshape(P, WT, WC).transpose(1, 0, 2), gate_up=gate_up, down=down)
    return {k: np.ascontiguousarray(v) for k, v in out.items()}


def kernel(**inputs):
    import concourse.bacc as bacc
    from concourse.bass_utils import run_bass_kernel_spmd

    nc = bacc.Bacc("TRN2", target_bir_lowering=False, num_devices=1)
    arrays = layout(inputs)
    args = [nc.dram_tensor(k, v.shape, mybir.dt.from_np(v.dtype), kind="ExternalInput").ap()
            for k, v in arrays.items()]
    out = nc.dram_tensor("out", [T, D], F32, kind="ExternalOutput").ap()
    program(nc, *args, out)
    result = run_bass_kernel_spmd(nc, [arrays], core_ids=[0])
    return result.results[0]["out"].reshape(1, T, D)
```

```python
import math

import numpy as np

import concourse.bass as bass
from concourse import mybir
from contextlib import ExitStack

F32 = mybir.dt.float32
F16 = mybir.dt.float16
ALU = mybir.AluOpType
ACT = mybir.ActivationFunctionType
AX = mybir.AxisListType

P = 128
T = 512
D = 512
TT = T // P
DC = D // P
SA = 16.0
SW = 256.0


class Chain:

    def __init__(self, eng, sem):
        self.eng, self.sem, self.n = eng, sem, 0

    def inc(self, ins):
        self.n += 1
        return ins.then_inc(self.sem, 1)

    def wait(self):
        self.eng.wait_ge(self.sem, self.n)

    def done(self, ins):
        self.inc(ins)
        self.wait()


class Space:

    def __init__(self, nc, ctx, prefix):
        self.nc, self.ctx, self.prefix, self.sems = nc, ctx, prefix, []
        ctx.callback(self.clear)

    def clear(self):
        if self.sems:
            self.nc.clear_and_free_semaphores(self.sems)
            self.nc.all_engine_barrier()

    def sb(self, name, shape, dt=F32):
        return self.ctx.enter_context(self.nc.sbuf_tensor(f"{self.prefix}_{name}", shape, dt))

    def ps(self, name, shape, dt=F32):
        return self.ctx.enter_context(self.nc.psum_tensor(f"{self.prefix}_{name}", shape, dt))

    def sem(self, name):
        self.sems.append(self.nc.alloc_semaphore(f"{self.prefix}_{name}"))
        return self.sems[-1]


def identity(nc, pool, tile, made):
    nc.gpsimd.memset(tile[:, :], 0.0).then_inc(made, 1)
    pool.wait_ge(made, 1)
    nc.gpsimd.affine_select(out=tile[:, :], in_=tile[:, :], compare_op=ALU.not_equal, fill=1.0,
                            base=0, pattern=[[-1, P]], channel_multiplier=1).then_inc(made, 1)


NH = 16
DH = 64
S = 8192
CK = 512
NCK = S // CK
PAIRS = NH // 2
KT = S // P
WC = 2048
TW = 3
WT = TW * (NCK // 2 - 1)


def latent_queries(nc, keep, x, wq, bq, wk, wv, q_dram):
    with ExitStack() as ctx:
        m = Space(nc, ctx, "lq")
        N = NH * DH
        xs = m.sb("xs", [P, TT, D])
        rows = Rows(m)
        xn = m.sb("xn", [P, TT, D])
        xh, xl = (m.sb(n, [P, DC, T], F16) for n in ("xh", "xl"))
        wf = [m.sb(f"wf{i}", [P, DC, N // 2]) for i in range(3)]
        wh, wl = (m.sb(n, [P, DC, N], F16) for n in ("wh", "wl"))
        bqc, bqs = m.sb("bqc", [P, PAIRS]), m.sb("bqs", [P, PAIRS])
        qf = m.sb("qf", [P, 4, T])
        qh, ql = (m.sb(n, [P, PAIRS, T], F16) for n in ("qh", "ql"))
        ident = m.sb("ident", [P, P])
        xT = m.ps("xT", [P, DC, T])
        qp = m.ps("qp", [P, 4, T])
        x_in, b_in, made, zero = m.sem("x_in"), m.sem("b_in"), m.sem("made"), m.sem("zero")
        w_in = [m.sem(f"w_in{i}") for i in range(3)]
        var_ready, sd_ready, xn_ready = m.sem("var_ready"), m.sem("sd_ready"), m.sem("xn_ready")
        xT_ready, xh_ready, xl_ready = m.sem("xT_ready"), m.sem("xh_ready"), m.sem("xl_ready")
        wh_ready, wl_ready, own_dve = m.sem("wh_ready"), m.sem("wl_ready"), m.sem("own_dve")
        b_ready, q_ready, qf_ready = m.sem("b_ready"), m.sem("q_ready"), m.sem("qf_ready")
        qh_ready, ql_ready, q_out = m.sem("qh_ready"), m.sem("ql_ready"), m.sem("q_out")
        block = ctx.enter_context(nc.Block())
        halves = [(w, slice(h * N // 2, (h + 1) * N // 2)) for w in range(3) for h in range(2)]
        his = (wh, keep.wkh, keep.wvh)
        los = (wl, keep.wkl, keep.wvl)

        @block.sync
        def _(sp):
            sp.dma_start(xs[:, :, :], x.rearrange("(t p) d -> p t d", p=P)).then_inc(x_in, 16)
            for n, (w, cols) in enumerate(halves):
                if n >= 3:
                    sp.wait_ge(wl_ready, n - 2)
                src = (wq, wk, wv)[w].rearrange("(c p) n -> p c n", p=P)
                sp.dma_start(wf[n % 3][:, :, :], src[:, :, cols]).then_inc(w_in[n % 3], 16)
                if n == 1:
                    sp.dma_start(bqc[:, :], bq).then_inc(b_in, 16)
            sp.wait_ge(qh_ready, PAIRS)
            sp.dma_start(q_dram[0].rearrange("(j p) t -> p j t", p=P), qh[:, :, :]).then_inc(q_out, 16)
            sp.wait_ge(ql_ready, PAIRS)
            sp.dma_start(q_dram[1].rearrange("(j p) t -> p j t", p=P), ql[:, :, :]).then_inc(q_out, 16)
            sp.wait_ge(q_out, 32)

        @block.gpsimd
        def _(pool):
            identity(nc, pool, ident, made)
            pool.wait_ge(made, 2)
            nc.gpsimd.memset(keep.qz[0][DH:P, :, :], 0.0).then_inc(zero, 1)
            pool.wait_ge(zero, 1)
            nc.gpsimd.memset(keep.qz[1][0:DH, :, :], 0.0).then_inc(zero, 1)

        @block.scalar
        def _(act):
            def split(n):
                w, cols = halves[n]
                act.wait_ge(w_in[n % 3], 16 * (n // 3 + 1))
                nc.scalar.activation(his[w][:, :, cols], wf[n % 3][:, :, :], ACT.Copy, scale=SW).then_inc(wh_ready, 1)

            split(0)
            act.wait_ge(var_ready, 1)
            nc.scalar.activation(rows.sd[:, :], rows.var[:, :], ACT.Sqrt).then_inc(sd_ready, 1)
            split(1)
            for c in range(DC):
                act.wait_ge(xT_ready, c + 1)
                nc.scalar.activation(xh[:, c, :], xT[:, c, :], ACT.Copy, scale=SA).then_inc(xh_ready, 1)
            split(2)
            act.wait_ge(b_ready, 1)
            for j in range(PAIRS):
                act.wait_ge(q_ready, j + 1)
                if j >= 4:
                    act.wait_ge(ql_ready, j - 3)
                nc.scalar.activation(qf[:, j % 4, :], qp[:, j % 4, :], ACT.Identity, bias=bqs[:, j:j + 1],
                                     scale=1.0 / SW).then_inc(qf_ready, 1)
                act.wait_ge(qf_ready, j + 1)
                for e in range(2):
                    half = slice(e * DH, (e + 1) * DH)
                    nc.scalar.activation(keep.qz[e][half, j, :], qf[half, j % 4, :], ACT.Copy)
                nc.scalar.activation(qh[:, j, :], qf[:, j % 4, :], ACT.Copy).then_inc(qh_ready, 1)
                if j % 2 and j < 6:
                    split(3 + j // 2)

        @block.vector
        def _(dve):
            own = Chain(dve, own_dve)

            def split(n):
                w, cols = halves[n]
                dve.wait_ge(wh_ready, n + 1)
                nc.vector.scalar_tensor_tensor(los[w][:, :, cols], wf[n % 3][:, :, :], SW, his[w][:, :, cols],
                                               ALU.mult, ALU.subtract).then_inc(wl_ready, 1)

            dve.wait_ge(x_in, 16)
            row_factor(nc, dve, own, xs, *rows.all, var_ready, sd_ready, 1, 1e-5, False)
            for t in range(TT):
                nc.vector.tensor_scalar(xn[:, t, :], xs[:, t, :], rows.mv[:, t, 0:1], rows.rs[:, t:t + 1],
                                        ALU.subtract, ALU.mult).then_inc(xn_ready, 1)
            dve.wait_ge(b_in, 16)
            nc.vector.tensor_scalar(bqs[:, :], bqc[:, :], SA, None, ALU.mult).then_inc(b_ready, 1)
            split(0)
            split(1)
            for c in range(DC):
                dve.wait_ge(xh_ready, c + 1)
                nc.vector.scalar_tensor_tensor(xl[:, c, :], xT[:, c, :], SA, xh[:, c, :], ALU.mult,
                                               ALU.subtract).then_inc(xl_ready, 1)
            split(2)
            for j in range(PAIRS):
                dve.wait_ge(qh_ready, j + 1)
                nc.vector.tensor_tensor(ql[:, j, :], qf[:, j % 4, :], qh[:, j, :],
                                        ALU.subtract).then_inc(ql_ready, 1)
                if j % 2 and j < 6:
                    split(3 + j // 2)

        @block.tensor
        def _(pe):
            pe.wait_ge(made, 2)
            pe.wait_ge(xn_ready, TT)
            transpose_rows(nc, xn, xT, ident, xT_ready)
            pe.wait_ge(wh_ready, 2)
            pe.wait_ge(wl_ready, 2)
            pe.wait_ge(xl_ready, DC)
            for j in range(PAIRS):
                if j >= 4:
                    pe.wait_ge(qf_ready, j - 3)
                cols = slice(j * P, (j + 1) * P)
                product(nc, qp[:, j % 4, :], [p for c in range(DC) for p in
                                              three(wh[:, c, cols], wl[:, c, cols], xh[:, c, :], xl[:, c, :])]
                        ).then_inc(q_ready, 1)


LOG_P_MAX = math.log(256.0)
ONE_K = 256.0
SCORE = 1.0 / (SA * SA * 8)


def context_keys_values(nc, keep, ctxT, bk, kd, vd, m_dram, wpack, wsplit):
    with ExitStack() as ctx:
        m = Space(nc, ctx, "kv")
        cf = [m.sb(f"cf{i}", [P, DC, CK]) for i in range(2)]
        ch, cl = ([m.sb(f"{n}{i}", [P, DC, CK], F16) for i in range(2)] for n in ("ch", "cl"))
        bkc, bks = m.sb("bkc", [P, PAIRS]), m.sb("bks", [P, PAIRS])
        kf = m.sb("kf", [P, 4, CK])
        ksh, ksl = ([m.sb(f"{n}{i}", [P, PAIRS, CK], F16) for i in range(2)] for n in ("ksh", "ksl"))
        vs = [m.sb(f"vs{i}", [P, NH, CK // P, 2 * DH], F16) for i in range(2)]
        tf = [m.sb(f"tf{i}", [P, WC]) for i in range(TW)]
        th, tl = ([m.sb(f"{n}{i}", [P, WC], F16) for i in range(TW)] for n in ("th", "tl"))
        mx = m.sb("mx", [P, NCK * NH * TT])
        mr, negm = m.sb("mr", [P, NH * TT]), m.sb("negm", [P, NH * TT])
        mrow = m.sb("mrow", [NH * TT, P], F16)
        ident = m.sb("ident", [P, P])
        kp, vp = m.ps("kp", [P, 2, CK]), m.ps("vp", [P, 2, CK])
        s1 = m.ps("s1", [P, 4, CK])
        t_in = [m.sem(f"t_in{i}") for i in range(TW)]
        t_out = [m.sem(f"t_out{i}") for i in range(TW)]
        th_ready = m.sem("th_ready")
        b_in, b_ready, made = m.sem("b_in"), m.sem("b_ready"), m.sem("made")
        c_in = [m.sem(f"c_in{i}") for i in range(2)]
        ch_ready, cl_ready = m.sem("ch_ready"), m.sem("cl_ready")
        k_ready, s1_ready = m.sem("k_ready"), m.sem("s1_ready")
        kf_ready, kl_ready, vl_ready, s1_max = m.sem("kf_ready"), m.sem("kl_ready"), m.sem("vl_ready"), m.sem("s1_max")
        tl_ready, v_ready = m.sem("tl_ready"), m.sem("v_ready")
        kh_ready, vh_ready = m.sem("kh_ready"), m.sem("vh_ready")
        k_out = [m.sem(f"k_out{i}") for i in range(2)]
        v_out = [m.sem(f"v_out{i}") for i in range(2)]
        mr_ready, negm_ready, mt_ready, mrow_ready, m_out = (
            m.sem(n) for n in ("mr_ready", "negm_ready", "mt_ready", "mrow_ready", "m_out"))
        block = ctx.enter_context(nc.Block())
        VT = 2 * (CK // P)
        MG = 4
        ctx_v = ctxT.rearrange("(c p) s -> p c s", p=P)

        def chunks(eng, chunk):
            chunk(0, 0, 0, None, {})
            with eng.Fori(0, NCK // 2 - 1) as i:
                for odd in (1, 0):
                    chunk(i * 2 + (2 - odd), odd, i + (1 - odd), i, {3: 0, 7: 1} if odd else {5: 2})
            chunk(NCK - 1, 1, NCK // 2 - 1, None, {})

        @block.sync
        def _(sp):
            for n in range(2):
                sp.dma_start(cf[n][:, :, :], ctx_v[:, :, n * CK:(n + 1) * CK]).then_inc(c_in[n], 16)
            sp.dma_start(bkc[:, :], bk).then_inc(b_in, 16)

            with sp.Fori(0, NCK // 2 - 1) as i:
                for odd in (1, 0):
                    sp.wait_ge(ch_ready, i * 2 + (2 - odd))
                    sp.wait_ge(cl_ready, i * 2 + (2 - odd))
                    sp.dma_start(cf[1 - odd][:, :, :],
                                 ctx_v[:, :, bass.ds(i * (2 * CK) + (3 - odd) * CK, CK)]).then_inc(c_in[1 - odd], 16)
                    for e in ((0, 1) if odd else (2,)):
                        sp.wait_ge(tl_ready, i * TW + e + 1)
                        sp.dma_start(tf[e][:, :], wpack[bass.ds(i * TW + e, 1), :, :]
                                     .rearrange("o p n -> (o p) n")).then_inc(t_in[e], 16)
            sp.wait_ge(mrow_ready, 1)
            sp.dma_start(m_dram.rearrange("(r p) -> r p", p=P), mrow[:, :]).then_inc(m_out, 16)
            sp.wait_ge(m_out, 16)
            for e in range(TW):
                sp.wait_ge(t_out[e], 32 * (NCK // 2))
            for par in range(2):
                sp.wait_ge(k_out[par], 64 * (NCK // 2 + 1))
                sp.wait_ge(v_out[par], 16 * (NCK // 2 + 1))

        @block.gpsimd
        def _(pool):
            identity(nc, pool, ident, made)

        @block.scalar
        def _(act):
            act.wait_ge(c_in[0], 16)
            nc.scalar.activation(ch[0][:, :, :], cf[0][:, :, :], ACT.Copy, scale=SA).then_inc(ch_ready, 1)
            act.wait_ge(b_ready, 1)

            def chunk(g, par, uses, i, tiles):
                act.wait_ge(k_out[par], 64 * (uses + 1))
                act.wait_ge(v_out[par], 16 * (uses + 1))
                for n in range(8):
                    act.wait_ge(k_ready, PAIRS * g + n + 1)
                    act.wait_ge(kl_ready, PAIRS * g + n + 1)
                    nc.scalar.activation(kf[:, n % 4, :], kp[:, n % 2, :], ACT.Identity,
                                         bias=bks[:, n:n + 1], scale=1.0 / SW).then_inc(kf_ready, 1)
                    act.wait_ge(kf_ready, PAIRS * g + n + 1 + 2)
                    nc.scalar.activation(ksh[par][:, n, :], kf[:, n % 4, :], ACT.Copy).then_inc(kh_ready, 1)
                    act.wait_ge(v_ready, VT * g + n + 2)
                    kt, half = n // 2, n % 2
                    nc.scalar.activation(
                        vs[par][:, half * 8:(half + 1) * 8, kt, 0:DH],
                        vp[:, n % 2, :].rearrange("p (h d) -> p h d", d=DH), ACT.Copy,
                        scale=1.0 / SW).then_inc(vh_ready, 1)
                    if n == 1 and (i is not None or g == 0):
                        nxt = 1 - par
                        act.wait_ge(c_in[nxt], 16 * (uses + 1) + 16 * par)
                        nc.scalar.activation(ch[nxt][:, :, :], cf[nxt][:, :, :], ACT.Copy,
                                             scale=SA).then_inc(ch_ready, 1)
                    if n in tiles:
                        e = tiles[n]
                        act.wait_ge(t_in[e], 16 * (i + 1))
                        act.wait_ge(t_out[e], 32 * (i + 1))
                        nc.scalar.activation(th[e][:, :], tf[e][:, :], ACT.Copy, scale=SW).then_inc(th_ready, 1)
                act.wait_ge(kl_ready, PAIRS * (g + 1) + 4)
                for s, ks in enumerate((ksh, ksl)):
                    for hd in range(2):
                        act.dma_start(kd[s].rearrange("d (j e) n -> d j e n", e=2)[:, :, hd, bass.ds(g * CK, CK)],
                                      ks[par][hd * DH:(hd + 1) * DH, :, :]).then_inc(k_out[par], 16)
                act.wait_ge(vl_ready, VT * (g + 1) + 2)
                act.dma_start(vd.rearrange("h p s -> p h s")[:, :, bass.ds(g * CK, CK)],
                              vs[par].rearrange("p h t c -> p h (t c)")).then_inc(v_out[par], 16)
                for e in tiles.values():
                    act.wait_ge(tl_ready, i * TW + e + 1 + TW)
                    for s, t in enumerate((th, tl)):
                        act.dma_start(wsplit[s].rearrange("p w n -> p (w n)")[:, bass.ds(i * (TW * WC) + e * WC, WC)],
                                      t[e][:, :]).then_inc(t_out[e], 16)

            chunks(act, chunk)
            act.wait_ge(mt_ready, 1)
            nc.scalar.activation(mrow[:, :], kp[0:NH * TT, 0, 0:P], ACT.Copy).then_inc(mrow_ready, 1)

        @block.vector
        def _(dve):
            dve.sem_inc(kf_ready, 2)
            dve.sem_inc(kl_ready, 4)
            dve.sem_inc(vl_ready, 2)
            dve.sem_inc(s1_max, 2)
            dve.sem_inc(tl_ready, TW)
            dve.sem_inc(v_ready, 1)
            for par in range(2):
                dve.sem_inc(k_out[par], 64)
                dve.sem_inc(v_out[par], 16)
            for e in range(TW):
                dve.sem_inc(t_out[e], 32)
            dve.wait_ge(b_in, 16)
            nc.vector.tensor_scalar(bks[:, :], bkc[:, :], SA, None, ALU.mult).then_inc(b_ready, 1)
            dve.wait_ge(ch_ready, 1)
            nc.vector.scalar_tensor_tensor(cl[0][:, :, :], cf[0][:, :, :], SA, ch[0][:, :, :],
                                           ALU.mult, ALU.subtract).then_inc(cl_ready, 1)

            def maxima(g, n, groups):
                if n == 0 and isinstance(g, int) and g == 0:
                    return
                for q in groups:
                    dve.wait_ge(s1_ready, g * (PAIRS * MG) + (n - 1) * MG + q + 1)
                    at = 2 * (n - 1) * TT + q * 2
                    nc.vector.reduce_max(mx[:, bass.ds(g * (NH * TT) + at, 2)], s1[:, (q % 2) * 2:(q % 2) * 2 + 2, :],
                                         AX.X).then_inc(s1_max, 1)

            def chunk(g, par, uses, i, tiles):
                for n in range(8):
                    maxima(g, n, (0, 1))
                    dve.wait_ge(kh_ready, PAIRS * g + n + 1)
                    nc.vector.tensor_tensor(ksl[par][:, n, :], kf[:, n % 4, :], ksh[par][:, n, :],
                                            ALU.subtract).then_inc(kl_ready, 1)
                    maxima(g, n, (2, 3))
                    dve.wait_ge(vh_ready, VT * g + n + 1)
                    kt, half = n // 2, n % 2
                    hs = slice(half * 8, (half + 1) * 8)
                    nc.vector.scalar_tensor_tensor(
                        vs[par][:, hs, kt, DH:2 * DH], vp[:, n % 2, :].rearrange("p (h d) -> p h d", d=DH),
                        1.0 / SW, vs[par][:, hs, kt, 0:DH], ALU.mult, ALU.subtract).then_inc(vl_ready, 1)
                    if n == 1 and (i is not None or g == 0):
                        dve.wait_ge(ch_ready, g + 2)
                        nxt = 1 - par
                        nc.vector.scalar_tensor_tensor(cl[nxt][:, :, :], cf[nxt][:, :, :], SA,
                                                       ch[nxt][:, :, :], ALU.mult,
                                                       ALU.subtract).then_inc(cl_ready, 1)
                    if n in tiles:
                        e = tiles[n]
                        dve.wait_ge(th_ready, i * TW + e + 1)
                        nc.vector.scalar_tensor_tensor(tl[e][:, :], tf[e][:, :], SW, th[e][:, :], ALU.mult,
                                                       ALU.subtract).then_inc(tl_ready, 1)

            chunks(dve, chunk)
            maxima(NCK, 0, range(MG))
            dve.wait_ge(s1_max, NCK * PAIRS * MG + 2)
            nc.vector.reduce_max(mr[:, :], mx.rearrange("p (c n) -> p n c", c=NCK), AX.X).then_inc(mr_ready, 1)
            dve.wait_ge(mr_ready, 1)
            nc.vector.tensor_scalar(negm[:, :], mr[:, :], -1.0 / ONE_K, LOG_P_MAX / SCORE / ONE_K, ALU.mult,
                                    ALU.add).then_inc(negm_ready, 1)

        @block.tensor
        def _(pe):
            def scores(g, par, n, q):
                if n == 0 and isinstance(g, int) and g == 0:
                    return
                j, keys = (n - 1) % PAIRS, ksh[par if n else 1 - par]
                pe.wait_ge(kh_ready, PAIRS * g + n)
                pe.wait_ge(s1_max, g * (PAIRS * MG) + (n - 1) * MG + q + 1)
                for e in range(2):
                    t = (q % 2) * 2 + e
                    last = nc.tensor.matmul(s1[:, t, :], keep.qz[q // 2][:, j, t * P:(t + 1) * P],
                                            keys[:, j, :], start=True, stop=True)
                last.then_inc(s1_ready, 1)

            def chunk(g, par, uses, i, tiles):
                pe.wait_ge(ch_ready, g + 1)
                pe.wait_ge(cl_ready, g + 1)
                for n in range(8):
                    pe.wait_ge(kf_ready, PAIRS * g + n + 1)
                    cols = slice(n * P, (n + 1) * P)
                    pairs = [p for c in range(DC) for p in three(keep.wkh[:, c, cols], keep.wkl[:, c, cols],
                                                                 ch[par][:, c, :], cl[par][:, c, :])]
                    product(nc, kp[:, n % 2, :], pairs[:6], stop=False)
                    scores(g, par, n, 0)
                    product(nc, kp[:, n % 2, :], pairs[6:], start=False).then_inc(k_ready, 1)
                    scores(g, par, n, 1)
                    pe.wait_ge(vl_ready, VT * g + n + 1)
                    kt, half = n // 2, n % 2
                    tok, cols = slice(kt * P, (kt + 1) * P), slice(half * 512, (half + 1) * 512)
                    pairs = [p for c in range(DC) for p in three(ch[par][:, c, tok], cl[par][:, c, tok],
                                                                 keep.wvh[:, c, cols], keep.wvl[:, c, cols])]
                    product(nc, vp[:, n % 2, :], pairs[:6], stop=False)
                    scores(g, par, n, 2)
                    product(nc, vp[:, n % 2, :], pairs[6:], start=False).then_inc(v_ready, 1)
                    scores(g, par, n, 3)

            chunks(pe, chunk)
            for q in range(MG):
                scores(NCK, 0, 0, q)
            pe.wait_ge(made, 2)
            pe.wait_ge(negm_ready, 1)
            nc.tensor.transpose(kp[0:NH * TT, 0, 0:P], negm[:, :], ident[:, :]).then_inc(mt_ready, 1)


RING = 8
LAG = 3
HP = KT // 2
PARTS = (slice(0, P), slice(DH, P), slice(0, P))
NQ = 4


def attention(nc, q_dram, m_dram, kd, vd, o_parts):
    with ExitStack() as ctx:
        m = Space(nc, ctx, "at")
        qh = m.sb("qh", [P, NH * T], F16)
        ql = m.sb("ql", [P, NH * T], F16)
        k_cur = m.sb("k_cur", [P, S], F16)
        k_one = m.sb("k_one", [P, S], F16)
        vs = m.sb("vs", [P, KT, P], F16)
        ones = m.sb("ones", [P, 32], F16)
        pf = m.sb("pf", [P, RING, 2, T])
        ph, pl = (m.sb(n, [P, RING, 2, T], F16) for n in ("ph", "pl"))
        parts = m.sb("parts", [P, 3, T])
        st = m.ps("st", [P, 2, 2, T])
        acc = m.ps("acc", [P, 3, T])

        q_in, q_rest_in, const_ready = m.sem("q_in"), m.sem("q_rest_in"), m.sem("const_ready")
        k_in = [m.sem(f"k_in{i}") for i in range(NQ)]
        v_in = [m.sem(f"v_in{i}") for i in range(NQ)]
        st_ready, pf_ready, ph_ready, ph_own = (m.sem(n) for n in ("st_ready", "pf_ready", "ph_ready", "ph_own"))
        pl_ready, pv_done, acc_read, o_out = (m.sem(n) for n in ("pl_ready", "pv_done", "acc_read", "o_out"))
        block = ctx.enter_context(nc.Block())
        QP = HP // NQ
        QK = S // NQ
        DVE_HI = 3

        @block.sync
        def _(sp):
            src = q_dram.rearrange("s (h d) t -> s d h t", d=DH)

            def load_queries(first, end, sem):
                for q, s, at in ((qh, 0, 0), (ql, 1, 0), (qh, 0, DH)):
                    sp.dma_start(q[at:at + DH, first * T:end * T].rearrange("d (h t) -> d h t", t=T),
                                 src[s][:, first:end, :]).then_inc(sem, 16)

            def load_keys(n, q):
                cols = slice(q * QK, (q + 1) * QK)
                for k, s, at in ((k_cur, 0, 0), (k_cur, 1, DH), (k_one, 0, 0)):
                    sp.dma_start(k[at:at + DH, cols],
                                 kd[s].rearrange("d h n -> d (h n)")[:, bass.ds(n * S + q * QK, QK)]).then_inc(k_in[q], 16)

            def load_values(n, q):
                sp.dma_start(vs[:, q * 2 * QP:(q + 1) * 2 * QP, :].rearrange("p k c -> p (k c)"),
                             vd.rearrange("h p s -> p h s")[:, bass.ds(n, 1), q * QK:(q + 1) * QK]
                             .rearrange("p h s -> p (h s)")).then_inc(v_in[q], 16)

            load_queries(0, 1, q_in)
            for q in range(NQ):
                load_keys(0, q)
                if q == 0:
                    sp.wait_ge(const_ready, 2)
                    sp.dma_start(ql[DH:DH + 1, :], m_dram.rearrange("(o n) -> o n", o=1)).then_inc(q_in, 16)
                load_values(0, q)
            load_queries(1, NH, q_rest_in)
            with sp.Fori(0, NH - 1) as h:
                for q in range(NQ):
                    sp.wait_ge(st_ready, h * HP + QP * (q + 1))
                    load_keys(h + 1, q)
                    sp.wait_ge(pv_done, h * HP + QP * (q + 1) + RING)
                    load_values(h + 1, q)
            sp.wait_ge(o_out, 48 * NH + 48)

        @block.gpsimd
        def _(pool):
            own = Chain(pool, const_ready)
            own.done(nc.gpsimd.memset(ones[:, :], 1.0))
            own.done(nc.gpsimd.memset(ql[DH:P, :], 0.0))
            own.done(nc.gpsimd.memset(k_one[DH:P, :], 0.0))
            own.done(nc.gpsimd.memset(k_one[DH:DH + 1, :], ONE_K))

        def turns(eng, pair, cut, end=None):
            for s in range(cut):
                pair(0, s)
            with eng.Fori(0, NH - 1) as h:
                for s in range(cut, HP + cut):
                    pair(h, s)
                if end:
                    end(h)
            for s in range(cut, HP):
                pair(NH - 1, s)
            if end:
                end(NH - 1)

        @block.scalar
        def _(act):
            def hi(h, s):
                g = h * HP + s
                act.wait_ge(pf_ready, g + 1)
                act.wait_ge(pv_done, g + 1)
                nc.scalar.activation(ph[:, s % RING, :, :], pf[:, s % RING, :, :], ACT.Copy).then_inc(ph_ready, 1)

            def pair(h, s):
                g = h * HP + s
                act.wait_ge(st_ready, g + 1)
                act.wait_ge(pl_ready, g + 1)
                nc.scalar.activation(pf[:, s % RING, :, :], st[:, s % 2, :, :], ACT.Exp,
                                     scale=SCORE).then_inc(pf_ready, 1)
                if s and (s - 1) % 4 != DVE_HI:
                    hi(h, s - 1)


            def end(h):
                act.wait_ge(acc_read, h * 3 + 6)
                for n, rows in enumerate(PARTS):
                    act.dma_start(o_parts[n][rows, bass.ds(h * T, T)],
                                  parts[rows, n, :]).then_inc(o_out, 16)

            turns(act, pair, LAG + 2, end)

        @block.vector
        def _(dve):
            dve.sem_inc(pl_ready, RING)
            dve.sem_inc(pv_done, RING)
            dve.sem_inc(acc_read, 3)
            dve.sem_inc(o_out, 48)

            def pair(h, s):
                g = h * HP + s
                if s % 4 == DVE_HI:
                    dve.wait_ge(pf_ready, g + 1)
                    dve.wait_ge(pv_done, g + 1)
                    nc.vector.tensor_copy(ph[:, s % RING, :, :], pf[:, s % RING, :, :]).then_inc(ph_own, 1)
                    dve.wait_ge(ph_own, h * (HP // 4) + s // 4 + 1)
                else:
                    dve.wait_ge(ph_ready, h * (HP // 4 * 3) + s // 4 * 3 + s % 4 + 1)
                nc.vector.tensor_tensor(pl[:, s % RING, :, :], pf[:, s % RING, :, :], ph[:, s % RING, :, :],
                                        ALU.subtract).then_inc(pl_ready, 1)

            def end(h):
                dve.wait_ge(pv_done, h * HP + HP + RING)
                dve.wait_ge(o_out, h * 48 + 48)
                for n, rows in enumerate(PARTS):
                    nc.vector.tensor_copy(parts[rows, n, :], acc[rows, n, :]).then_inc(acc_read, 1)

            turns(dve, pair, LAG - 2, end)

        @block.tensor
        def _(pe):
            def values(h, s):
                if s % QP == 0:
                    pe.wait_ge(v_in[s // QP], 16 * (h + 1))
                pe.wait_ge(pl_ready, h * HP + s + 1 + RING)
                first, final = s == 0, s == HP - 1
                r = s % RING
                if first:
                    pe.wait_ge(acc_read, h * 3 + 1)
                nc.tensor.matmul(acc[:, 0, :], vs[:, 2 * s, :], ph[:, r, 0, :], start=first, stop=False)
                if first:
                    pe.wait_ge(acc_read, h * 3 + 2)
                nc.tensor.matmul(acc[0:DH, 0, :], vs[:, 2 * s, 0:DH], pl[:, r, 0, :], start=False, stop=False)
                nc.tensor.matmul(acc[DH:P, 1, :], vs[:, 2 * s + 1, 0:DH], pl[:, r, 1, :], start=first, stop=final)
                nc.tensor.matmul(acc[:, 0, :], vs[:, 2 * s + 1, :], ph[:, r, 1, :], start=False, stop=final)
                if first:
                    pe.wait_ge(acc_read, h * 3 + 3)
                for e, (p, half) in enumerate((p, half) for p in (ph, pl) for half in range(2)):
                    last = nc.tensor.matmul(acc[e * 32:(e + 1) * 32, 2, :], ones[:, :], p[:, r, half, :],
                                            start=first, stop=final, tile_position=(0, e * 32))
                last.then_inc(pv_done, 1)

            def pair(h, s):
                ahead, w = divmod(s, HP)
                g = h * HP + s
                if ahead and w == 0:
                    pe.wait_ge(q_rest_in, 48)
                if w % QP == 0:
                    pe.wait_ge(k_in[w // QP], 48 * (h + ahead + 1))
                if not isinstance(g, int) or g >= 2:
                    pe.wait_ge(pf_ready, g - 1)
                q = bass.ds((h + ahead) * T, T)
                for e in range(2):
                    tile = slice((2 * w + e) * P, (2 * w + e + 1) * P)
                    nc.tensor.matmul(st[:, s % 2, e, :], k_cur[:, tile], qh[:, q], start=True, stop=False)
                    last = nc.tensor.matmul(st[:, s % 2, e, :], k_one[:, tile], ql[:, q], start=False, stop=True)
                last.then_inc(st_ready, 1)
                if s >= LAG:
                    values(h, s - LAG)

            pe.wait_ge(q_in, 64)
            pe.wait_ge(const_ready, 4)
            turns(pe, pair, LAG)
            for s in range(HP - LAG, HP):
                values(NH - 1, s)


class W:
    O = (0, 2)
    IN = (2, 4)
    W1 = (6, 4)
    W3 = (10, 4)
    W2 = (14, 4)
    OUT = (18, 2)
    SMALL = (20, 1)


def load_split(eng, wsplit, where, hi, lo, sem):
    at, n = where
    for s, t in enumerate((hi, lo)):
        eng.dma_start(t, wsplit[s][:, at:at + n, :].rearrange("p w n -> p (w n)")).then_inc(sem, 16)


UNSCALE = 1.0 / (SA * SW)


def row_factor(nc, dve, own, src, st, mv, var, sd, rs, tmp, var_ready, sd_ready, n, eps, rms):
    for t in range(TT):
        own.inc(nc.vector.bn_stats(st[:, t, :], src[:, t, :]))
    own.wait()
    for t in range(TT):
        own.inc(nc.vector.bn_aggr(mv[:, t, :], st[:, t, :]))
    own.wait()
    if rms:
        own.done(nc.vector.tensor_tensor(tmp[:, :], mv[:, :, 0], mv[:, :, 0], ALU.mult))
        own.done(nc.vector.tensor_tensor(tmp[:, :], tmp[:, :], mv[:, :, 1], ALU.add))
        nc.vector.tensor_scalar(var[:, :], tmp[:, :], eps, None, ALU.add).then_inc(var_ready, 1)
    else:
        nc.vector.tensor_scalar(var[:, :], mv[:, :, 1], eps, None, ALU.add).then_inc(var_ready, 1)
    dve.wait_ge(var_ready, n)
    dve.wait_ge(sd_ready, n)
    own.done(nc.vector.reciprocal(rs[:, :], sd[:, :]))
    own.done(nc.vector.tensor_tensor(tmp[:, :], rs[:, :], rs[:, :], ALU.mult))
    own.done(nc.vector.tensor_tensor(tmp[:, :], tmp[:, :], var[:, :], ALU.mult))
    own.done(nc.vector.tensor_scalar(tmp[:, :], tmp[:, :], -0.5, 1.5, ALU.mult, ALU.add))
    own.done(nc.vector.tensor_tensor(rs[:, :], rs[:, :], tmp[:, :], ALU.mult))


class Rows:

    def __init__(self, m):
        self.st, self.mv = m.sb("st", [P, TT, 6]), m.sb("mv", [P, TT, 2])
        self.var, self.sd, self.rs, self.tmp = (m.sb(n, [P, TT]) for n in ("var", "sd", "rs", "tmp"))
        self.all = (self.st, self.mv, self.var, self.sd, self.rs, self.tmp)


def transpose_rows(nc, src, dst, ident, ready):
    for c in range(DC):
        for t in range(TT):
            last = nc.tensor.transpose(dst[:, c, t * P:(t + 1) * P], src[:, t, c * P:(c + 1) * P], ident[:, :])
        last.then_inc(ready, 1)


def product(nc, out, pairs, start=True, stop=True):
    for n, (a, b) in enumerate(pairs):
        last = nc.tensor.matmul(out, a, b, start=(start and n == 0), stop=(stop and n == len(pairs) - 1))
    return last


def three(ah, al, bh, bl):
    return [(ah, bh), (ah, bl), (al, bh)]


def project_attention(nc, keep, x, o_parts, r_dram, bv, bo, n1w, wsplit):
    with ExitStack() as ctx:
        m = Space(nc, ctx, "pa")
        a0, a1, a2 = (m.sb(f"a{i}", [P, PAIRS, T]) for i in range(3))
        rb = m.sb("rb", [P, PAIRS, T])
        dn = m.sb("dn", [P, 4, DH])
        oh, ol = (m.sb(n, [P, PAIRS, T], F16) for n in ("oh", "ol"))
        woh, wol = (m.sb(n, [P, PAIRS, D], F16) for n in ("woh", "wol"))
        bvc, bvs, nw, nws = (m.sb(n, [P, k]) for n, k in (("bvc", PAIRS), ("bvs", PAIRS), ("nw", DC), ("nws", DC)))
        bob, xs, h = m.sb("bob", [P, D]), m.sb("xs", [P, TT, D]), m.sb("h", [P, TT, D])
        rows = Rows(m)
        ident = m.sb("ident", [P, P])
        yp = m.ps("yp", [P, TT, D])
        hT = m.ps("hT", [P, DC, T])
        parts_in, den_in, small_in, w_in = m.sem("parts_in"), m.sem("den_in"), m.sem("small_in"), m.sem("w_in")
        next_in, consts = m.sem("next_in"), m.sem("consts")
        r_ready, r_out, rb_in, own_dve = m.sem("r_ready"), m.sem("r_out"), m.sem("rb_in"), m.sem("own_dve")
        s_ready, oh_ready, ol_ready, y_ready = m.sem("s_ready"), m.sem("oh_ready"), m.sem("ol_ready"), m.sem("y_ready")
        var_ready, sd_ready, h_ready = m.sem("var_ready"), m.sem("sd_ready"), m.sem("h_ready")
        hT_ready, hh_ready, hl_ready, made = m.sem("hT_ready"), m.sem("hh_ready"), m.sem("hl_ready"), m.sem("made")
        block = ctx.enter_context(nc.Block())

        @block.sync
        def _(sp):
            for e in range(4):
                sp.dma_start(dn[:, e, :], o_parts[2][e * 32].rearrange("(p c) -> p c", p=P)).then_inc(den_in, 16)
            for hd in range(2):
                for n, (dst, rows_) in enumerate(((a0, 0), (a1, DH), (a2, DH))):
                    src = o_parts[n // 2][rows_:rows_ + DH, :].rearrange("p (j e t) -> p j e t", e=2, t=T)
                    sp.dma_start(dst[hd * DH:(hd + 1) * DH, :, :], src[:, :, hd, :]).then_inc(parts_in, 16)
            sp.dma_start(xs[:, :, :], x.rearrange("(t p) d -> p t d", p=P)).then_inc(small_in, 16)
            sp.dma_start(bob[:, :], bo.partition_broadcast(P)).then_inc(small_in, 16)
            sp.dma_start(bvc[:, :], bv).then_inc(small_in, 16)
            sp.dma_start(nw[:, :], n1w).then_inc(small_in, 16)
            load_split(sp, wsplit, W.O, woh.rearrange("p j d -> p (j d)"), wol.rearrange("p j d -> p (j d)"), w_in)
            sp.wait_ge(r_ready, 1)
            sp.dma_start(r_dram.rearrange("(p c) -> p c", p=P), dn[:, 0, :]).then_inc(r_out, 16)
            sp.wait_ge(r_out, 16)
            for hd in range(2):
                src = r_dram.rearrange("(j e t) -> j e t", e=2, t=T)[:, hd, :].partition_broadcast(DH)
                sp.dma_start(rb[hd * DH:(hd + 1) * DH, :, :], src).then_inc(rb_in, 16)
            load_split(sp, wsplit, W.IN, keep.big[0][:, :], keep.big[1][:, :], next_in)
            sp.wait_ge(rb_in, 32)
            sp.wait_ge(next_in, 32)

        @block.gpsimd
        def _(pool):
            identity(nc, pool, ident, made)

        @block.scalar
        def _(act):
            act.wait_ge(consts, 2)
            for j in range(PAIRS):
                act.wait_ge(s_ready, j + 1)
                nc.scalar.activation(oh[:, j, :], a0[:, j, :], ACT.Identity, bias=bvs[:, j:j + 1]).then_inc(oh_ready, 1)
            for n in range(2):
                act.wait_ge(var_ready, n + 1)
                nc.scalar.activation(rows.sd[:, :], rows.var[:, :], ACT.Sqrt).then_inc(sd_ready, 1)
            act.wait_ge(small_in, 64)
            for c in range(DC):
                act.wait_ge(hT_ready, c + 1)
                nc.scalar.activation(keep.hh[:, c, :], hT[:, c, :], ACT.Copy, scale=nws[:, c:c + 1]).then_inc(hh_ready, 1)

        @block.vector
        def _(dve):
            own = Chain(dve, own_dve)
            dve.wait_ge(den_in, 64)
            for e in range(1, 4):
                own.done(nc.vector.tensor_tensor(dn[:, 0, :], dn[:, 0, :], dn[:, e, :], ALU.add))
            nc.vector.reciprocal(dn[:, 0, :], dn[:, 0, :]).then_inc(r_ready, 1)
            dve.wait_ge(small_in, 64)
            nc.vector.tensor_scalar(bvs[:, :], bvc[:, :], SA, None, ALU.mult).then_inc(consts, 1)
            nc.vector.tensor_scalar(nws[:, :], nw[:, :], SA, None, ALU.mult).then_inc(consts, 1)
            for t in range(TT):
                own.inc(nc.vector.tensor_tensor(xs[:, t, :], xs[:, t, :], bob[:, :], ALU.add))
            dve.wait_ge(parts_in, 96)
            own.done(nc.vector.tensor_tensor(a0[:, :, :], a0[:, :, :], a1[:, :, :], ALU.add))
            dve.wait_ge(consts, 2)

            def low(j):
                dve.wait_ge(oh_ready, j + 1)
                nc.vector.scalar_tensor_tensor(ol[:, j, :], a0[:, j, :], bvs[:, j:j + 1], oh[:, j, :],
                                               ALU.add, ALU.subtract).then_inc(ol_ready, 1)

            for j in range(PAIRS):
                own.done(nc.vector.tensor_tensor(a0[:, j, :], a0[:, j, :], a2[:, j, :], ALU.add))
                if j == 0:
                    dve.wait_ge(rb_in, 32)
                nc.vector.tensor_tensor(a0[:, j, :], a0[:, j, :], rb[:, j, :], ALU.mult).then_inc(s_ready, 1)
                if j:
                    low(j - 1)
            low(PAIRS - 1)
            for t in range(TT):
                dve.wait_ge(y_ready, t + 1)
                own.inc(nc.vector.scalar_tensor_tensor(keep.x1[:, t, :], yp[:, t, :], UNSCALE, xs[:, t, :],
                                                       ALU.mult, ALU.add))
            own.wait()
            row_factor(nc, dve, own, keep.x1, *rows.all, var_ready, sd_ready, 1, 1e-5, False)
            for t in range(TT):
                own.inc(nc.vector.tensor_scalar(keep.a[:, t, :], keep.x1[:, t, :], rows.mv[:, t, 0:1],
                                                rows.rs[:, t:t + 1], ALU.subtract, ALU.mult))
            own.wait()
            row_factor(nc, dve, own, keep.a, *rows.all, var_ready, sd_ready, 2, 1e-6, True)
            for t in range(TT):
                nc.vector.tensor_scalar(h[:, t, :], keep.a[:, t, :], rows.rs[:, t:t + 1], None,
                                        ALU.mult).then_inc(h_ready, 1)
            for c in range(DC):
                dve.wait_ge(hh_ready, c + 1)
                nc.vector.scalar_tensor_tensor(keep.hl[:, c, :], hT[:, c, :], nws[:, c:c + 1], keep.hh[:, c, :],
                                               ALU.mult, ALU.subtract).then_inc(hl_ready, 1)

        @block.tensor
        def _(pe):
            pe.wait_ge(made, 2)
            pe.wait_ge(w_in, 32)
            for j in range(PAIRS):
                pe.wait_ge(ol_ready, j + 1)
                for t in range(TT):
                    tok = slice(t * P, (t + 1) * P)
                    last = product(nc, yp[:, t, :], three(oh[:, j, tok], ol[:, j, tok], woh[:, j, :], wol[:, j, :]),
                                   start=(j == 0), stop=(j == PAIRS - 1))
                    if j == PAIRS - 1:
                        last.then_inc(y_ready, 1)
            pe.wait_ge(h_ready, TT)
            transpose_rows(nc, h, hT, ident, hT_ready)


DI = 1024
DIC = DI // P
DS = 16
DR = 32


def mamba_inputs(nc, keep, convw, convb, dtb, xd_dram, wsplit):
    with ExitStack() as ctx:
        m = Space(nc, ctx, "mi")
        wh, wl = (keep.big[i].rearrange("p (c n) -> p c n", c=DC) for i in range(2))
        sh, sl = (m.sb(n, [P, WC], F16) for n in ("sh", "sl"))
        xp = m.sb("xp", [P, DIC, T + 3])
        cw, cb, db = m.sb("cw", [P, DIC, 4]), m.sb("cb", [P, DIC]), m.sb("db", [P, DIC])
        xih, xil = keep.yh, keep.yl
        xd = m.sb("xd", [2 * DS + DR, T])
        dh, dl = (m.sb(n, [DR, T], F16) for n in ("dh", "dl"))
        pre, soft = keep.delta, m.sb("soft", [P, DIC, T])
        zp = m.ps("zp", [P, 4, T])
        xdp = m.ps("xdp", [2 * DS + DR, T])
        dp = m.ps("dp", [P, 2, T])
        small_in, pad, own_dve = m.sem("small_in"), m.sem("pad"), m.sem("own_dve")
        p_ready, p_read = m.sem("p_ready"), m.sem("p_read")
        conv_ready, xin_ready, xih_ready, xil_ready = (m.sem(n) for n in ("conv_ready", "xin_ready", "xih_ready", "xil_ready"))
        xd_ready, xd_read, xd_out, dh_ready, dl_ready = (m.sem(n) for n in ("xd_ready", "xd_read", "xd_out", "dh_ready", "dl_ready"))
        d_ready, pre_ready, abs_ready, ln_ready = (m.sem(n) for n in ("d_ready", "pre_ready", "abs_ready", "ln_ready"))
        block = ctx.enter_context(nc.Block())
        xpw = [s[:, 0:DIC * 64].rearrange("p (c n) -> p c n", c=DIC) for s in (sh, sl)]
        dtw = [s[0:DR, DIC * 64 + 64:DIC * 64 + 64 + DI] for s in (sh, sl)]

        @block.sync
        def _(sp):
            sp.dma_start(cw[:, :, :], convw).then_inc(small_in, 16)
            sp.dma_start(cb[:, :], convb).then_inc(small_in, 16)
            sp.dma_start(db[:, :], dtb).then_inc(small_in, 16)
            load_split(sp, wsplit, W.SMALL, sh[:, :], sl[:, :], small_in)
            sp.wait_ge(xd_read, 1)
            sp.dma_start(xd_dram, xd[DR:DR + 2 * DS, :]).then_inc(xd_out, 16)
            sp.wait_ge(xd_out, 16)

        @block.gpsimd
        def _(pool):
            nc.gpsimd.memset(xp[:, :, 0:3], 0.0).then_inc(pad, 1)

        @block.scalar
        def _(act):
            for f in range(2 * DIC):
                act.wait_ge(p_ready, f + 1)
                if f < DIC:
                    nc.scalar.activation(xp[:, f, 3:], zp[:, f % 4, :], ACT.Copy, scale=UNSCALE).then_inc(p_read, 1)
                else:
                    c = f - DIC
                    nc.scalar.activation(keep.zs[:, c, :], zp[:, f % 4, :], ACT.Silu, scale=UNSCALE).then_inc(p_read, 1)
                    if f == DIC:
                        act.wait_ge(small_in, 80)
                    act.wait_ge(conv_ready, c + 1)
                    nc.scalar.activation(keep.xin[:, c, :], soft[:, c, :], ACT.Silu, bias=cb[:, c:c + 1]).then_inc(xin_ready, 1)
                    act.wait_ge(xin_ready, c + 1)
                    nc.scalar.activation(xih[:, c, :], keep.xin[:, c, :], ACT.Copy, scale=SA).then_inc(xih_ready, 1)
            act.wait_ge(xd_ready, 1)
            nc.scalar.activation(xd[:, :], xdp[:, :], ACT.Copy, scale=UNSCALE).then_inc(xd_read, 1)
            act.wait_ge(xd_read, 1)
            nc.scalar.activation(dh[:, :], xd[0:DR, :], ACT.Copy, scale=SA).then_inc(dh_ready, 1)
            for f in range(DIC):
                act.wait_ge(d_ready, f + 1)
                nc.scalar.activation(pre[:, f, :], dp[:, f % 2, :], ACT.Identity, bias=db[:, f:f + 1],
                                     scale=UNSCALE).then_inc(pre_ready, 1)
            act.wait_ge(pre_ready, DIC)
            act.wait_ge(xin_ready, DIC)
            nc.scalar.activation(soft[:, :, :], pre[:, :, :], ACT.Abs).then_inc(abs_ready, 1)
            act.wait_ge(abs_ready, 1)
            nc.scalar.activation(soft[:, :, :], soft[:, :, :], ACT.Exp, scale=-1.0).then_inc(ln_ready, 1)
            act.wait_ge(ln_ready, 1)
            nc.scalar.activation(soft[:, :, :], soft[:, :, :], ACT.Ln, bias=1.0).then_inc(ln_ready, 1)

        @block.vector
        def _(dve):
            own = Chain(dve, own_dve)
            dve.wait_ge(small_in, 80)
            dve.wait_ge(pad, 1)
            for f in range(DIC):
                dve.wait_ge(p_read, f + 1)
                c = soft[:, f, :]
                own.done(nc.vector.tensor_scalar(c, xp[:, f, 0:T], cw[:, f, 0:1], None, ALU.mult))
                for k in range(1, 4):
                    ins = nc.vector.scalar_tensor_tensor(c, xp[:, f, k:k + T], cw[:, f, k:k + 1], c, ALU.mult, ALU.add)
                    if k < 3:
                        own.done(ins)
                ins.then_inc(conv_ready, 1)
            for f in range(DIC):
                dve.wait_ge(xih_ready, f + 1)
                nc.vector.scalar_tensor_tensor(xil[:, f, :], keep.xin[:, f, :], SA, xih[:, f, :], ALU.mult,
                                               ALU.subtract).then_inc(xil_ready, 1)
            dve.wait_ge(dh_ready, 1)
            nc.vector.scalar_tensor_tensor(dl[:, :], xd[0:DR, :], SA, dh[:, :], ALU.mult, ALU.subtract).then_inc(dl_ready, 1)
            dve.wait_ge(abs_ready, 1)
            own.done(nc.vector.tensor_scalar(pre[:, :, :], pre[:, :, :], 0.0, None, ALU.max))
            dve.wait_ge(ln_ready, 2)
            own.inc(nc.vector.tensor_tensor(pre[:, :, :], pre[:, :, :], soft[:, :, :], ALU.add))

        @block.tensor
        def _(pe):
            for f in range(2 * DIC):
                if f >= 4:
                    pe.wait_ge(p_read, f - 3)
                cols = slice(f * P, (f + 1) * P)
                product(nc, zp[:, f % 4, :], [p for c in range(DC) for p in
                                              three(wh[:, c, cols], wl[:, c, cols], keep.hh[:, c, :], keep.hl[:, c, :])]
                        ).then_inc(p_ready, 1)
            pe.wait_ge(small_in, 80)
            pe.wait_ge(xil_ready, DIC)
            product(nc, xdp[:, :], [p for c in range(DIC) for p in
                                    three(xpw[0][:, c, :], xpw[1][:, c, :], xih[:, c, :], xil[:, c, :])]
                    ).then_inc(xd_ready, 1)
            pe.wait_ge(dl_ready, 1)
            for f in range(DIC):
                if f >= 2:
                    pe.wait_ge(pre_ready, f - 1)
                cols = slice(f * P, (f + 1) * P)
                product(nc, dp[:, f % 2, :], three(dtw[0][:, cols], dtw[1][:, cols], dh[:, :], dl[:, :])
                        ).then_inc(d_ready, 1)


def mamba_scan(nc, keep, a_log, dskip, xd_dram, wsplit):
    HN = 4
    PASSES = DS // HN
    with ExitStack() as ctx:
        m = Space(nc, ctx, "ms")
        bb, cc = ([keep.big[i + q // 2][:, (q % 2) * 2 * WC:(q % 2 + 1) * 2 * WC].bitcast(F32)
                   .rearrange("p (n t) -> p n t", t=T) for q in range(PASSES)] for i in (0, 2))
        al, aneg, dk = m.sb("al", [P, DIC, DS]), m.sb("aneg", [P, DIC, DS]), m.sb("dk", [P, DIC])
        da = [m.sb(f"da{i}", [P, HN, T]) for i in range(2)]
        hs = [m.sb(f"hs{i}", [P, HN, T]) for i in range(2)]
        u = m.sb("u", [P, T])
        y = m.sb("y", [P, 2, T])
        ident = m.sb("ident", [P, P])
        yp = m.ps("yp", [P, 2, T])
        in_sem, made, a_ready, zero_ready = m.sem("in_sem"), m.sem("made"), m.sem("a_ready"), m.sem("zero_ready")
        da_ready, scanned, hc_ready, summed = (m.sem(n) for n in ("da_ready", "scanned", "hc_ready", "summed"))
        b_in, c_in = ([m.sem(f"{n}{q}") for q in range(PASSES)] for n in ("b_in", "c_in"))
        next_in = m.sem("next_in")
        own_dve, y_ready, yh_ready, yl_ready = (m.sem(n) for n in ("own_dve", "y_ready", "yh_ready", "yl_ready"))
        block = ctx.enter_context(nc.Block())
        passes = [(f, q) for f in range(DIC) for q in range(PASSES)]

        @block.sync
        def _(sp):
            sp.dma_start(al[:, :, :], a_log).then_inc(in_sem, 16)
            sp.dma_start(dk[:, :], dskip).then_inc(in_sem, 16)
            for q in range(PASSES):
                for dst, at, sem in ((bb, q * HN, b_in[q]), (cc, DS + q * HN, c_in[q])):
                    sp.dma_start(dst[q], xd_dram[at:at + HN, :].partition_broadcast(P)).then_inc(sem, 16)
            load_split(sp, wsplit, W.OUT, keep.hidden.rearrange("p c n -> p (c n)"),
                       keep.outl.rearrange("p c n -> p (c n)"), next_in)
            sp.wait_ge(next_in, 32)

        @block.gpsimd
        def _(pool):
            identity(nc, pool, ident, made)
            for i in range(2):
                nc.gpsimd.memset(da[i][:, :, 0:1], 0.0).then_inc(zero_ready, 1)

        @block.scalar
        def _(act):
            def high(f):
                act.wait_ge(y_ready, f + 1)
                nc.scalar.activation(keep.yh[:, f, :], y[:, f % 2, :], ACT.Copy, scale=SA).then_inc(yh_ready, 1)

            act.wait_ge(in_sem, 32)
            nc.scalar.activation(aneg[:, :, :], al[:, :, :], ACT.Exp).then_inc(a_ready, 1)
            act.wait_ge(a_ready, 2)
            act.wait_ge(zero_ready, 2)
            for i, (f, q) in enumerate(passes):
                if i >= 2:
                    act.wait_ge(scanned, i - 1)
                for n in range(HN):
                    s = q * HN + n
                    last = nc.scalar.activation(da[i % 2][:, n, 1:], keep.delta[:, f, 1:], ACT.Exp,
                                                scale=aneg[:, f, s:s + 1])
                last.then_inc(da_ready, 1)
                if q == 2 and f:
                    high(f - 1)
            high(DIC - 1)

        @block.vector
        def _(dve):
            own = Chain(dve, own_dve)
            dve.wait_ge(a_ready, 1)
            nc.vector.tensor_scalar(aneg[:, :, :], aneg[:, :, :], -1.0, None, ALU.mult).then_inc(a_ready, 1)

            def gate(f):
                dve.wait_ge(summed, PASSES * (f + 1))
                if f >= 2:
                    dve.wait_ge(yl_ready, f - 1)
                own.done(nc.vector.scalar_tensor_tensor(y[:, f % 2, :], keep.xin[:, f, :], dk[:, f:f + 1],
                                                        yp[:, f % 2, :], ALU.mult, ALU.add))
                nc.vector.tensor_tensor(y[:, f % 2, :], y[:, f % 2, :], keep.zs[:, f, :], ALU.mult).then_inc(y_ready, 1)

            def low(f):
                dve.wait_ge(yh_ready, f + 1)
                nc.vector.scalar_tensor_tensor(keep.yl[:, f, :], y[:, f % 2, :], SA, keep.yh[:, f, :], ALU.mult,
                                               ALU.subtract).then_inc(yl_ready, 1)

            for i, (f, q) in enumerate(passes):
                b = hs[i % 2]
                if q == 0:
                    own.done(nc.vector.tensor_tensor(u[:, :], keep.delta[:, f, :], keep.xin[:, f, :], ALU.mult))
                if i >= 2:
                    dve.wait_ge(summed, i - 1)
                if f == 0:
                    dve.wait_ge(b_in[q], 16)
                own.done(nc.vector.tensor_tensor(b[:, :, :], u[:, :].unsqueeze(1).to_broadcast([P, HN, T]),
                                                 bb[q], ALU.mult))
                dve.wait_ge(da_ready, i + 1)
                flat = b.rearrange("p n t -> p (n t)")
                nc.vector.tensor_tensor_scan(flat, da[i % 2].rearrange("p n t -> p (n t)"), flat, 0.0,
                                             ALU.mult, ALU.add).then_inc(scanned, 1)
                dve.wait_ge(scanned, i + 1)
                if f == 0:
                    dve.wait_ge(c_in[q], 16)
                nc.vector.tensor_tensor(b[:, :, :], b[:, :, :], cc[q], ALU.mult).then_inc(hc_ready, 1)
                if q == 1 and f:
                    gate(f - 1)
                if q == 3 and f:
                    low(f - 1)
            gate(DIC - 1)
            low(DIC - 1)

        @block.tensor
        def _(pe):
            pe.wait_ge(made, 2)
            for i, (f, q) in enumerate(passes):
                pe.wait_ge(hc_ready, i + 1)
                if q == 0 and f >= 2:
                    pe.wait_ge(y_ready, f - 1)
                for n in range(HN):
                    last = nc.tensor.matmul(yp[:, f % 2, :], ident[:, :], hs[i % 2][:, n, :],
                                            start=(q == 0 and n == 0), stop=(q == PASSES - 1 and n == HN - 1))
                last.then_inc(summed, 1)


def mamba_output(nc, keep, n2w, wsplit):
    with ExitStack() as ctx:
        m = Space(nc, ctx, "mo")
        wh, wl = keep.hidden, keep.outl
        nw, nws, h = m.sb("nw", [P, DC]), m.sb("nws", [P, DC]), m.sb("h", [P, TT, D])
        rows = Rows(m)
        ident = m.sb("ident", [P, P])
        op = m.ps("op", [P, TT, D])
        hT = m.ps("hT", [P, DC, T])
        next_in, n_in, own_dve, o_ready, made = (m.sem(n) for n in ("next_in", "n_in", "own_dve", "o_ready", "made"))
        var_ready, sd_ready, h_ready = m.sem("var_ready"), m.sem("sd_ready"), m.sem("h_ready")
        hT_ready, hh_ready, hl_ready = m.sem("hT_ready"), m.sem("hh_ready"), m.sem("hl_ready")
        nws_ready = m.sem("nws_ready")
        block = ctx.enter_context(nc.Block())

        @block.sync
        def _(sp):
            sp.dma_start(nw[:, :], n2w).then_inc(n_in, 16)
            load_split(sp, wsplit, W.W1, keep.big[0][:, :], keep.big[1][:, :], next_in)
            load_split(sp, wsplit, W.W3, keep.big[2][:, :], keep.big[3][:, :], next_in)
            sp.wait_ge(next_in, 64)

        @block.gpsimd
        def _(pool):
            identity(nc, pool, ident, made)

        @block.scalar
        def _(act):
            act.wait_ge(var_ready, 1)
            nc.scalar.activation(rows.sd[:, :], rows.var[:, :], ACT.Sqrt).then_inc(sd_ready, 1)
            act.wait_ge(nws_ready, 1)
            for c in range(DC):
                act.wait_ge(hT_ready, c + 1)
                nc.scalar.activation(keep.hh[:, c, :], hT[:, c, :], ACT.Copy, scale=nws[:, c:c + 1]).then_inc(hh_ready, 1)

        @block.vector
        def _(dve):
            own = Chain(dve, own_dve)
            dve.wait_ge(n_in, 16)
            nc.vector.tensor_scalar(nws[:, :], nw[:, :], SA, None, ALU.mult).then_inc(nws_ready, 1)
            dve.wait_ge(nws_ready, 1)
            for t in range(TT):
                dve.wait_ge(o_ready, t + 1)
                own.inc(nc.vector.scalar_tensor_tensor(keep.a[:, t, :], op[:, t, :], UNSCALE, keep.a[:, t, :],
                                                       ALU.mult, ALU.add))
            own.wait()
            row_factor(nc, dve, own, keep.a, *rows.all, var_ready, sd_ready, 1, 1e-6, True)
            for t in range(TT):
                nc.vector.tensor_scalar(h[:, t, :], keep.a[:, t, :], rows.rs[:, t:t + 1], None,
                                        ALU.mult).then_inc(h_ready, 1)
            for c in range(DC):
                dve.wait_ge(hh_ready, c + 1)
                nc.vector.scalar_tensor_tensor(keep.hl[:, c, :], hT[:, c, :], nws[:, c:c + 1], keep.hh[:, c, :],
                                               ALU.mult, ALU.subtract).then_inc(hl_ready, 1)

        @block.tensor
        def _(pe):
            pe.wait_ge(made, 2)
            for t in range(TT):
                tok = slice(t * P, (t + 1) * P)
                product(nc, op[:, t, :], [p for j in range(DIC) for p in
                                          three(keep.yh[:, j, tok], keep.yl[:, j, tok], wh[:, j, :], wl[:, j, :])]
                        ).then_inc(o_ready, 1)
            pe.wait_ge(h_ready, TT)
            transpose_rows(nc, h, hT, ident, hT_ready)


DF = 2048
DFC = DF // P
NE = 16
NX = NE + 2
EH = 512
EHC = EH // P


class ExpertPlaces:

    def __init__(self, keep):
        b = keep.big
        f32 = lambda t: t.bitcast(F32)
        self.gf = [f32(b[i][:, :]).rearrange("p (c n) -> p c n", c=DC) for i in (0, 2)]
        self.df = [f32(b[1][:, i * 2 * WC:(i + 1) * 2 * WC]).rearrange("p (c n) -> p c n", c=EHC) for i in range(2)]
        self.gh, self.gl = ([b[3][:, i * 2 * WC:(i + 1) * 2 * WC].rearrange("p (c n) -> p c n", c=DC)] for i in range(2))


def gated_mlp(nc, keep, wsplit, gate_up, down):
    with ExitStack() as ctx:
        m = Space(nc, ctx, "gm")
        w1h, w1l, w3h, w3l = (b.rearrange("p (c n) -> p c n", c=DC) for b in keep.big)
        ex = ExpertPlaces(keep)
        w2h, w2l = (m.sb(n, [P, DFC, D], F16) for n in ("w2h", "w2l"))
        sg, mf = m.sb("sg", [P, 2, T]), m.sb("mf", [P, 2, T])
        mh, ml = (m.sb(n, [P, DFC, T], F16) for n in ("mh", "ml"))
        rows = Rows(m)
        gp, up = m.ps("gp", [P, 2, T]), m.ps("up", [P, 2, T])
        op = m.ps("op", [P, TT, D])
        w2_in, own_dve = m.sem("w2_in"), m.sem("own_dve")
        next_in, next_h, next_l = m.sem("next_in"), m.sem("next_h"), m.sem("next_l")
        g_ready, u_ready, sg_ready, mf_ready, mh_ready, ml_ready = (
            m.sem(n) for n in ("g_ready", "u_ready", "sg_ready", "mf_ready", "mh_ready", "ml_ready"))
        o_ready, var_ready, sd_ready = m.sem("o_ready"), m.sem("var_ready"), m.sem("sd_ready")
        block = ctx.enter_context(nc.Block())

        @block.sync
        def _(sp):
            load_split(sp, wsplit, W.W2, w2h.rearrange("p c n -> p (c n)"), w2l.rearrange("p c n -> p (c n)"), w2_in)
            sp.wait_ge(u_ready, DFC)
            sp.dma_start(ex.gf[0], gate_up[0:D, :].rearrange("(c p) n -> p c n", p=P)).then_inc(next_in, 16)
            sp.dma_start(ex.df[0], down[0:EH, :].rearrange("(c p) n -> p c n", p=P)).then_inc(next_in, 16)
            sp.wait_ge(next_in, 32)

        @block.scalar
        def _(act):
            for f in range(DFC):
                act.wait_ge(g_ready, f + 1)
                if f >= 2:
                    act.wait_ge(mf_ready, f - 1)
                nc.scalar.activation(sg[:, f % 2, :], gp[:, f % 2, :], ACT.Silu, scale=UNSCALE).then_inc(sg_ready, 1)
                if f:
                    act.wait_ge(mf_ready, f)
                    nc.scalar.activation(mh[:, f - 1, :], mf[:, (f - 1) % 2, :], ACT.Copy).then_inc(mh_ready, 1)
            act.wait_ge(mf_ready, DFC)
            nc.scalar.activation(mh[:, DFC - 1, :], mf[:, (DFC - 1) % 2, :], ACT.Copy).then_inc(mh_ready, 1)
            act.wait_ge(next_in, 32)
            nc.scalar.activation(ex.gh[0], ex.gf[0], ACT.Copy, scale=SW).then_inc(next_h, 1)
            act.wait_ge(var_ready, 1)
            nc.scalar.activation(rows.sd[:, :], rows.var[:, :], ACT.Sqrt).then_inc(sd_ready, 1)

        @block.vector
        def _(dve):
            own = Chain(dve, own_dve)

            def low(f):
                dve.wait_ge(mh_ready, f + 1)
                nc.vector.tensor_tensor(ml[:, f, :], mf[:, f % 2, :], mh[:, f, :], ALU.subtract).then_inc(ml_ready, 1)

            for f in range(DFC):
                if f >= 2:
                    low(f - 2)
                    dve.wait_ge(ml_ready, f - 1)
                dve.wait_ge(u_ready, f + 1)
                dve.wait_ge(sg_ready, f + 1)
                nc.vector.scalar_tensor_tensor(mf[:, f % 2, :], up[:, f % 2, :], SA * UNSCALE, sg[:, f % 2, :],
                                               ALU.mult, ALU.mult).then_inc(mf_ready, 1)
            for t in range(TT):
                own.inc(nc.vector.tensor_tensor(keep.x1[:, t, :], keep.x1[:, t, :], keep.a[:, t, :], ALU.add))
            low(DFC - 2)
            low(DFC - 1)
            dve.wait_ge(next_h, 1)
            nc.vector.scalar_tensor_tensor(ex.gl[0], ex.gf[0], SW, ex.gh[0], ALU.mult,
                                           ALU.subtract).then_inc(next_l, 1)
            own.wait()
            for t in range(TT):
                dve.wait_ge(o_ready, t + 1)
                own.inc(nc.vector.scalar_tensor_tensor(keep.x1[:, t, :], op[:, t, :], UNSCALE, keep.x1[:, t, :],
                                                       ALU.mult, ALU.add))
            own.wait()
            row_factor(nc, dve, own, keep.x1, *rows.all, var_ready, sd_ready, 1, 1e-5, False)
            for t in range(TT):
                own.inc(nc.vector.tensor_scalar(keep.a[:, t, :], keep.x1[:, t, :], rows.mv[:, t, 0:1],
                                                rows.rs[:, t:t + 1], ALU.subtract, ALU.mult))

        @block.tensor
        def _(pe):
            for f in range(DFC):
                cols = slice(f * P, (f + 1) * P)
                if f >= 2:
                    pe.wait_ge(sg_ready, f - 1)
                product(nc, gp[:, f % 2, :], [p for c in range(DC) for p in
                                              three(w1h[:, c, cols], w1l[:, c, cols], keep.hh[:, c, :], keep.hl[:, c, :])]
                        ).then_inc(g_ready, 1)
                if f >= 2:
                    pe.wait_ge(mf_ready, f - 1)
                product(nc, up[:, f % 2, :], [p for c in range(DC) for p in
                                              three(w3h[:, c, cols], w3l[:, c, cols], keep.hh[:, c, :], keep.hl[:, c, :])]
                        ).then_inc(u_ready, 1)
            pe.wait_ge(w2_in, 32)
            pe.wait_ge(ml_ready, DFC)
            for t in range(TT):
                tok = slice(t * P, (t + 1) * P)
                product(nc, op[:, t, :], [p for j in range(DFC) for p in
                                          three(mh[:, j, tok], ml[:, j, tok], w2h[:, j, :], w2l[:, j, :])]
                        ).then_inc(o_ready, 1)




def route(nc, keep, gates, wsplit):
    with ExitStack() as ctx:
        m = Space(nc, ctx, "ro")
        rh, rl = (m.sb(n, [P, DC, NE], F16) for n in ("rh", "rl"))
        ident = m.sb("ident", [P, P])
        shape = [P, TT, NE]
        lg, rank, eq, one, two, sig = (m.sb(n, shape) for n in ("lg", "rank", "eq", "one", "two", "sig"))
        top, first = m.sb("top", [P, TT]), m.sb("first", [P, TT])
        hT = m.ps("hT", [P, DC, T])
        lp = m.ps("lp", [P, TT, T])
        w_in, made, rank_ready, own_dve = m.sem("w_in"), m.sem("made"), m.sem("rank_ready"), m.sem("own_dve")
        hT_ready, hh_ready, hl_ready, l_ready = (m.sem(n) for n in ("hT_ready", "hh_ready", "hl_ready", "l_ready"))
        lg_ready, sig_ready = m.sem("lg_ready"), m.sem("sig_ready")
        block = ctx.enter_context(nc.Block())

        @block.sync
        def _(sp):
            at = DIC * 64
            for s, r in enumerate((rh, rl)):
                sp.dma_start(r.rearrange("p c n -> p (c n)"), wsplit[s][:, W.SMALL[0], at:at + DC * NE]).then_inc(w_in, 16)

        @block.gpsimd
        def _(pool):
            identity(nc, pool, ident, made)
            for e in range(NE):
                nc.gpsimd.memset(rank[:, :, e:e + 1], float(NE - e)).then_inc(rank_ready, 1)
            nc.gpsimd.memset(gates[:, :, NE:NX], UNSCALE).then_inc(rank_ready, 1)

        @block.scalar
        def _(act):
            for c in range(DC):
                act.wait_ge(hT_ready, c + 1)
                nc.scalar.activation(keep.hh[:, c, :], hT[:, c, :], ACT.Copy, scale=SA).then_inc(hh_ready, 1)
            act.wait_ge(lg_ready, TT)
            nc.scalar.activation(sig[:, :, :], lg[:, :, :], ACT.Sigmoid).then_inc(sig_ready, 1)

        @block.vector
        def _(dve):
            own = Chain(dve, own_dve)
            for c in range(DC):
                dve.wait_ge(hh_ready, c + 1)
                nc.vector.scalar_tensor_tensor(keep.hl[:, c, :], hT[:, c, :], SA, keep.hh[:, c, :],
                                               ALU.mult, ALU.subtract).then_inc(hl_ready, 1)
            for t in range(TT):
                dve.wait_ge(l_ready, t + 1)
                nc.vector.tensor_scalar(lg[:, t, :], lp[:, t, 0:NE], UNSCALE, None, ALU.mult).then_inc(lg_ready, 1)
            dve.wait_ge(lg_ready, TT)
            dve.wait_ge(rank_ready, NE + 1)

            def pick(src, dst):
                own.done(nc.vector.reduce_max(top[:, :], src[:, :, :], AX.X))
                own.done(nc.vector.tensor_tensor(eq[:, :, :], src[:, :, :], top[:, :].unsqueeze(2).to_broadcast(shape),
                                                 ALU.is_equal))
                own.done(nc.vector.tensor_tensor(eq[:, :, :], eq[:, :, :], rank[:, :, :], ALU.mult))
                own.done(nc.vector.reduce_max(first[:, :], eq[:, :, :], AX.X))
                own.done(nc.vector.tensor_tensor(dst[:, :, :], eq[:, :, :], first[:, :].unsqueeze(2).to_broadcast(shape),
                                                 ALU.is_equal))

            pick(lg, one)
            own.done(nc.vector.scalar_tensor_tensor(two[:, :, :], one[:, :, :], -1e30, lg[:, :, :], ALU.mult, ALU.add))
            pick(two, two)
            own.done(nc.vector.tensor_tensor(one[:, :, :], one[:, :, :], two[:, :, :], ALU.add))
            own.done(nc.vector.tensor_scalar(one[:, :, :], one[:, :, :], UNSCALE, None, ALU.mult))
            dve.wait_ge(sig_ready, 1)
            own.inc(nc.vector.tensor_tensor(gates[:, :, 0:NE], one[:, :, :], sig[:, :, :], ALU.mult))

        @block.tensor
        def _(pe):
            pe.wait_ge(made, 2)
            transpose_rows(nc, keep.a, hT, ident, hT_ready)
            pe.wait_ge(w_in, 32)
            pe.wait_ge(hl_ready, DC)
            for t in range(TT):
                tok = slice(t * P, (t + 1) * P)
                product(nc, lp[:, t, 0:NE], [p for c in range(DC) for p in
                                             three(keep.hh[:, c, tok], keep.hl[:, c, tok], rh[:, c, :], rl[:, c, :])]
                        ).then_inc(l_ready, 1)


def experts(nc, keep, gates, gate_up, down, out):
    with ExitStack() as ctx:
        m = Space(nc, ctx, "ex")
        ex = ExpertPlaces(keep)
        gf, df = ex.gf, ex.df
        gh, gl = ([first, m.sb(n, [P, DC, 2 * EH], F16)] for n, first in (("gh", ex.gh[0]), ("gl", ex.gl[0])))
        dh, dl = ([m.sb(f"{n}{i}", [P, EHC, D], F16) for i in range(2)] for n in ("dh", "dl"))
        sg, mf = m.sb("sg", [P, EHC, T]), m.sb("mf", [P, EHC, T])
        mh, ml = ([m.sb(f"{n}{i}", [P, EHC, T], F16) for i in range(2)] for n in ("mh", "ml"))
        gp, up = m.ps("gp", [P, 2, T]), m.ps("up", [P, 2, T])
        op = m.ps("op", [P, TT, D])
        g_in, d_in = ([m.sem(f"{n}{i}") for i in range(2)] for n in ("g_in", "d_in"))
        gh_ready, gl_ready, dh_ready, dl_ready = (m.sem(n) for n in ("gh_ready", "gl_ready", "dh_ready", "dl_ready"))
        g_ready, u_ready = m.sem("g_ready"), m.sem("u_ready")
        sg_ready, mf_ready, o_read = m.sem("sg_ready"), m.sem("mf_ready"), m.sem("o_read")
        mh_ready, ml_ready, o_ready, y_out = (m.sem(n) for n in ("mh_ready", "ml_ready", "o_ready", "y_out"))
        block = ctx.enter_context(nc.Block())

        @block.sync
        def _(sp):
            def load_gate_up(e, par):
                sp.dma_start(gf[par], gate_up.rearrange("(e c p) n -> p e c n", p=P, c=DC)[:, bass.ds(e, 1), :, :]
                             .rearrange("p o c n -> p (o c) n")).then_inc(g_in[par], 16)

            def load_down(e, par):
                sp.dma_start(df[par], down.rearrange("(e c p) n -> p e c n", p=P, c=EHC)[:, bass.ds(e, 1), :, :]
                             .rearrange("p o c n -> p (o c) n")).then_inc(d_in[par], 16)

            load_gate_up(1, 1)
            load_down(1, 1)
            with sp.Fori(0, NX // 2 - 1) as i:
                for par in range(2):
                    sp.wait_ge(gl_ready, i * (2 * DC) + (par + 1) * DC)
                    load_gate_up(i * 2 + par + 2, par)
                    sp.wait_ge(dl_ready, i * 4 + 2 * par + 2)
                    load_down(i * 2 + par + 2, par)
            sp.wait_ge(y_out, 16)

        def loop(eng, body):
            body(0, 0, 0, "first")
            with eng.Fori(0, NX // 2 - 1) as i:
                body(i * 2 + 1, 1, i, "inner")
                body(i * 2 + 2, 0, i + 1, "inner")
            body(NX - 1, 1, NX // 2 - 1, "last")

        @block.scalar
        def _(act):
            def split_down(par, p):
                cs = slice(2 * p, 2 * p + 2)
                nc.scalar.activation(dh[par][:, cs, :], df[par][:, cs, :], ACT.Copy, scale=SW).then_inc(dh_ready, 1)

            def split_next(e, par, turn, j):
                nxt = 1 - par
                if j == 0:
                    act.wait_ge(g_in[nxt], (turn + 1) * 16)
                if j < 2:
                    for c in (2 * j, 2 * j + 1):
                        nc.scalar.activation(gh[nxt][:, c, :], gf[nxt][:, c, :], ACT.Copy, scale=SW).then_inc(gh_ready, 1)
                else:
                    if j == 2:
                        act.wait_ge(d_in[nxt], (turn + 1) * 16)
                        if not isinstance(e, int) or e:
                            act.wait_ge(o_ready, e * TT)
                    split_down(nxt, j - 2)

            def high(e, par, j):
                act.wait_ge(mf_ready, e * EHC + j + 1 + 2)
                nc.scalar.activation(mh[par][:, j, :], mf[:, j, :], ACT.Copy).then_inc(mh_ready, 1)

            def body(e, par, turn, kind):
                for j in range(EHC):
                    act.wait_ge(g_ready, e * EHC + j + 1)
                    nc.scalar.activation(sg[:, j, :], gp[:, j % 2, :], ACT.Silu, scale=UNSCALE).then_inc(sg_ready, 1)
                    if j:
                        high(e, par, j - 1)
                    if kind != "last":
                        split_next(e, par, turn, j)
                high(e, par, EHC - 1)

            split_down(0, 0)
            split_down(0, 1)
            loop(act, body)

        @block.vector
        def _(dve):
            dve.sem_inc(sg_ready, 2)
            dve.sem_inc(mf_ready, 2)
            dve.sem_inc(o_read, TT)
            dve.sem_inc(gl_ready, DC)

            def split_down(e, par, p):
                cs = slice(2 * p, 2 * p + 2)
                dve.wait_ge(dh_ready, e * 2 + p + 1)
                nc.vector.scalar_tensor_tensor(dl[par][:, cs, :], df[par][:, cs, :], SW, dh[par][:, cs, :], ALU.mult,
                                               ALU.subtract).then_inc(dl_ready, 1)

            def split_next(e, par, j):
                nxt = 1 - par
                if j < 2:
                    for c in (2 * j, 2 * j + 1):
                        dve.wait_ge(gh_ready, e * DC + c + 1)
                        nc.vector.scalar_tensor_tensor(gl[nxt][:, c, :], gf[nxt][:, c, :], SW, gh[nxt][:, c, :],
                                                       ALU.mult, ALU.subtract).then_inc(gl_ready, 1)
                else:
                    split_down(e + 1, nxt, j - 2)

            def low(e, par, j):
                dve.wait_ge(mh_ready, e * EHC + j + 1)
                nc.vector.tensor_tensor(ml[par][:, j, :], mf[:, j, :], mh[par][:, j, :], ALU.subtract).then_inc(ml_ready, 1)

            def add(e):
                for t in range(TT):
                    dve.wait_ge(o_ready, e * TT + t + 1)
                    dve.wait_ge(o_read, e * TT + t + 1)
                    nc.vector.scalar_tensor_tensor(keep.x1[:, t, :], op[:, t, :], gates[:, t, bass.ds(e, 1)],
                                                   keep.x1[:, t, :], ALU.mult, ALU.add).then_inc(o_read, 1)

            def body(e, par, turn, kind):
                for j in range(EHC):
                    dve.wait_ge(u_ready, e * EHC + j + 1)
                    dve.wait_ge(sg_ready, e * EHC + j + 1 + 2)
                    dve.wait_ge(ml_ready, e * EHC) if kind != "first" else None
                    nc.vector.scalar_tensor_tensor(mf[:, j, :], up[:, j % 2, :], SA * UNSCALE, sg[:, j, :], ALU.mult,
                                                   ALU.mult).then_inc(mf_ready, 1)
                    if j:
                        low(e, par, j - 1)
                    if j == 2 and kind != "first":
                        add(e - 1)
                    if kind != "last":
                        split_next(e, par, j)
                low(e, par, EHC - 1)

            split_down(0, 0, 0)
            split_down(0, 0, 1)
            loop(dve, body)
            add(NX - 1)

        @block.tensor
        def _(pe):
            def down_proj(e, par):
                pe.wait_ge(ml_ready, e * EHC + EHC)
                pe.wait_ge(dl_ready, e * 2 + 2)
                for t in range(TT):
                    tok = slice(t * P, (t + 1) * P)
                    pe.wait_ge(o_read, e * TT + t + 1)
                    product(nc, op[:, t, :], [p for j in range(EHC) for p in
                                              three(mh[par][:, j, tok], ml[par][:, j, tok], dh[par][:, j, :], dl[par][:, j, :])]
                            ).then_inc(o_ready, 1)

            def body(e, par, turn, kind):
                pe.wait_ge(gl_ready, e * DC + DC)
                for j in range(EHC):
                    for half, bank, free, ready in ((0, gp, sg_ready, g_ready), (1, up, mf_ready, u_ready)):
                        cols = slice(half * EH + j * P, half * EH + (j + 1) * P)
                        pe.wait_ge(free, e * EHC + j + 1)
                        product(nc, bank[:, j % 2, :], [p for c in range(DC) for p in
                                                        three(gh[par][:, c, cols], gl[par][:, c, cols],
                                                              keep.hh[:, c, :], keep.hl[:, c, :])]
                                ).then_inc(ready, 1)
                    if j == 1 and kind != "first":
                        down_proj(e - 1, 1 - par)

            loop(pe, body)
            down_proj(NX - 1, 1)

        @block.gpsimd
        def _(pool):
            pool.wait_ge(o_read, NX * TT + TT)
            pool.dma_start(out.rearrange("(t p) d -> p t d", p=P), keep.x1[:, :, :]).then_inc(y_out, 16)


class Keep:
    pass


def program(nc, x, ctxT, wq, bq, wk, bk, wv, bv, bo, n1w, n2w, convw, convb, dtb, a_log, dskip, wpack, gate_up,
            down, out):
    def scratch(name, shape, dt=F32):
        return nc.dram_tensor(name, shape, dt).ap()

    q_dram = scratch("q_dram", [2, NH * DH, T], F16)
    kd = scratch("kd", [2, DH, NH, S], F16)
    vd = scratch("vd", [NH, P, S], F16)
    wsplit = scratch("wsplit", [2, P, WT, WC], F16)
    o_parts = scratch("o_parts", [3, P, NH * T])
    m_dram = scratch("m_dram", [NH * T], F16)
    r_dram = scratch("r_dram", [NH * T])
    xd_dram = scratch("xd_dram", [2 * DS, T])

    with ExitStack() as outer:
        m = Space(nc, outer, "first")
        keep = Keep()
        keep.wkh, keep.wkl, keep.wvh, keep.wvl = (m.sb(n, [P, DC, NH * DH], F16) for n in ("wkh", "wkl", "wvh", "wvl"))
        keep.qz = [m.sb(f"qz{i}", [P, PAIRS, T], F16) for i in range(2)]
        latent_queries(nc, keep, x, wq, bq, wk, wv, q_dram)
        context_keys_values(nc, keep, ctxT, bk, kd, vd, m_dram, wpack, wsplit)
    attention(nc, q_dram, m_dram, kd, vd, o_parts)
    with ExitStack() as outer:
        m = Space(nc, outer, "keep")
        keep = Keep()
        keep.x1, keep.a = m.sb("x1", [P, TT, D]), m.sb("a", [P, TT, D])
        keep.hidden = m.sb("hidden", [P, 2 * DC, T], F16)
        keep.hh, keep.hl = keep.hidden[:, 0:DC, :], keep.hidden[:, DC:2 * DC, :]
        keep.big = [m.sb(f"big{i}", [P, 4 * WC], F16) for i in range(4)]
        gates = m.sb("gates", [P, TT, NX])
        project_attention(nc, keep, x, o_parts, r_dram, bv, bo, n1w, wsplit)
        with ExitStack() as inner:
            m = Space(nc, inner, "mamba")
            keep.xin, keep.zs, keep.delta = (m.sb(n, [P, DIC, T]) for n in ("xin", "zs", "delta"))
            keep.yh, keep.yl = (m.sb(n, [P, DIC, T], F16) for n in ("yh", "yl"))
            mamba_inputs(nc, keep, convw, convb, dtb, xd_dram, wsplit)
            with ExitStack() as output:
                keep.outl = Space(nc, output, "output").sb("outl", [P, DIC, D], F16)
                mamba_scan(nc, keep, a_log, dskip, xd_dram, wsplit)
                mamba_output(nc, keep, n2w, wsplit)
        gated_mlp(nc, keep, wsplit, gate_up, down)
        route(nc, keep, gates, wsplit)
        experts(nc, keep, gates, gate_up, down, out)


def columns(v):
    return v.reshape(-1, P).T


def layout(inputs):
    a = {k: np.asarray(v) for k, v in inputs.items()}
    g = lambda n: a["L0_xattn_" + n]
    b = lambda n: a["L0_attn_" + n]
    f = lambda n: a["L0_ffn_" + n]

    def rows(w):
        return w.reshape(-1, P, w.shape[1]).transpose(1, 0, 2).reshape(P, -1)

    dtw = np.concatenate([b("dt_proj_w").T, np.zeros((P - DR, DI), np.float32)])
    small = np.concatenate([rows(b("x_proj_w").T), rows(f("router_w").T), dtw], axis=1)
    small = np.concatenate([small, np.zeros((P, WC - small.shape[1]), np.float32)], axis=1)
    packed = np.concatenate([rows(g("Wo")), rows(b("in_proj_w").T), rows(b("w1").T), rows(b("w3").T),
                             rows(b("w2").T), rows(b("out_proj_w").T), small], axis=1)
    packed = np.concatenate([packed, np.zeros((P, WT * WC - packed.shape[1]), np.float32)], axis=1)
    sg, su, sd = f("shared_gate_w").T, f("shared_up_w").T, f("shared_down_w").T
    shared = [np.concatenate([sg[:, h * EH:(h + 1) * EH], su[:, h * EH:(h + 1) * EH]], axis=1) for h in range(2)]
    gate_up = np.concatenate([f("gate_up_w").reshape(NE * D, 2 * EH)] + shared)
    down = np.concatenate([f("down_w").reshape(NE * EH, D), sd])
    out = dict(
        x=a["x"][0], ctxT=a["ctx_1024"][0].T, wq=g("Wq"), bq=columns(g("bq")), wk=g("Wk"), bk=columns(g("bk")),
        wv=g("Wv"), bv=columns(g("bv")), bo=g("bo"), n1w=columns(b("norm1_w")), n2w=columns(b("norm2_w")),
        convw=b("conv_w").reshape(DIC, P, 4).transpose(1, 0, 2), convb=columns(b("conv_b")),
        dtb=columns(b("dt_proj_b")), a_log=b("A_log").reshape(DIC, P, DS).transpose(1, 0, 2), dskip=columns(b("D")),
        wpack=packed.reshape(P, WT, WC).transpose(1, 0, 2), gate_up=gate_up, down=down)
    return {k: np.ascontiguousarray(v) for k, v in out.items()}


def kernel(**inputs):
    import concourse.bacc as bacc
    from concourse.bass_utils import run_bass_kernel_spmd

    nc = bacc.Bacc("TRN2", target_bir_lowering=False, num_devices=1)
    arrays = layout(inputs)
    args = [nc.dram_tensor(k, v.shape, mybir.dt.from_np(v.dtype), kind="ExternalInput").ap()
            for k, v in arrays.items()]
    out = nc.dram_tensor("out", [T, D], F32, kind="ExternalOutput").ap()
    program(nc, *args, out)
    result = run_bass_kernel_spmd(nc, [arrays], core_ids=[0])
    return result.results[0]["out"].reshape(1, T, D)
```

```python
import math

import numpy as np

import concourse.bass as bass
from concourse import mybir
from contextlib import ExitStack

F32 = mybir.dt.float32
F16 = mybir.dt.float16
ALU = mybir.AluOpType
ACT = mybir.ActivationFunctionType
AX = mybir.AxisListType

P = 128
T = 512
D = 512
TT = T // P
DC = D // P
SA = 16.0
SW = 256.0


class Chain:

    def __init__(self, eng, sem):
        self.eng, self.sem, self.n = eng, sem, 0

    def inc(self, ins):
        self.n += 1
        return ins.then_inc(self.sem, 1)

    def wait(self):
        self.eng.wait_ge(self.sem, self.n)

    def done(self, ins):
        self.inc(ins)
        self.wait()


class Space:

    def __init__(self, nc, ctx, prefix):
        self.nc, self.ctx, self.prefix, self.sems = nc, ctx, prefix, []
        ctx.callback(self.clear)

    def clear(self):
        if self.sems:
            self.nc.clear_and_free_semaphores(self.sems)
            self.nc.all_engine_barrier()

    def sb(self, name, shape, dt=F32):
        return self.ctx.enter_context(self.nc.sbuf_tensor(f"{self.prefix}_{name}", shape, dt))

    def ps(self, name, shape, dt=F32):
        return self.ctx.enter_context(self.nc.psum_tensor(f"{self.prefix}_{name}", shape, dt))

    def sem(self, name):
        self.sems.append(self.nc.alloc_semaphore(f"{self.prefix}_{name}"))
        return self.sems[-1]


def identity(nc, pool, tile, made):
    nc.gpsimd.memset(tile[:, :], 0.0).then_inc(made, 1)
    pool.wait_ge(made, 1)
    nc.gpsimd.affine_select(out=tile[:, :], in_=tile[:, :], compare_op=ALU.not_equal, fill=1.0,
                            base=0, pattern=[[-1, P]], channel_multiplier=1).then_inc(made, 1)


NH = 16
DH = 64
S = 8192
CK = 512
NCK = S // CK
PAIRS = NH // 2
KT = S // P
WC = 2048
TW = 3
WT = TW * (NCK // 2 - 1)


def latent_queries(nc, keep, x, wq, bq, wk, wv, bk, ctxT, q_dram):
    with ExitStack() as ctx:
        m = Space(nc, ctx, "lq")
        N = NH * DH
        xs = m.sb("xs", [P, TT, D])
        rows = Rows(m)
        xn = m.sb("xn", [P, TT, D])
        xh, xl = (m.sb(n, [P, DC, T], F16) for n in ("xh", "xl"))
        wf = [m.sb(f"wf{i}", [P, DC, N // 2]) for i in range(3)]
        wh, wl = (m.sb(n, [P, DC, N], F16) for n in ("wh", "wl"))
        bqc, bqs = m.sb("bqc", [P, PAIRS]), m.sb("bqs", [P, PAIRS])
        qf = m.sb("qf", [P, 4, T])
        qh, ql = (m.sb(n, [P, PAIRS, T], F16) for n in ("qh", "ql"))
        ident = m.sb("ident", [P, P])
        xT = m.ps("xT", [P, DC, T])
        qp = m.ps("qp", [P, 4, T])
        x_in, b_in, made, zero = m.sem("x_in"), m.sem("b_in"), m.sem("made"), m.sem("zero")
        w_in = [m.sem(f"w_in{i}") for i in range(3)]
        var_ready, sd_ready, xn_ready = m.sem("var_ready"), m.sem("sd_ready"), m.sem("xn_ready")
        xT_ready, xh_ready, xl_ready = m.sem("xT_ready"), m.sem("xh_ready"), m.sem("xl_ready")
        wh_ready, wl_ready, own_dve = m.sem("wh_ready"), m.sem("wl_ready"), m.sem("own_dve")
        b_ready, q_ready, qf_ready = m.sem("b_ready"), m.sem("q_ready"), m.sem("qf_ready")
        qh_ready, ql_ready, q_out = m.sem("qh_ready"), m.sem("ql_ready"), m.sem("q_out")
        c_in, ch_ready, qz_ready = m.sem("c_in"), m.sem("ch_ready"), m.sem("qz_ready")
        block = ctx.enter_context(nc.Block())
        halves = [(w, slice(h * N // 2, (h + 1) * N // 2)) for w in range(3) for h in range(2)]
        his = (wh, keep.wkh, keep.wvh)
        los = (wl, keep.wkl, keep.wvl)

        @block.sync
        def _(sp):
            sp.dma_start(xs[:, :, :], x.rearrange("(t p) d -> p t d", p=P)).then_inc(x_in, 16)
            for n, (w, cols) in enumerate(halves):
                if n >= 3:
                    sp.wait_ge(wl_ready, n - 2)
                src = (wq, wk, wv)[w].rearrange("(c p) n -> p c n", p=P)
                sp.dma_start(wf[n % 3][:, :, :], src[:, :, cols]).then_inc(w_in[n % 3], 16)
                if n == 1:
                    sp.dma_start(bqc[:, :], bq).then_inc(b_in, 16)
            sp.dma_start(keep.bkc[:, :], bk).then_inc(c_in, 16)
            for n in range(2):
                sp.dma_start(keep.cf[n][:, :, :], ctxT.rearrange("(c p) s -> p c s", p=P)[:, :, n * CK:(n + 1) * CK]
                             ).then_inc(c_in, 16)
            for js in (slice(0, 4), slice(4, 8)):
                sp.wait_ge(ql_ready, js.stop)
                for s, q in enumerate((qh, ql)):
                    sp.dma_start(q_dram[s].rearrange("(j p) t -> p j t", p=P)[:, js, :], q[:, js, :]).then_inc(q_out, 16)
            sp.wait_ge(c_in, 48)
            sp.wait_ge(q_out, 64)

        @block.gpsimd
        def _(pool):
            identity(nc, pool, ident, made)
            pool.wait_ge(made, 2)
            nc.gpsimd.memset(keep.qz[0][DH:P, :, :], 0.0).then_inc(zero, 1)
            pool.wait_ge(zero, 1)
            nc.gpsimd.memset(keep.qz[1][0:DH, :, :], 0.0).then_inc(zero, 1)

        @block.scalar
        def _(act):
            def split(n):
                w, cols = halves[n]
                act.wait_ge(w_in[n % 3], 16 * (n // 3 + 1))
                nc.scalar.activation(his[w][:, :, cols], wf[n % 3][:, :, :], ACT.Copy, scale=SW).then_inc(wh_ready, 1)

            act.wait_ge(var_ready, 1)
            nc.scalar.activation(rows.sd[:, :], rows.var[:, :], ACT.Sqrt).then_inc(sd_ready, 1)
            split(0)
            for c in range(DC):
                act.wait_ge(xT_ready, c + 1)
                nc.scalar.activation(xh[:, c, :], xT[:, c, :], ACT.Copy, scale=SA).then_inc(xh_ready, 1)
            split(1)
            split(2)
            act.wait_ge(b_ready, 1)
            for j in range(PAIRS):
                act.wait_ge(q_ready, j + 1)
                if j >= 4:
                    act.wait_ge(ql_ready, j - 3)
                nc.scalar.activation(qf[:, j % 4, :], qp[:, j % 4, :], ACT.Identity, bias=bqs[:, j:j + 1],
                                     scale=1.0 / SW).then_inc(qf_ready, 1)
                act.wait_ge(qf_ready, j + 1)
                nc.scalar.activation(qh[:, j, :], qf[:, j % 4, :], ACT.Copy).then_inc(qh_ready, 1)
                if j % 2 and j < 6:
                    split(3 + j // 2)
            act.wait_ge(c_in, 48)
            nc.scalar.activation(keep.ch[0][:, :, :], keep.cf[0][:, :, :], ACT.Copy, scale=SA).then_inc(ch_ready, 1)

        @block.vector
        def _(dve):
            own = Chain(dve, own_dve)

            def split(n):
                w, cols = halves[n]
                dve.wait_ge(wh_ready, n + 1)
                nc.vector.scalar_tensor_tensor(los[w][:, :, cols], wf[n % 3][:, :, :], SW, his[w][:, :, cols],
                                               ALU.mult, ALU.subtract).then_inc(wl_ready, 1)

            dve.wait_ge(x_in, 16)
            row_factor(nc, dve, own, xs, *rows.all, var_ready, sd_ready, 1, 1e-5, False)
            for t in range(TT):
                nc.vector.tensor_scalar(xn[:, t, :], xs[:, t, :], rows.mv[:, t, 0:1], rows.rs[:, t:t + 1],
                                        ALU.subtract, ALU.mult).then_inc(xn_ready, 1)
            dve.wait_ge(b_in, 16)
            nc.vector.tensor_scalar(bqs[:, :], bqc[:, :], SA, None, ALU.mult).then_inc(b_ready, 1)
            split(0)
            for c in range(DC):
                dve.wait_ge(xh_ready, c + 1)
                nc.vector.scalar_tensor_tensor(xl[:, c, :], xT[:, c, :], SA, xh[:, c, :], ALU.mult,
                                               ALU.subtract).then_inc(xl_ready, 1)
            split(1)
            split(2)
            for j in range(PAIRS):
                dve.wait_ge(qf_ready, j + 1)
                for e in range(2):
                    half = slice(e * DH, (e + 1) * DH)
                    nc.vector.tensor_copy(keep.qz[e][half, j, :], qf[half, j % 4, :]).then_inc(qz_ready, 1)
                dve.wait_ge(qh_ready, j + 1)
                nc.vector.tensor_tensor(ql[:, j, :], qf[:, j % 4, :], qh[:, j, :],
                                        ALU.subtract).then_inc(ql_ready, 1)
                if j % 2 and j < 6:
                    split(3 + j // 2)
            dve.wait_ge(c_in, 48)
            nc.vector.tensor_scalar(keep.bks[:, :], keep.bkc[:, :], SA, None, ALU.mult)
            dve.wait_ge(ch_ready, 1)
            nc.vector.scalar_tensor_tensor(keep.cl[0][:, :, :], keep.cf[0][:, :, :], SA, keep.ch[0][:, :, :],
                                           ALU.mult, ALU.subtract)

        @block.tensor
        def _(pe):
            pe.wait_ge(made, 2)
            pe.wait_ge(xn_ready, TT)
            transpose_rows(nc, xn, xT, ident, xT_ready)
            pe.wait_ge(xl_ready, DC)
            for j in range(PAIRS):
                if j % 4 == 0:
                    pe.wait_ge(wl_ready, j // 4 + 1)
                if j >= 4:
                    pe.wait_ge(qf_ready, j - 3)
                cols = slice(j * P, (j + 1) * P)
                product(nc, qp[:, j % 4, :], [p for c in range(DC) for p in
                                              three(wh[:, c, cols], wl[:, c, cols], xh[:, c, :], xl[:, c, :])]
                        ).then_inc(q_ready, 1)


LOG_P_MAX = math.log(256.0)
ONE_K = 256.0
SCORE = 1.0 / (SA * SA * 8)


def context_keys_values(nc, keep, ctxT, kd, vd, m_dram, wpack, wsplit):
    with ExitStack() as ctx:
        m = Space(nc, ctx, "kv")
        cf, ch, cl, bks = keep.cf, keep.ch, keep.cl, keep.bks
        kf = m.sb("kf", [P, 4, CK])
        ksh, ksl = ([m.sb(f"{n}{i}", [P, PAIRS, CK], F16) for i in range(2)] for n in ("ksh", "ksl"))
        vs = [m.sb(f"vs{i}", [P, NH, CK // P, 2 * DH], F16) for i in range(2)]
        tf = [m.sb(f"tf{i}", [P, WC]) for i in range(TW)]
        th, tl = ([m.sb(f"{n}{i}", [P, WC], F16) for i in range(TW)] for n in ("th", "tl"))
        mx = m.sb("mx", [P, NCK * NH * TT])
        mr, negm = m.sb("mr", [P, NH * TT]), m.sb("negm", [P, NH * TT])
        mrow = m.sb("mrow", [NH * TT, P], F16)
        ident = m.sb("ident", [P, P])
        kp, vp = m.ps("kp", [P, 2, CK]), m.ps("vp", [P, 2, CK])
        s1 = m.ps("s1", [P, 4, CK])
        t_in = [m.sem(f"t_in{i}") for i in range(TW)]
        t_out = [m.sem(f"t_out{i}") for i in range(TW)]
        th_ready = m.sem("th_ready")
        made = m.sem("made")
        c_in = [m.sem(f"c_in{i}") for i in range(2)]
        ch_ready, cl_ready = m.sem("ch_ready"), m.sem("cl_ready")
        k_ready, s1_ready = m.sem("k_ready"), m.sem("s1_ready")
        kf_ready, kl_ready, vl_ready, s1_max = m.sem("kf_ready"), m.sem("kl_ready"), m.sem("vl_ready"), m.sem("s1_max")
        tl_ready, v_ready = m.sem("tl_ready"), m.sem("v_ready")
        kh_ready, vh_ready = m.sem("kh_ready"), m.sem("vh_ready")
        k_out = [m.sem(f"k_out{i}") for i in range(2)]
        v_out = [m.sem(f"v_out{i}") for i in range(2)]
        mr_ready, negm_ready, mt_ready, mrow_ready, m_out = (
            m.sem(n) for n in ("mr_ready", "negm_ready", "mt_ready", "mrow_ready", "m_out"))
        block = ctx.enter_context(nc.Block())
        VT = 2 * (CK // P)
        MG = 4
        ctx_v = ctxT.rearrange("(c p) s -> p c s", p=P)

        def chunks(eng, chunk):
            chunk(0, 0, 0, None, {})
            with eng.Fori(0, NCK // 2 - 1) as i:
                for odd in (1, 0):
                    chunk(i * 2 + (2 - odd), odd, i + (1 - odd), i, {2: 0, 6: 1} if odd else {4: 2})
            chunk(NCK - 1, 1, NCK // 2 - 1, None, {})

        @block.sync
        def _(sp):
            with sp.Fori(0, NCK // 2 - 1) as i:
                for odd in (1, 0):
                    sp.wait_ge(ch_ready, i * 2 + (2 - odd))
                    sp.wait_ge(cl_ready, i * 2 + (2 - odd))
                    sp.dma_start(cf[1 - odd][:, :, :],
                                 ctx_v[:, :, bass.ds(i * (2 * CK) + (3 - odd) * CK, CK)]).then_inc(c_in[1 - odd], 16)
                    for e in ((0, 1) if odd else (2,)):
                        sp.wait_ge(tl_ready, i * TW + e + 1)
                        sp.dma_start(tf[e][:, :], wpack[bass.ds(i * TW + e, 1), :, :]
                                     .rearrange("o p n -> (o p) n")).then_inc(t_in[e], 16)
            sp.wait_ge(mrow_ready, 1)
            sp.dma_start(m_dram.rearrange("(r p) -> r p", p=P), mrow[:, :]).then_inc(m_out, 16)
            sp.wait_ge(m_out, 16)
            for e in range(TW):
                sp.wait_ge(t_out[e], 32 * (NCK // 2))
            for par in range(2):
                sp.wait_ge(k_out[par], 64 * (NCK // 2 + 1))
                sp.wait_ge(v_out[par], 16 * (NCK // 2 + 1))

        @block.gpsimd
        def _(pool):
            identity(nc, pool, ident, made)

        @block.scalar
        def _(act):
            def chunk(g, par, uses, i, tiles):
                act.wait_ge(k_out[par], 64 * (uses + 1))
                act.wait_ge(v_out[par], 16 * (uses + 1))
                for n in range(8):
                    act.wait_ge(k_ready, PAIRS * g + n + 1)
                    act.wait_ge(kl_ready, PAIRS * g + n + 1)
                    nc.scalar.activation(kf[:, n % 4, :], kp[:, n % 2, :], ACT.Identity,
                                         bias=bks[:, n:n + 1], scale=1.0 / SW).then_inc(kf_ready, 1)
                    act.wait_ge(kf_ready, PAIRS * g + n + 1 + 2)
                    nc.scalar.activation(ksh[par][:, n, :], kf[:, n % 4, :], ACT.Copy).then_inc(kh_ready, 1)
                    act.wait_ge(v_ready, VT * g + n + 2)
                    kt, half = n // 2, n % 2
                    nc.scalar.activation(
                        vs[par][:, half * 8:(half + 1) * 8, kt, 0:DH],
                        vp[:, n % 2, :].rearrange("p (h d) -> p h d", d=DH), ACT.Copy,
                        scale=1.0 / SW).then_inc(vh_ready, 1)
                    if n == 0 and (i is not None or g == 0):
                        nxt = 1 - par
                        act.wait_ge(c_in[nxt], 16 * (uses + 1) + 16 * par)
                        nc.scalar.activation(ch[nxt][:, :, :], cf[nxt][:, :, :], ACT.Copy,
                                             scale=SA).then_inc(ch_ready, 1)
                    if n in tiles:
                        e = tiles[n]
                        act.wait_ge(t_in[e], 16 * (i + 1))
                        act.wait_ge(t_out[e], 32 * (i + 1))
                        nc.scalar.activation(th[e][:, :], tf[e][:, :], ACT.Copy, scale=SW).then_inc(th_ready, 1)
                act.wait_ge(kl_ready, PAIRS * (g + 1) + 4)
                for s, ks in enumerate((ksh, ksl)):
                    for hd in range(2):
                        act.dma_start(kd[s].rearrange("d (j e) n -> d j e n", e=2)[:, :, hd, bass.ds(g * CK, CK)],
                                      ks[par][hd * DH:(hd + 1) * DH, :, :]).then_inc(k_out[par], 16)
                act.wait_ge(vl_ready, VT * (g + 1) + 2)
                act.dma_start(vd.rearrange("h p s -> p h s")[:, :, bass.ds(g * CK, CK)],
                              vs[par].rearrange("p h t c -> p h (t c)")).then_inc(v_out[par], 16)
                for e in tiles.values():
                    act.wait_ge(tl_ready, i * TW + e + 1 + TW)
                    for s, t in enumerate((th, tl)):
                        act.dma_start(wsplit[s].rearrange("p w n -> p (w n)")[:, bass.ds(i * (TW * WC) + e * WC, WC)],
                                      t[e][:, :]).then_inc(t_out[e], 16)

            chunks(act, chunk)
            act.wait_ge(mt_ready, 1)
            nc.scalar.activation(mrow[:, :], kp[0:NH * TT, 0, 0:P], ACT.Copy).then_inc(mrow_ready, 1)

        @block.vector
        def _(dve):
            dve.sem_inc(kf_ready, 2)
            dve.sem_inc(kl_ready, 4)
            dve.sem_inc(vl_ready, 2)
            dve.sem_inc(s1_max, 2)
            dve.sem_inc(tl_ready, TW)
            dve.sem_inc(v_ready, 1)
            for par in range(2):
                dve.sem_inc(k_out[par], 64)
                dve.sem_inc(v_out[par], 16)
                dve.sem_inc(c_in[par], 16)
            dve.sem_inc(ch_ready, 1)
            dve.sem_inc(cl_ready, 1)
            for e in range(TW):
                dve.sem_inc(t_out[e], 32)

            def maxima(g, n, groups):
                if n == 0 and isinstance(g, int) and g == 0:
                    return
                for q in groups:
                    dve.wait_ge(s1_ready, g * (PAIRS * MG) + (n - 1) * MG + q + 1)
                    at = 2 * (n - 1) * TT + q * 2
                    nc.vector.reduce_max(mx[:, bass.ds(g * (NH * TT) + at, 2)], s1[:, (q % 2) * 2:(q % 2) * 2 + 2, :],
                                         AX.X).then_inc(s1_max, 1)

            def chunk(g, par, uses, i, tiles):
                nxt = 1 - par

                def half_split(n, p):
                    if n == 1 and (i is not None or g == 0):
                        dve.wait_ge(ch_ready, g + 2)
                        cs = slice(2 * p, 2 * p + 2)
                        ins = nc.vector.scalar_tensor_tensor(cl[nxt][:, cs, :], cf[nxt][:, cs, :], SA, ch[nxt][:, cs, :],
                                                             ALU.mult, ALU.subtract)
                        if p:
                            ins.then_inc(cl_ready, 1)
                    if n - 1 in tiles:
                        e = tiles[n - 1]
                        dve.wait_ge(th_ready, i * TW + e + 1)
                        cs = slice(p * WC // 2, (p + 1) * WC // 2)
                        ins = nc.vector.scalar_tensor_tensor(tl[e][:, cs], tf[e][:, cs], SW, th[e][:, cs], ALU.mult,
                                                             ALU.subtract)
                        if p:
                            ins.then_inc(tl_ready, 1)

                for n in range(8):
                    maxima(g, n, (0, 1))
                    dve.wait_ge(kh_ready, PAIRS * g + n + 1)
                    nc.vector.tensor_tensor(ksl[par][:, n, :], kf[:, n % 4, :], ksh[par][:, n, :],
                                            ALU.subtract).then_inc(kl_ready, 1)
                    half_split(n, 0)
                    maxima(g, n, (2, 3))
                    dve.wait_ge(vh_ready, VT * g + n + 1)
                    kt, half = n // 2, n % 2
                    hs = slice(half * 8, (half + 1) * 8)
                    nc.vector.scalar_tensor_tensor(
                        vs[par][:, hs, kt, DH:2 * DH], vp[:, n % 2, :].rearrange("p (h d) -> p h d", d=DH),
                        1.0 / SW, vs[par][:, hs, kt, 0:DH], ALU.mult, ALU.subtract).then_inc(vl_ready, 1)
                    half_split(n, 1)

            chunks(dve, chunk)
            maxima(NCK, 0, range(MG))
            dve.wait_ge(s1_max, NCK * PAIRS * MG + 2)
            nc.vector.reduce_max(mr[:, :], mx.rearrange("p (c n) -> p n c", c=NCK), AX.X).then_inc(mr_ready, 1)
            dve.wait_ge(mr_ready, 1)
            nc.vector.tensor_scalar(negm[:, :], mr[:, :], -1.0 / ONE_K, LOG_P_MAX / SCORE / ONE_K, ALU.mult,
                                    ALU.add).then_inc(negm_ready, 1)

        @block.tensor
        def _(pe):
            def scores(g, par, n, q):
                if n == 0 and isinstance(g, int) and g == 0:
                    return
                j, keys = (n - 1) % PAIRS, ksh[par if n else 1 - par]
                pe.wait_ge(kh_ready, PAIRS * g + n)
                pe.wait_ge(s1_max, g * (PAIRS * MG) + (n - 1) * MG + q + 1)
                for e in range(2):
                    t = (q % 2) * 2 + e
                    last = nc.tensor.matmul(s1[:, t, :], keep.qz[q // 2][:, j, t * P:(t + 1) * P],
                                            keys[:, j, :], start=True, stop=True)
                last.then_inc(s1_ready, 1)

            def chunk(g, par, uses, i, tiles):
                pe.wait_ge(ch_ready, g + 1)
                pe.wait_ge(cl_ready, g + 1)
                for n in range(8):
                    pe.wait_ge(kf_ready, PAIRS * g + n + 1)
                    cols = slice(n * P, (n + 1) * P)
                    pairs = [p for c in range(DC) for p in three(keep.wkh[:, c, cols], keep.wkl[:, c, cols],
                                                                 ch[par][:, c, :], cl[par][:, c, :])]
                    product(nc, kp[:, n % 2, :], pairs[:6], stop=False)
                    scores(g, par, n, 0)
                    product(nc, kp[:, n % 2, :], pairs[6:], start=False).then_inc(k_ready, 1)
                    scores(g, par, n, 1)
                    pe.wait_ge(vl_ready, VT * g + n + 1)
                    kt, half = n // 2, n % 2
                    tok, cols = slice(kt * P, (kt + 1) * P), slice(half * 512, (half + 1) * 512)
                    pairs = [p for c in range(DC) for p in three(ch[par][:, c, tok], cl[par][:, c, tok],
                                                                 keep.wvh[:, c, cols], keep.wvl[:, c, cols])]
                    product(nc, vp[:, n % 2, :], pairs[:6], stop=False)
                    scores(g, par, n, 2)
                    product(nc, vp[:, n % 2, :], pairs[6:], start=False).then_inc(v_ready, 1)
                    scores(g, par, n, 3)

            chunks(pe, chunk)
            for q in range(MG):
                scores(NCK, 0, 0, q)
            pe.wait_ge(made, 2)
            pe.wait_ge(negm_ready, 1)
            nc.tensor.transpose(kp[0:NH * TT, 0, 0:P], negm[:, :], ident[:, :]).then_inc(mt_ready, 1)


RING = 8
LAG = 3
HP = KT // 2
NQ = 4


def attention(nc, keep, q_dram, m_dram, kd, vd, sums):
    with ExitStack() as ctx:
        m = Space(nc, ctx, "at")
        qh = m.sb("qh", [P, NH * T], F16)
        ql = m.sb("ql", [P, NH * T], F16)
        k_cur = m.sb("k_cur", [P, S], F16)
        k_one = m.sb("k_one", [P, S], F16)
        vs = m.sb("vs", [P, KT, P], F16)
        ones = m.sb("ones", [P, 32], F16)
        pf = m.sb("pf", [P, RING, 2, T])
        ph, pl = (m.sb(n, [P, RING, 2, T], F16) for n in ("ph", "pl"))
        parts = m.sb("parts", [P, 2, T])
        st = m.ps("st", [P, 2, 2, T])
        acc = m.ps("acc", [P, 3, T])

        ql_zero = m.sem("ql_zero")
        q_in, q_rest_in, const_ready = m.sem("q_in"), m.sem("q_rest_in"), m.sem("const_ready")
        k_in = [m.sem(f"k_in{i}") for i in range(NQ)]
        v_in = [m.sem(f"v_in{i}") for i in range(NQ)]
        st_ready, pf_ready, ph_ready, ph_own = (m.sem(n) for n in ("st_ready", "pf_ready", "ph_ready", "ph_own"))
        pl_ready, pv_done, acc_read, o_out = (m.sem(n) for n in ("pl_ready", "pv_done", "acc_read", "o_out"))
        block = ctx.enter_context(nc.Block())
        QP = HP // NQ
        QK = S // NQ
        DVE_HI = 3

        @block.sync
        def _(sp):
            src = q_dram.rearrange("s (h d) t -> s d h t", d=DH)

            def load_queries(first, end, sem):
                for q, s, at in ((qh, 0, 0), (ql, 1, 0), (qh, 0, DH)):
                    sp.dma_start(q[at:at + DH, first * T:end * T].rearrange("d (h t) -> d h t", t=T),
                                 src[s][:, first:end, :]).then_inc(sem, 16)

            def load_keys(n, q):
                cols = slice(q * QK, (q + 1) * QK)
                for k, s, at in ((k_cur, 0, 0), (k_cur, 1, DH), (k_one, 0, 0)):
                    sp.dma_start(k[at:at + DH, cols],
                                 kd[s].rearrange("d h n -> d (h n)")[:, bass.ds(n * S + q * QK, QK)]).then_inc(k_in[q], 16)

            def load_values(n, q):
                sp.dma_start(vs[:, q * 2 * QP:(q + 1) * 2 * QP, :].rearrange("p k c -> p (k c)"),
                             vd.rearrange("h p s -> p h s")[:, bass.ds(n, 1), q * QK:(q + 1) * QK]
                             .rearrange("p h s -> p (h s)")).then_inc(v_in[q], 16)

            load_queries(0, 1, q_in)
            for q in range(NQ):
                load_keys(0, q)
                if q == 0:
                    sp.wait_ge(ql_zero, 1)
                    sp.dma_start(ql[DH:DH + 1, :], m_dram.rearrange("(o n) -> o n", o=1)).then_inc(q_in, 16)
                load_values(0, q)
            load_queries(1, NH, q_rest_in)

            def load_next(h):
                for q in range(NQ):
                    sp.wait_ge(st_ready, h * HP + QP * (q + 1))
                    load_keys(h + 1, q)
                    sp.wait_ge(pv_done, h * HP + QP * (q + 1) + RING)
                    load_values(h + 1, q)

            def store(j, e):
                h = 2 * j + e
                sp.wait_ge(acc_read, 3 * h + 6)
                sp.dma_start(sums[:, bass.ds(h * T, T)],
                             parts[0:P:32, 1, :]).then_inc(o_out, 16)
                for n in range(2):
                    sp.dma_start(keep.heads[n].rearrange("p j t -> p (j t)")[e * DH:(e + 1) * DH, bass.ds(j * T, T)],
                                 parts[n * DH:(n + 1) * DH, 0, :]).then_inc(o_out, 16)

            with sp.Fori(0, NH // 2 - 1) as j:
                for e in range(2):
                    load_next(2 * j + e)
                    store(j, e)
            load_next(NH - 2)
            store(PAIRS - 1, 0)
            store(PAIRS - 1, 1)
            sp.wait_ge(o_out, 48 * NH + 48)

        @block.gpsimd
        def _(pool):
            own = Chain(pool, const_ready)
            own.done(nc.gpsimd.memset(ones[:, :], 1.0))
            for q in range(NQ):
                cols = slice(q * QK, (q + 1) * QK)
                own.done(nc.gpsimd.memset(k_one[DH:P, cols], 0.0))
                own.done(nc.gpsimd.memset(k_one[DH:DH + 1, cols], ONE_K))

        def turns(eng, pair, cut, end=None):
            for s in range(cut):
                pair(0, s)
            with eng.Fori(0, NH - 1) as h:
                for s in range(cut, HP + cut):
                    pair(h, s)
                if end:
                    end(h)
            for s in range(cut, HP):
                pair(NH - 1, s)
            if end:
                end(NH - 1)

        @block.scalar
        def _(act):
            def hi(h, s):
                g = h * HP + s
                act.wait_ge(pf_ready, g + 1)
                act.wait_ge(pv_done, g + 1)
                nc.scalar.activation(ph[:, s % RING, :, :], pf[:, s % RING, :, :], ACT.Copy).then_inc(ph_ready, 1)

            def pair(h, s):
                g = h * HP + s
                act.wait_ge(st_ready, g + 1)
                act.wait_ge(pl_ready, g + 1)
                nc.scalar.activation(pf[:, s % RING, :, :], st[:, s % 2, :, :], ACT.Exp,
                                     scale=SCORE).then_inc(pf_ready, 1)
                if s and (s - 1) % 4 != DVE_HI:
                    hi(h, s - 1)


            turns(act, pair, LAG)

        @block.vector
        def _(dve):
            nc.vector.memset(ql[DH:P, :], 0.0).then_inc(ql_zero, 1)
            dve.sem_inc(pl_ready, RING)
            dve.sem_inc(pv_done, RING)
            dve.sem_inc(acc_read, 3)
            dve.sem_inc(o_out, 48)

            def pair(h, s):
                g = h * HP + s
                if s % 4 == DVE_HI:
                    dve.wait_ge(pf_ready, g + 1)
                    dve.wait_ge(pv_done, g + 1)
                    nc.vector.tensor_copy(ph[:, s % RING, :, :], pf[:, s % RING, :, :]).then_inc(ph_own, 1)
                    dve.wait_ge(ph_own, h * (HP // 4) + s // 4 + 1)
                else:
                    dve.wait_ge(ph_ready, h * (HP // 4 * 3) + s // 4 * 3 + s % 4 + 1)
                nc.vector.tensor_tensor(pl[:, s % RING, :, :], pf[:, s % RING, :, :], ph[:, s % RING, :, :],
                                        ALU.subtract).then_inc(pl_ready, 1)

            def end(h):
                dve.wait_ge(pv_done, h * HP + HP + RING)
                dve.wait_ge(o_out, h * 48 + 48)
                nc.vector.tensor_copy(parts[:, 0, :], acc[:, 0, :]).then_inc(acc_read, 1)
                dve.wait_ge(acc_read, h * 3 + 4)
                nc.vector.tensor_tensor(parts[DH:P, 0, :], acc[DH:P, 1, :], parts[DH:P, 0, :],
                                        ALU.add).then_inc(acc_read, 1)
                nc.vector.tensor_copy(parts[:, 1, :], acc[:, 2, :]).then_inc(acc_read, 1)

            turns(dve, pair, LAG - 2, end)

        @block.tensor
        def _(pe):
            def values(h, s):
                if s % QP == 0:
                    pe.wait_ge(v_in[s // QP], 16 * (h + 1))
                pe.wait_ge(pl_ready, h * HP + s + 1 + RING)
                first, final = s == 0, s == HP - 1
                r = s % RING
                if first:
                    pe.wait_ge(acc_read, h * 3 + 1)
                nc.tensor.matmul(acc[:, 0, :], vs[:, 2 * s, :], ph[:, r, 0, :], start=first, stop=False)
                if first:
                    pe.wait_ge(acc_read, h * 3 + 2)
                nc.tensor.matmul(acc[0:DH, 0, :], vs[:, 2 * s, 0:DH], pl[:, r, 0, :], start=False, stop=False)
                nc.tensor.matmul(acc[DH:P, 1, :], vs[:, 2 * s + 1, 0:DH], pl[:, r, 1, :], start=first, stop=final)
                nc.tensor.matmul(acc[:, 0, :], vs[:, 2 * s + 1, :], ph[:, r, 1, :], start=False, stop=final)
                if first:
                    pe.wait_ge(acc_read, h * 3 + 3)
                for e, (p, half) in enumerate((p, half) for p in (ph, pl) for half in range(2)):
                    last = nc.tensor.matmul(acc[e * 32:(e + 1) * 32, 2, :], ones[:, :], p[:, r, half, :],
                                            start=first, stop=final, tile_position=(0, e * 32))
                last.then_inc(pv_done, 1)

            def pair(h, s):
                ahead, w = divmod(s, HP)
                g = h * HP + s
                if ahead and w == 0:
                    pe.wait_ge(q_rest_in, 48)
                if w % QP == 0:
                    pe.wait_ge(k_in[w // QP], 48 * (h + ahead + 1))
                    pe.wait_ge(const_ready, 3 + 2 * (w // QP))
                if not isinstance(g, int) or g >= 2:
                    pe.wait_ge(pf_ready, g - 1)
                q = bass.ds((h + ahead) * T, T)
                for e in range(2):
                    tile = slice((2 * w + e) * P, (2 * w + e + 1) * P)
                    nc.tensor.matmul(st[:, s % 2, e, :], k_cur[:, tile], qh[:, q], start=True, stop=False)
                    last = nc.tensor.matmul(st[:, s % 2, e, :], k_one[:, tile], ql[:, q], start=False, stop=True)
                last.then_inc(st_ready, 1)
                if s >= LAG:
                    values(h, s - LAG)

            pe.wait_ge(q_in, 64)
            turns(pe, pair, LAG)
            for s in range(HP - LAG, HP):
                values(NH - 1, s)


class W:
    O = (0, 2)
    IN = (2, 4)
    W1 = (6, 4)
    W3 = (10, 4)
    W2 = (14, 4)
    OUT = (18, 2)
    SMALL = (20, 1)


def load_split(eng, wsplit, where, hi, lo, sem):
    at, n = where
    for s, t in enumerate((hi, lo)):
        eng.dma_start(t, wsplit[s][:, at:at + n, :].rearrange("p w n -> p (w n)")).then_inc(sem, 16)


UNSCALE = 1.0 / (SA * SW)


def row_factor(nc, dve, own, src, st, mv, var, sd, rs, tmp, var_ready, sd_ready, n, eps, rms):
    for t in range(TT):
        own.inc(nc.vector.bn_stats(st[:, t, :], src[:, t, :]))
    own.wait()
    for t in range(TT):
        own.inc(nc.vector.bn_aggr(mv[:, t, :], st[:, t, :]))
    own.wait()
    if rms:
        own.done(nc.vector.tensor_tensor(tmp[:, :], mv[:, :, 0], mv[:, :, 0], ALU.mult))
        own.done(nc.vector.tensor_tensor(tmp[:, :], tmp[:, :], mv[:, :, 1], ALU.add))
        nc.vector.tensor_scalar(var[:, :], tmp[:, :], eps, None, ALU.add).then_inc(var_ready, 1)
    else:
        nc.vector.tensor_scalar(var[:, :], mv[:, :, 1], eps, None, ALU.add).then_inc(var_ready, 1)
    dve.wait_ge(var_ready, n)
    dve.wait_ge(sd_ready, n)
    own.done(nc.vector.reciprocal(rs[:, :], sd[:, :]))
    own.done(nc.vector.tensor_tensor(tmp[:, :], rs[:, :], rs[:, :], ALU.mult))
    own.done(nc.vector.tensor_tensor(tmp[:, :], tmp[:, :], var[:, :], ALU.mult))
    own.done(nc.vector.tensor_scalar(tmp[:, :], tmp[:, :], -0.5, 1.5, ALU.mult, ALU.add))
    own.done(nc.vector.tensor_tensor(rs[:, :], rs[:, :], tmp[:, :], ALU.mult))


class Rows:

    def __init__(self, m):
        self.st, self.mv = m.sb("st", [P, TT, 6]), m.sb("mv", [P, TT, 2])
        self.var, self.sd, self.rs, self.tmp = (m.sb(n, [P, TT]) for n in ("var", "sd", "rs", "tmp"))
        self.all = (self.st, self.mv, self.var, self.sd, self.rs, self.tmp)


def transpose_rows(nc, src, dst, ident, ready):
    for c in range(DC):
        for t in range(TT):
            last = nc.tensor.transpose(dst[:, c, t * P:(t + 1) * P], src[:, t, c * P:(c + 1) * P], ident[:, :])
        last.then_inc(ready, 1)


def product(nc, out, pairs, start=True, stop=True):
    for n, (a, b) in enumerate(pairs):
        last = nc.tensor.matmul(out, a, b, start=(start and n == 0), stop=(stop and n == len(pairs) - 1))
    return last


def three(ah, al, bh, bl):
    return [(ah, bh), (ah, bl), (al, bh)]


def project_attention(nc, keep, x, sums, r_dram, bv, bo, n1w, wsplit):
    with ExitStack() as ctx:
        m = Space(nc, ctx, "pa")
        a0, a1 = keep.heads
        rb = m.sb("rb", [P, PAIRS, T])
        dn = m.sb("dn", [P, 4, DH])
        oh, ol = (m.sb(n, [P, PAIRS, T], F16) for n in ("oh", "ol"))
        woh, wol = (m.sb(n, [P, PAIRS, D], F16) for n in ("woh", "wol"))
        bvc, bvs, nw, nws = (m.sb(n, [P, k]) for n, k in (("bvc", PAIRS), ("bvs", PAIRS), ("nw", DC), ("nws", DC)))
        bob, xs, h = m.sb("bob", [P, D]), m.sb("xs", [P, TT, D]), m.sb("h", [P, TT, D])
        rows = Rows(m)
        ident = m.sb("ident", [P, P])
        yp = m.ps("yp", [P, TT, D])
        hT = m.ps("hT", [P, DC, T])
        den_in, small_in, w_in = m.sem("den_in"), m.sem("small_in"), m.sem("w_in")
        next_in, consts, vec_in = m.sem("next_in"), m.sem("consts"), m.sem("vec_in")
        r_parts = (slice(0, 2), slice(2, PAIRS))
        rb_in = [m.sem(f"rb_in{n}") for n in range(len(r_parts))]
        r_ready, r_out, own_dve = m.sem("r_ready"), m.sem("r_out"), m.sem("own_dve")
        s_ready, oh_ready, ol_ready, y_ready = m.sem("s_ready"), m.sem("oh_ready"), m.sem("ol_ready"), m.sem("y_ready")
        var_ready, sd_ready, h_ready = m.sem("var_ready"), m.sem("sd_ready"), m.sem("h_ready")
        hT_ready, hh_ready, hl_ready, made = m.sem("hT_ready"), m.sem("hh_ready"), m.sem("hl_ready"), m.sem("made")
        block = ctx.enter_context(nc.Block())

        @block.sync
        def _(sp):
            for e in range(4):
                sp.dma_start(dn[:, e, :], sums[e].rearrange("(p c) -> p c", p=P)).then_inc(den_in, 16)
            sp.dma_start(bvc[:, :], bv).then_inc(vec_in, 16)
            sp.dma_start(nw[:, :], n1w).then_inc(vec_in, 16)
            sp.dma_start(bob[:, :], bo.partition_broadcast(P)).then_inc(small_in, 16)
            load_split(sp, wsplit, W.O, woh.rearrange("p j d -> p (j d)"), wol.rearrange("p j d -> p (j d)"), w_in)
            sp.wait_ge(r_ready, 1)
            sp.dma_start(r_dram.rearrange("(p c) -> p c", p=P), dn[:, 0, :]).then_inc(r_out, 16)
            sp.wait_ge(r_out, 16)
            for n, js in enumerate(r_parts):
                for hd in range(2):
                    src = r_dram.rearrange("(j e t) -> j e t", e=2, t=T)[js, hd, :].partition_broadcast(DH)
                    sp.dma_start(rb[hd * DH:(hd + 1) * DH, js, :], src).then_inc(rb_in[n], 16)
            sp.dma_start(xs[:, :, :], x.rearrange("(t p) d -> p t d", p=P)).then_inc(small_in, 16)
            load_split(sp, wsplit, W.IN, keep.big[2][:, :], keep.big[3][:, :], next_in)
            sp.wait_ge(next_in, 32)

        @block.gpsimd
        def _(pool):
            identity(nc, pool, ident, made)

        @block.scalar
        def _(act):
            act.wait_ge(consts, 2)
            for j in range(PAIRS):
                act.wait_ge(s_ready, j + 1)
                nc.scalar.activation(oh[:, j, :], a0[:, j, :], ACT.Identity, bias=bvs[:, j:j + 1]).then_inc(oh_ready, 1)
            for n in range(2):
                act.wait_ge(var_ready, n + 1)
                nc.scalar.activation(rows.sd[:, :], rows.var[:, :], ACT.Sqrt).then_inc(sd_ready, 1)
            for c in range(DC):
                act.wait_ge(hT_ready, c + 1)
                nc.scalar.activation(keep.hh[:, c, :], hT[:, c, :], ACT.Copy, scale=nws[:, c:c + 1]).then_inc(hh_ready, 1)

        @block.vector
        def _(dve):
            own = Chain(dve, own_dve)
            dve.wait_ge(den_in, 64)
            for e in range(1, 4):
                own.done(nc.vector.tensor_tensor(dn[:, 0, :], dn[:, 0, :], dn[:, e, :], ALU.add))
            nc.vector.reciprocal(dn[:, 0, :], dn[:, 0, :]).then_inc(r_ready, 1)
            dve.wait_ge(vec_in, 32)
            nc.vector.tensor_scalar(bvs[:, :], bvc[:, :], SA, None, ALU.mult).then_inc(consts, 1)
            nc.vector.tensor_scalar(nws[:, :], nw[:, :], SA, None, ALU.mult).then_inc(consts, 1)
            dve.wait_ge(consts, 2)

            def bias(t):
                dve.wait_ge(small_in, 32)
                own.inc(nc.vector.tensor_tensor(xs[:, t, :], xs[:, t, :], bob[:, :], ALU.add))

            def low(j):
                dve.wait_ge(oh_ready, j + 1)
                nc.vector.scalar_tensor_tensor(ol[:, j, :], a0[:, j, :], bvs[:, j:j + 1], oh[:, j, :],
                                               ALU.add, ALU.subtract).then_inc(ol_ready, 1)

            for j in range(PAIRS):
                own.done(nc.vector.tensor_tensor(a0[:, j, :], a0[:, j, :], a1[:, j, :], ALU.add))
                for n, js in enumerate(r_parts):
                    if j == js.start:
                        dve.wait_ge(rb_in[n], 32)
                nc.vector.tensor_tensor(a0[:, j, :], a0[:, j, :], rb[:, j, :], ALU.mult).then_inc(s_ready, 1)
                if j:
                    low(j - 1)
            low(PAIRS - 1)
            for t in range(TT):
                bias(t)
            own.wait()
            for t in range(TT):
                dve.wait_ge(y_ready, t + 1)
                own.inc(nc.vector.scalar_tensor_tensor(keep.x1[:, t, :], yp[:, t, :], UNSCALE, xs[:, t, :],
                                                       ALU.mult, ALU.add))
            own.wait()
            row_factor(nc, dve, own, keep.x1, *rows.all, var_ready, sd_ready, 1, 1e-5, False)
            for t in range(TT):
                own.inc(nc.vector.tensor_scalar(keep.a[:, t, :], keep.x1[:, t, :], rows.mv[:, t, 0:1],
                                                rows.rs[:, t:t + 1], ALU.subtract, ALU.mult))
            own.wait()
            row_factor(nc, dve, own, keep.a, *rows.all, var_ready, sd_ready, 2, 1e-6, True)
            for t in range(TT):
                nc.vector.tensor_scalar(h[:, t, :], keep.a[:, t, :], rows.rs[:, t:t + 1], None,
                                        ALU.mult).then_inc(h_ready, 1)
            for c in range(DC):
                dve.wait_ge(hh_ready, c + 1)
                nc.vector.scalar_tensor_tensor(keep.hl[:, c, :], hT[:, c, :], nws[:, c:c + 1], keep.hh[:, c, :],
                                               ALU.mult, ALU.subtract).then_inc(hl_ready, 1)

        @block.tensor
        def _(pe):
            pe.wait_ge(made, 2)
            pe.wait_ge(w_in, 32)
            for j in range(PAIRS):
                pe.wait_ge(ol_ready, j + 1)
                for t in range(TT):
                    tok = slice(t * P, (t + 1) * P)
                    last = product(nc, yp[:, t, :], three(oh[:, j, tok], ol[:, j, tok], woh[:, j, :], wol[:, j, :]),
                                   start=(j == 0), stop=(j == PAIRS - 1))
                    if j == PAIRS - 1:
                        last.then_inc(y_ready, 1)
            pe.wait_ge(h_ready, TT)
            transpose_rows(nc, h, hT, ident, hT_ready)


DI = 1024
DIC = DI // P
DS = 16
DR = 32


HN = 4
PASSES = DS // HN


def scan_rows(keep, first):
    return [keep.big[first + q // 2][:, (q % 2) * 2 * WC:(q % 2 + 1) * 2 * WC].bitcast(F32)
            .rearrange("p (n t) -> p n t", t=T) for q in range(PASSES)]


def mamba_inputs(nc, keep, convw, convb, dtb, xd_dram, wsplit):
    with ExitStack() as ctx:
        m = Space(nc, ctx, "mi")
        wh, wl = (keep.big[i].rearrange("p (c n) -> p c n", c=DC) for i in (2, 3))
        sh, sl = (m.sb(n, [P, WC], F16) for n in ("sh", "sl"))
        xp = m.sb("xp", [P, DIC, T + 3])
        cw, cb, db = m.sb("cw", [P, DIC, 4]), m.sb("cb", [P, DIC]), m.sb("db", [P, DIC])
        xih, xil = keep.yh, keep.yl
        xd = m.sb("xd", [2 * DS + DR, T])
        dtw = m.sb("dtw", [3 * DR, DI], F16)
        ds = m.sb("ds", [3 * DR, T], F16)
        pre, soft = keep.delta, m.sb("soft", [P, DIC, T])
        zp = m.ps("zp", [P, 4, T])
        xdp = m.ps("xdp", [2 * DS + DR, T])
        dp = m.ps("dp", [P, 2, T])
        dtw_in, next_in = m.sem("dtw_in"), m.sem("next_in")
        small_in, pad, own_dve = m.sem("small_in"), m.sem("pad"), m.sem("own_dve")
        p_ready, p_read = m.sem("p_ready"), m.sem("p_read")
        conv_ready, xin_ready, xih_ready, xil_ready = (m.sem(n) for n in ("conv_ready", "xin_ready", "xih_ready", "xil_ready"))
        xd_ready, xd_read, xd_out, dh_ready, dl_ready = (m.sem(n) for n in ("xd_ready", "xd_read", "xd_out", "dh_ready", "dl_ready"))
        d_ready, pre_ready, abs_ready, exp_ready, ln_ready = (
            m.sem(n) for n in ("d_ready", "pre_ready", "abs_ready", "exp_ready", "ln_ready"))
        halves = (slice(0, DIC // 2), slice(DIC // 2, DIC))
        block = ctx.enter_context(nc.Block())
        LAST = 2 * DIC - 1
        x_after = {DIC + 1: (0,), DIC + 2: (1, 2), DIC + 3: (3,), DIC + 4: (4, 5), DIC + 5: (6, 7)}
        xpw = [s[:, 0:DIC * 64].rearrange("p (c n) -> p c n", c=DIC) for s in (sh, sl)]

        @block.sync
        def _(sp):
            sp.dma_start(cw[:, :, :], convw).then_inc(small_in, 16)
            sp.dma_start(cb[:, :], convb).then_inc(small_in, 16)
            sp.dma_start(db[:, :], dtb).then_inc(small_in, 16)
            load_split(sp, wsplit, W.SMALL, sh[:, :], sl[:, :], small_in)
            for n, s in enumerate((0, 1, 0)):
                at = DIC * 64 + 64
                sp.dma_start(dtw[n * DR:(n + 1) * DR, :], wsplit[s][0:DR, W.SMALL[0], at:at + DI]).then_inc(dtw_in, 16)
            sp.wait_ge(xd_read, 1)
            sp.dma_start(xd_dram, xd[DR:DR + 2 * DS, :]).then_inc(xd_out, 16)
            sp.wait_ge(xd_out, 16)
            for q, dst in enumerate(scan_rows(keep, 0)):
                sp.dma_start(dst, xd_dram[q * HN:(q + 1) * HN, :].partition_broadcast(P)).then_inc(next_in, 16)
            sp.wait_ge(next_in, 16 * PASSES)

        @block.gpsimd
        def _(pool):
            nc.gpsimd.memset(xp[:, :, 0:3], 0.0).then_inc(pad, 1)

        @block.scalar
        def _(act):
            def conv_out(c):
                if c == 0:
                    act.wait_ge(small_in, 80)
                act.wait_ge(conv_ready, c + 1)
                nc.scalar.activation(keep.xin[:, c, :], soft[:, c, :], ACT.Silu, bias=cb[:, c:c + 1]).then_inc(xin_ready, 1)
                act.wait_ge(xin_ready, c + 1)
                nc.scalar.activation(xih[:, c, :], keep.xin[:, c, :], ACT.Copy, scale=SA).then_inc(xih_ready, 1)

            after = {c + 1 + c // 2: c for c in range(DIC)}
            for f in range(2 * DIC):
                if f == LAST:
                    act.wait_ge(xd_ready, 1)
                    nc.scalar.activation(xd[:, :], xdp[:, :], ACT.Copy, scale=UNSCALE).then_inc(xd_read, 1)
                    act.wait_ge(xd_read, 1)
                    for n in range(2):
                        nc.scalar.activation(ds[n * DR:(n + 1) * DR, :], xd[0:DR, :], ACT.Copy, scale=SA).then_inc(dh_ready, 1)
                    act.wait_ge(xin_ready, DIC)
                    for c in range(DIC):
                        act.wait_ge(pre_ready, c + 1)
                        nc.scalar.activation(soft[:, c, :], pre[:, c, :], ACT.Abs).then_inc(abs_ready, 1)
                    for half in halves:
                        act.wait_ge(abs_ready, half.stop)
                        nc.scalar.activation(soft[:, half, :], soft[:, half, :], ACT.Exp, scale=-1.0).then_inc(exp_ready, 1)
                    for n, half in enumerate(halves):
                        act.wait_ge(exp_ready, n + 1)
                        nc.scalar.activation(soft[:, half, :], soft[:, half, :], ACT.Ln, bias=1.0).then_inc(ln_ready, 1)
                act.wait_ge(p_ready, f + 1)
                if f < DIC:
                    nc.scalar.activation(xp[:, f, 3:], zp[:, f % 4, :], ACT.Copy, scale=UNSCALE).then_inc(p_read, 1)
                else:
                    nc.scalar.activation(keep.zs[:, f - DIC, :], zp[:, f % 4, :], ACT.Silu,
                                         scale=UNSCALE).then_inc(p_read, 1)
                if f in after:
                    conv_out(after[f])

        @block.vector
        def _(dve):
            own = Chain(dve, own_dve)

            def low(c):
                dve.wait_ge(xih_ready, c + 1)
                nc.vector.scalar_tensor_tensor(xil[:, c, :], keep.xin[:, c, :], SA, xih[:, c, :], ALU.mult,
                                               ALU.subtract).then_inc(xil_ready, 1)

            dve.wait_ge(small_in, 80)
            dve.wait_ge(pad, 1)
            for f in range(DIC):
                dve.wait_ge(p_read, f + 1)
                c = soft[:, f, :]
                own.done(nc.vector.tensor_scalar(c, xp[:, f, 0:T], cw[:, f, 0:1], None, ALU.mult))
                for k in range(1, 4):
                    ins = nc.vector.scalar_tensor_tensor(c, xp[:, f, k:k + T], cw[:, f, k:k + 1], c, ALU.mult, ALU.add)
                    if k < 3:
                        own.done(ins)
                ins.then_inc(conv_ready, 1)
                if f:
                    low(f - 1)
            low(DIC - 1)
            dve.wait_ge(dh_ready, 1)
            nc.vector.scalar_tensor_tensor(ds[2 * DR:3 * DR, :], xd[0:DR, :], SA, ds[0:DR, :], ALU.mult,
                                           ALU.subtract).then_inc(dl_ready, 1)
            for f in range(DIC):
                dve.wait_ge(d_ready, f + 1)
                nc.vector.tensor_scalar(pre[:, f, :], dp[:, f % 2, :], UNSCALE, db[:, f:f + 1],
                                        ALU.mult, ALU.add).then_inc(pre_ready, 1)
            dve.wait_ge(pre_ready, DIC)
            for n, half in enumerate(halves):
                dve.wait_ge(ln_ready, n + 1)
                own.inc(nc.vector.scalar_tensor_tensor(pre[:, half, :], pre[:, half, :], 0.0, soft[:, half, :],
                                                       ALU.max, ALU.add))

        @block.tensor
        def _(pe):
            def x_proj(c):
                pe.wait_ge(xil_ready, c + 1)
                last = product(nc, xdp[:, :], three(xpw[0][:, c, :], xpw[1][:, c, :], xih[:, c, :], xil[:, c, :]),
                               start=(c == 0), stop=(c == DIC - 1))
                if c == DIC - 1:
                    last.then_inc(xd_ready, 1)

            for f in range(2 * DIC):
                if f == LAST:
                    pe.wait_ge(dtw_in, 48)
                    pe.wait_ge(dh_ready, 2)
                    pe.wait_ge(dl_ready, 1)
                    for c in range(DIC):
                        if c >= 2:
                            pe.wait_ge(pre_ready, c - 1)
                        nc.tensor.matmul(dp[:, c % 2, :], dtw[:, c * P:(c + 1) * P], ds[:, :], start=True,
                                         stop=True).then_inc(d_ready, 1)
                if f >= 4:
                    pe.wait_ge(p_read, f - 3)
                cols = slice(f * P, (f + 1) * P)
                product(nc, zp[:, f % 4, :], [p for c in range(DC) for p in
                                              three(wh[:, c, cols], wl[:, c, cols], keep.hh[:, c, :], keep.hl[:, c, :])]
                        ).then_inc(p_ready, 1)
                if DIC < f < LAST - 1:
                    if f == DIC + 1:
                        pe.wait_ge(small_in, 80)
                    for c in x_after[f]:
                        x_proj(c)


def mamba_scan(nc, keep, a_log, dskip, xd_dram, wsplit):
    with ExitStack() as ctx:
        m = Space(nc, ctx, "ms")
        bb, cc = (scan_rows(keep, first) for first in (0, 2))
        al, aneg, dk = m.sb("al", [P, DIC, DS]), m.sb("aneg", [P, DIC, DS]), m.sb("dk", [P, DIC])
        da = [m.sb(f"da{i}", [P, HN, T]) for i in range(2)]
        hs = [m.sb(f"hs{i}", [P, HN, T]) for i in range(2)]
        u = m.sb("u", [P, T])
        xk = m.sb("xk", [P, 2, T])
        y = m.sb("y", [P, 2, T])
        ident = m.sb("ident", [P, P])
        yp = m.ps("yp", [P, 2, T])
        op = m.ps("op", [P, TT, D])
        o_ready = m.sem("o_ready")
        wh, wl = keep.hidden, keep.outl
        in_sem, made, a_ready, zero_ready = m.sem("in_sem"), m.sem("made"), m.sem("a_ready"), m.sem("zero_ready")
        da_ready, scanned, hc_ready, summed = (m.sem(n) for n in ("da_ready", "scanned", "hc_ready", "summed"))
        xk_ready = m.sem("xk_ready")
        c_in = [m.sem(f"c_in{q}") for q in range(PASSES)]
        w_in = m.sem("w_in")
        own_dve, y_ready, yh_ready, yl_ready = (m.sem(n) for n in ("own_dve", "y_ready", "yh_ready", "yl_ready"))
        block = ctx.enter_context(nc.Block())
        passes = [(f, q) for f in range(DIC) for q in range(PASSES)]

        @block.sync
        def _(sp):
            sp.dma_start(al[:, :, :], a_log).then_inc(in_sem, 16)
            sp.dma_start(dk[:, :], dskip).then_inc(in_sem, 16)
            for q in range(PASSES):
                sp.dma_start(cc[q], xd_dram[DS + q * HN:DS + (q + 1) * HN, :].partition_broadcast(P)).then_inc(c_in[q], 16)
            load_split(sp, wsplit, W.OUT, keep.hidden.rearrange("p c n -> p (c n)"),
                       keep.outl.rearrange("p c n -> p (c n)"), w_in)

        @block.gpsimd
        def _(pool):
            identity(nc, pool, ident, made)
            for i in range(2):
                nc.gpsimd.memset(da[i][:, :, 0:1], 0.0).then_inc(zero_ready, 1)

        @block.scalar
        def _(act):
            def high(f):
                act.wait_ge(y_ready, f + 1)
                nc.scalar.activation(keep.yh[:, f, :], y[:, f % 2, :], ACT.Copy, scale=SA).then_inc(yh_ready, 1)

            act.wait_ge(in_sem, 32)
            nc.scalar.activation(aneg[:, :, :], al[:, :, :], ACT.Exp).then_inc(a_ready, 1)
            act.wait_ge(a_ready, 2)
            act.wait_ge(zero_ready, 2)
            for i, (f, q) in enumerate(passes):
                if q == 0:
                    if f >= 2:
                        act.wait_ge(summed, PASSES * (f - 2) + 1)
                    nc.scalar.activation(xk[:, f % 2, :], keep.xin[:, f, :], ACT.Copy,
                                         scale=dk[:, f:f + 1]).then_inc(xk_ready, 1)
                if i >= 2:
                    act.wait_ge(scanned, i - 1)
                for n in range(HN):
                    s = q * HN + n
                    last = nc.scalar.activation(da[i % 2][:, n, 1:], keep.delta[:, f, 1:], ACT.Exp,
                                                scale=aneg[:, f, s:s + 1])
                last.then_inc(da_ready, 1)
                if q == 2 and f:
                    high(f - 1)
            high(DIC - 1)

        @block.vector
        def _(dve):
            own = Chain(dve, own_dve)
            dve.wait_ge(a_ready, 1)
            nc.vector.tensor_scalar(aneg[:, :, :], aneg[:, :, :], -1.0, None, ALU.mult).then_inc(a_ready, 1)

            def gate(f):
                dve.wait_ge(summed, PASSES * (f + 1))
                if f >= 2:
                    dve.wait_ge(yl_ready, f - 1)
                nc.vector.tensor_tensor(y[:, f % 2, :], yp[:, f % 2, :], keep.zs[:, f, :], ALU.mult).then_inc(y_ready, 1)

            def low(f):
                dve.wait_ge(yh_ready, f + 1)
                nc.vector.scalar_tensor_tensor(keep.yl[:, f, :], y[:, f % 2, :], SA, keep.yh[:, f, :], ALU.mult,
                                               ALU.subtract).then_inc(yl_ready, 1)

            for i, (f, q) in enumerate(passes):
                b = hs[i % 2]
                if q == 0:
                    own.done(nc.vector.tensor_tensor(u[:, :], keep.delta[:, f, :], keep.xin[:, f, :], ALU.mult))
                if i >= 2:
                    dve.wait_ge(summed, i - 1)
                own.done(nc.vector.tensor_tensor(b[:, :, :], u[:, :].unsqueeze(1).to_broadcast([P, HN, T]),
                                                 bb[q], ALU.mult))
                dve.wait_ge(da_ready, i + 1)
                flat = b.rearrange("p n t -> p (n t)")
                nc.vector.tensor_tensor_scan(flat, da[i % 2].rearrange("p n t -> p (n t)"), flat, 0.0,
                                             ALU.mult, ALU.add).then_inc(scanned, 1)
                dve.wait_ge(scanned, i + 1)
                if f == 0:
                    dve.wait_ge(c_in[q], 16)
                nc.vector.tensor_tensor(b[:, :, :], b[:, :, :], cc[q], ALU.mult).then_inc(hc_ready, 1)
                if q == 1 and f:
                    gate(f - 1)
                if q == 3 and f:
                    low(f - 1)
            gate(DIC - 1)
            low(DIC - 1)
            for t in range(TT):
                dve.wait_ge(o_ready, t + 1)
                nc.vector.scalar_tensor_tensor(keep.a[:, t, :], op[:, t, :], UNSCALE, keep.a[:, t, :],
                                               ALU.mult, ALU.add)

        @block.tensor
        def _(pe):
            def out_proj(j):
                pe.wait_ge(yl_ready, j + 1)
                for t in range(TT):
                    tok = slice(t * P, (t + 1) * P)
                    last = product(nc, op[:, t, :], three(keep.yh[:, j, tok], keep.yl[:, j, tok], wh[:, j, :], wl[:, j, :]),
                                   start=(j == 0), stop=(j == DIC - 1))
                    if j == DIC - 1:
                        last.then_inc(o_ready, 1)

            pe.wait_ge(made, 2)
            for i, (f, q) in enumerate(passes):
                if q == 0:
                    if f >= 2:
                        pe.wait_ge(y_ready, f - 1)
                    pe.wait_ge(xk_ready, f + 1)
                    nc.tensor.matmul(yp[:, f % 2, :], ident[:, :], xk[:, f % 2, :], start=True, stop=False)
                pe.wait_ge(hc_ready, i + 1)
                for n in range(HN):
                    last = nc.tensor.matmul(yp[:, f % 2, :], ident[:, :], hs[i % 2][:, n, :],
                                            start=False, stop=(q == PASSES - 1 and n == HN - 1))
                last.then_inc(summed, 1)
                if q == 0 and f >= 2:
                    if f == 2:
                        pe.wait_ge(w_in, 32)
                    out_proj(f - 2)
            out_proj(DIC - 2)
            out_proj(DIC - 1)


DF = 2048
DFC = DF // P


def load_gates(eng, keep, wsplit, cols, sem):
    for n, at in enumerate((W.W1[0], W.W3[0])):
        for s in range(2):
            eng.dma_start(keep.big[2 * n + s].rearrange("p (c n) -> p c n", c=DC)[:, :, cols],
                          wsplit[s][:, at:at + DC, cols]).then_inc(sem, 16)


def second_norm(nc, keep, n2w, wsplit):
    with ExitStack() as ctx:
        m = Space(nc, ctx, "mo")
        nw, nws, h = m.sb("nw", [P, DC]), m.sb("nws", [P, DC]), m.sb("h", [P, TT, D])
        rows = Rows(m)
        ident = m.sb("ident", [P, P])
        hT = m.ps("hT", [P, DC, T])
        next_in, n_in, own_dve, made = (m.sem(n) for n in ("next_in", "n_in", "own_dve", "made"))
        var_ready, sd_ready, h_ready = m.sem("var_ready"), m.sem("sd_ready"), m.sem("h_ready")
        hT_ready, hh_ready, hl_ready = m.sem("hT_ready"), m.sem("hh_ready"), m.sem("hl_ready")
        nws_ready = m.sem("nws_ready")
        block = ctx.enter_context(nc.Block())

        @block.sync
        def _(sp):
            sp.dma_start(nw[:, :], n2w).then_inc(n_in, 16)
            load_gates(sp, keep, wsplit, slice(0, DF // 2), next_in)
            sp.wait_ge(next_in, 64)

        @block.gpsimd
        def _(pool):
            identity(nc, pool, ident, made)

        @block.scalar
        def _(act):
            act.wait_ge(var_ready, 1)
            nc.scalar.activation(rows.sd[:, :], rows.var[:, :], ACT.Sqrt).then_inc(sd_ready, 1)
            act.wait_ge(nws_ready, 1)
            for c in range(DC):
                act.wait_ge(hT_ready, c + 1)
                nc.scalar.activation(keep.hh[:, c, :], hT[:, c, :], ACT.Copy, scale=nws[:, c:c + 1]).then_inc(hh_ready, 1)

        @block.vector
        def _(dve):
            own = Chain(dve, own_dve)
            row_factor(nc, dve, own, keep.a, *rows.all, var_ready, sd_ready, 1, 1e-6, True)
            dve.wait_ge(n_in, 16)
            nc.vector.tensor_scalar(nws[:, :], nw[:, :], SA, None, ALU.mult).then_inc(nws_ready, 1)
            dve.wait_ge(nws_ready, 1)
            for t in range(TT):
                nc.vector.tensor_scalar(h[:, t, :], keep.a[:, t, :], rows.rs[:, t:t + 1], None,
                                        ALU.mult).then_inc(h_ready, 1)
            for c in range(DC):
                dve.wait_ge(hh_ready, c + 1)
                nc.vector.scalar_tensor_tensor(keep.hl[:, c, :], hT[:, c, :], nws[:, c:c + 1], keep.hh[:, c, :],
                                               ALU.mult, ALU.subtract).then_inc(hl_ready, 1)

        @block.tensor
        def _(pe):
            pe.wait_ge(made, 2)
            pe.wait_ge(h_ready, TT)
            transpose_rows(nc, h, hT, ident, hT_ready)


NE = 16
NX = NE + 2
EH = 512
EHC = EH // P


class ExpertPlaces:

    def __init__(self, keep):
        b = keep.big
        f32 = lambda t: t.bitcast(F32)
        self.gf = [f32(b[i][:, :]).rearrange("p (c n) -> p c n", c=DC) for i in (0, 2)]
        self.df = [f32(b[1][:, i * 2 * WC:(i + 1) * 2 * WC]).rearrange("p (c n) -> p c n", c=EHC) for i in range(2)]
        self.gh, self.gl = ([b[3][:, i * 2 * WC:(i + 1) * 2 * WC].rearrange("p (c n) -> p c n", c=DC)] for i in range(2))


def gated_mlp(nc, keep, wsplit, gate_up, down):
    with ExitStack() as ctx:
        m = Space(nc, ctx, "gm")
        w1h, w1l, w3h, w3l = (b.rearrange("p (c n) -> p c n", c=DC) for b in keep.big)
        ex = ExpertPlaces(keep)
        w2h, w2l = (m.sb(n, [P, DFC, D], F16) for n in ("w2h", "w2l"))
        sg, mf = m.sb("sg", [P, 2, T]), m.sb("mf", [P, 2, T])
        mh, ml = (m.sb(n, [P, DFC, T], F16) for n in ("mh", "ml"))
        rows = Rows(m)
        gp, up = m.ps("gp", [P, 2, T]), m.ps("up", [P, 2, T])
        op = m.ps("op", [P, TT, D])
        w_in, w2_in, own_dve = m.sem("w_in"), m.sem("w2_in"), m.sem("own_dve")
        next_in, next_h, next_l = m.sem("next_in"), m.sem("next_h"), m.sem("next_l")
        g_ready, u_ready, sg_ready, mf_ready, mh_ready, ml_ready = (
            m.sem(n) for n in ("g_ready", "u_ready", "sg_ready", "mf_ready", "mh_ready", "ml_ready"))
        o_ready, var_ready, sd_ready = m.sem("o_ready"), m.sem("var_ready"), m.sem("sd_ready")
        block = ctx.enter_context(nc.Block())

        @block.sync
        def _(sp):
            load_gates(sp, keep, wsplit, slice(DF // 2, DF), w_in)
            load_split(sp, wsplit, W.W2, w2h.rearrange("p c n -> p (c n)"), w2l.rearrange("p c n -> p (c n)"), w2_in)
            sp.wait_ge(u_ready, DFC)
            sp.dma_start(ex.gf[0], gate_up[0:D, :].rearrange("(c p) n -> p c n", p=P)).then_inc(next_in, 16)
            sp.dma_start(ex.df[0], down[0:EH, :].rearrange("(c p) n -> p c n", p=P)).then_inc(next_in, 16)
            sp.wait_ge(next_in, 32)

        @block.scalar
        def _(act):
            for f in range(DFC):
                act.wait_ge(g_ready, f + 1)
                if f >= 2:
                    act.wait_ge(mf_ready, f - 1)
                nc.scalar.activation(sg[:, f % 2, :], gp[:, f % 2, :], ACT.Silu, scale=UNSCALE).then_inc(sg_ready, 1)
                if f:
                    act.wait_ge(mf_ready, f)
                    nc.scalar.activation(mh[:, f - 1, :], mf[:, (f - 1) % 2, :], ACT.Copy).then_inc(mh_ready, 1)
            act.wait_ge(mf_ready, DFC)
            nc.scalar.activation(mh[:, DFC - 1, :], mf[:, (DFC - 1) % 2, :], ACT.Copy).then_inc(mh_ready, 1)
            act.wait_ge(next_in, 32)
            nc.scalar.activation(ex.gh[0], ex.gf[0], ACT.Copy, scale=SW).then_inc(next_h, 1)
            act.wait_ge(var_ready, 1)
            nc.scalar.activation(rows.sd[:, :], rows.var[:, :], ACT.Sqrt).then_inc(sd_ready, 1)

        @block.vector
        def _(dve):
            own = Chain(dve, own_dve)

            def low(f):
                dve.wait_ge(mh_ready, f + 1)
                nc.vector.tensor_tensor(ml[:, f, :], mf[:, f % 2, :], mh[:, f, :], ALU.subtract).then_inc(ml_ready, 1)

            for f in range(DFC):
                if f >= 2:
                    low(f - 2)
                    dve.wait_ge(ml_ready, f - 1)
                dve.wait_ge(u_ready, f + 1)
                dve.wait_ge(sg_ready, f + 1)
                nc.vector.scalar_tensor_tensor(mf[:, f % 2, :], up[:, f % 2, :], SA * UNSCALE, sg[:, f % 2, :],
                                               ALU.mult, ALU.mult).then_inc(mf_ready, 1)
            for t in range(TT):
                own.inc(nc.vector.tensor_tensor(keep.x1[:, t, :], keep.x1[:, t, :], keep.a[:, t, :], ALU.add))
            low(DFC - 2)
            low(DFC - 1)
            dve.wait_ge(next_h, 1)
            nc.vector.scalar_tensor_tensor(ex.gl[0], ex.gf[0], SW, ex.gh[0], ALU.mult,
                                           ALU.subtract).then_inc(next_l, 1)
            own.wait()
            for t in range(TT):
                dve.wait_ge(o_ready, t + 1)
                own.inc(nc.vector.scalar_tensor_tensor(keep.x1[:, t, :], op[:, t, :], UNSCALE, keep.x1[:, t, :],
                                                       ALU.mult, ALU.add))
            own.wait()
            row_factor(nc, dve, own, keep.x1, *rows.all, var_ready, sd_ready, 1, 1e-5, False)
            for t in range(TT):
                own.inc(nc.vector.tensor_scalar(keep.a[:, t, :], keep.x1[:, t, :], rows.mv[:, t, 0:1],
                                                rows.rs[:, t:t + 1], ALU.subtract, ALU.mult))

        @block.tensor
        def _(pe):
            for f in range(DFC):
                cols = slice(f * P, (f + 1) * P)
                if f == DFC // 2:
                    pe.wait_ge(w_in, 64)
                if f >= 2:
                    pe.wait_ge(sg_ready, f - 1)
                product(nc, gp[:, f % 2, :], [p for c in range(DC) for p in
                                              three(w1h[:, c, cols], w1l[:, c, cols], keep.hh[:, c, :], keep.hl[:, c, :])]
                        ).then_inc(g_ready, 1)
                if f >= 2:
                    pe.wait_ge(mf_ready, f - 1)
                product(nc, up[:, f % 2, :], [p for c in range(DC) for p in
                                              three(w3h[:, c, cols], w3l[:, c, cols], keep.hh[:, c, :], keep.hl[:, c, :])]
                        ).then_inc(u_ready, 1)
            pe.wait_ge(w2_in, 32)
            for t in range(TT):
                tok = slice(t * P, (t + 1) * P)
                for j in range(DFC):
                    if t == 0:
                        pe.wait_ge(ml_ready, j + 1)
                    last = product(nc, op[:, t, :], three(mh[:, j, tok], ml[:, j, tok], w2h[:, j, :], w2l[:, j, :]),
                                   start=(j == 0), stop=(j == DFC - 1))
                last.then_inc(o_ready, 1)




def route(nc, keep, gates, wsplit):
    with ExitStack() as ctx:
        m = Space(nc, ctx, "ro")
        rh, rl = (m.sb(n, [P, DC, NE], F16) for n in ("rh", "rl"))
        ident = m.sb("ident", [P, P])
        shape = [P, TT, NE]
        lg, rank, eq, one, two, sig = (m.sb(n, shape) for n in ("lg", "rank", "eq", "one", "two", "sig"))
        top, first = m.sb("top", [P, TT]), m.sb("first", [P, TT])
        hT = m.ps("hT", [P, DC, T])
        lp = m.ps("lp", [P, TT, T])
        w_in, made, rank_ready, own_dve = m.sem("w_in"), m.sem("made"), m.sem("rank_ready"), m.sem("own_dve")
        hT_ready, hh_ready, hl_ready, l_ready = (m.sem(n) for n in ("hT_ready", "hh_ready", "hl_ready", "l_ready"))
        lg_ready, sig_ready = m.sem("lg_ready"), m.sem("sig_ready")
        block = ctx.enter_context(nc.Block())

        @block.sync
        def _(sp):
            at = DIC * 64
            for s, r in enumerate((rh, rl)):
                sp.dma_start(r.rearrange("p c n -> p (c n)"), wsplit[s][:, W.SMALL[0], at:at + DC * NE]).then_inc(w_in, 16)

        @block.gpsimd
        def _(pool):
            identity(nc, pool, ident, made)
            for e in range(NE):
                nc.gpsimd.memset(rank[:, :, e:e + 1], float(NE - e)).then_inc(rank_ready, 1)
            nc.gpsimd.memset(gates[:, :, NE:NX], UNSCALE).then_inc(rank_ready, 1)

        @block.scalar
        def _(act):
            for c in range(DC):
                act.wait_ge(hT_ready, c + 1)
                nc.scalar.activation(keep.hh[:, c, :], hT[:, c, :], ACT.Copy, scale=SA).then_inc(hh_ready, 1)
            act.wait_ge(lg_ready, TT)
            nc.scalar.activation(sig[:, :, :], lg[:, :, :], ACT.Sigmoid).then_inc(sig_ready, 1)

        @block.vector
        def _(dve):
            own = Chain(dve, own_dve)
            for c in range(DC):
                dve.wait_ge(hh_ready, c + 1)
                nc.vector.scalar_tensor_tensor(keep.hl[:, c, :], hT[:, c, :], SA, keep.hh[:, c, :],
                                               ALU.mult, ALU.subtract).then_inc(hl_ready, 1)
            for t in range(TT):
                dve.wait_ge(l_ready, t + 1)
                nc.vector.tensor_scalar(lg[:, t, :], lp[:, t, 0:NE], UNSCALE, None, ALU.mult).then_inc(lg_ready, 1)
            dve.wait_ge(lg_ready, TT)
            dve.wait_ge(rank_ready, NE + 1)

            def pick(src, dst):
                own.done(nc.vector.reduce_max(top[:, :], src[:, :, :], AX.X))
                own.done(nc.vector.tensor_tensor(eq[:, :, :], src[:, :, :], top[:, :].unsqueeze(2).to_broadcast(shape),
                                                 ALU.is_equal))
                own.done(nc.vector.tensor_tensor(eq[:, :, :], eq[:, :, :], rank[:, :, :], ALU.mult))
                own.done(nc.vector.reduce_max(first[:, :], eq[:, :, :], AX.X))
                own.done(nc.vector.tensor_tensor(dst[:, :, :], eq[:, :, :], first[:, :].unsqueeze(2).to_broadcast(shape),
                                                 ALU.is_equal))

            pick(lg, one)
            own.done(nc.vector.scalar_tensor_tensor(two[:, :, :], one[:, :, :], -1e30, lg[:, :, :], ALU.mult, ALU.add))
            pick(two, two)
            own.done(nc.vector.tensor_tensor(one[:, :, :], one[:, :, :], two[:, :, :], ALU.add))
            own.done(nc.vector.tensor_scalar(one[:, :, :], one[:, :, :], UNSCALE, None, ALU.mult))
            dve.wait_ge(sig_ready, 1)
            own.inc(nc.vector.tensor_tensor(gates[:, :, 0:NE], one[:, :, :], sig[:, :, :], ALU.mult))

        @block.tensor
        def _(pe):
            pe.wait_ge(made, 2)
            transpose_rows(nc, keep.a, hT, ident, hT_ready)
            pe.wait_ge(w_in, 32)
            pe.wait_ge(hl_ready, DC)
            for t in range(TT):
                tok = slice(t * P, (t + 1) * P)
                product(nc, lp[:, t, 0:NE], [p for c in range(DC) for p in
                                             three(keep.hh[:, c, tok], keep.hl[:, c, tok], rh[:, c, :], rl[:, c, :])]
                        ).then_inc(l_ready, 1)


def experts(nc, keep, gates, gate_up, down, out):
    with ExitStack() as ctx:
        m = Space(nc, ctx, "ex")
        ex = ExpertPlaces(keep)
        gf, df = ex.gf, ex.df
        gh, gl = ([first, m.sb(n, [P, DC, 2 * EH], F16)] for n, first in (("gh", ex.gh[0]), ("gl", ex.gl[0])))
        dh, dl = ([m.sb(f"{n}{i}", [P, EHC, D], F16) for i in range(2)] for n in ("dh", "dl"))
        sg, mf = m.sb("sg", [P, EHC, T]), m.sb("mf", [P, EHC, T])
        mh, ml = ([m.sb(f"{n}{i}", [P, EHC, T], F16) for i in range(2)] for n in ("mh", "ml"))
        gp, up = m.ps("gp", [P, 2, T]), m.ps("up", [P, 2, T])
        op = m.ps("op", [P, TT, D])
        g_in, d_in = ([m.sem(f"{n}{i}") for i in range(2)] for n in ("g_in", "d_in"))
        gh_ready, gl_ready, dh_ready, dl_ready = (m.sem(n) for n in ("gh_ready", "gl_ready", "dh_ready", "dl_ready"))
        g_ready, u_ready = m.sem("g_ready"), m.sem("u_ready")
        sg_ready, mf_ready, o_read = m.sem("sg_ready"), m.sem("mf_ready"), m.sem("o_read")
        mh_ready, ml_ready, o_ready, y_out = (m.sem(n) for n in ("mh_ready", "ml_ready", "o_ready", "y_out"))
        block = ctx.enter_context(nc.Block())

        @block.sync
        def _(sp):
            def load_gate_up(e, par):
                sp.dma_start(gf[par], gate_up.rearrange("(e c p) n -> p e c n", p=P, c=DC)[:, bass.ds(e, 1), :, :]
                             .rearrange("p o c n -> p (o c) n")).then_inc(g_in[par], 16)

            def load_down(e, par):
                sp.dma_start(df[par], down.rearrange("(e c p) n -> p e c n", p=P, c=EHC)[:, bass.ds(e, 1), :, :]
                             .rearrange("p o c n -> p (o c) n")).then_inc(d_in[par], 16)

            load_gate_up(1, 1)
            load_down(1, 1)
            with sp.Fori(0, NX // 2 - 1) as i:
                for par in range(2):
                    sp.wait_ge(gl_ready, i * (2 * DC) + (par + 1) * DC)
                    load_gate_up(i * 2 + par + 2, par)
                    sp.wait_ge(dl_ready, i * 4 + 2 * par + 2)
                    load_down(i * 2 + par + 2, par)
            for t in range(TT):
                sp.wait_ge(o_read, NX * TT + t + 1)
                sp.dma_start(out[t * P:(t + 1) * P, :], keep.x1[:, t, :]).then_inc(y_out, 16)
            sp.wait_ge(y_out, 16 * TT)

        def loop(eng, body):
            body(0, 0, 0, "first")
            with eng.Fori(0, NX // 2 - 1) as i:
                body(i * 2 + 1, 1, i, "inner")
                body(i * 2 + 2, 0, i + 1, "inner")
            body(NX - 1, 1, NX // 2 - 1, "last")

        @block.scalar
        def _(act):
            def split_down(par, p):
                cs = slice(2 * p, 2 * p + 2)
                nc.scalar.activation(dh[par][:, cs, :], df[par][:, cs, :], ACT.Copy, scale=SW).then_inc(dh_ready, 1)

            def split_next(e, par, turn, j):
                nxt = 1 - par
                if j == 0:
                    act.wait_ge(g_in[nxt], (turn + 1) * 16)
                if j < 2:
                    for c in (2 * j, 2 * j + 1):
                        nc.scalar.activation(gh[nxt][:, c, :], gf[nxt][:, c, :], ACT.Copy, scale=SW).then_inc(gh_ready, 1)
                else:
                    if j == 2:
                        act.wait_ge(d_in[nxt], (turn + 1) * 16)
                        if not isinstance(e, int) or e:
                            act.wait_ge(o_ready, e * TT)
                    split_down(nxt, j - 2)

            def high(e, par, j):
                act.wait_ge(mf_ready, e * EHC + j + 1 + 2)
                nc.scalar.activation(mh[par][:, j, :], mf[:, j, :], ACT.Copy).then_inc(mh_ready, 1)

            def body(e, par, turn, kind):
                for j in range(EHC):
                    act.wait_ge(g_ready, e * EHC + j + 1)
                    nc.scalar.activation(sg[:, j, :], gp[:, j % 2, :], ACT.Silu, scale=UNSCALE).then_inc(sg_ready, 1)
                    if j:
                        high(e, par, j - 1)
                    if kind != "last":
                        split_next(e, par, turn, j)
                high(e, par, EHC - 1)

            split_down(0, 0)
            split_down(0, 1)
            loop(act, body)

        @block.vector
        def _(dve):
            dve.sem_inc(sg_ready, 2)
            dve.sem_inc(mf_ready, 2)
            dve.sem_inc(o_read, TT)
            dve.sem_inc(gl_ready, DC)

            def split_down(e, par, p):
                cs = slice(2 * p, 2 * p + 2)
                dve.wait_ge(dh_ready, e * 2 + p + 1)
                nc.vector.scalar_tensor_tensor(dl[par][:, cs, :], df[par][:, cs, :], SW, dh[par][:, cs, :], ALU.mult,
                                               ALU.subtract).then_inc(dl_ready, 1)

            def split_next(e, par, j):
                nxt = 1 - par
                if j < 2:
                    for c in (2 * j, 2 * j + 1):
                        dve.wait_ge(gh_ready, e * DC + c + 1)
                        nc.vector.scalar_tensor_tensor(gl[nxt][:, c, :], gf[nxt][:, c, :], SW, gh[nxt][:, c, :],
                                                       ALU.mult, ALU.subtract).then_inc(gl_ready, 1)
                else:
                    split_down(e + 1, nxt, j - 2)

            def low(e, par, j):
                dve.wait_ge(mh_ready, e * EHC + j + 1)
                nc.vector.tensor_tensor(ml[par][:, j, :], mf[:, j, :], mh[par][:, j, :], ALU.subtract).then_inc(ml_ready, 1)

            def add(e):
                for t in range(TT):
                    dve.wait_ge(o_ready, e * TT + t + 1)
                    dve.wait_ge(o_read, e * TT + t + 1)
                    nc.vector.scalar_tensor_tensor(keep.x1[:, t, :], op[:, t, :], gates[:, t, bass.ds(e, 1)],
                                                   keep.x1[:, t, :], ALU.mult, ALU.add).then_inc(o_read, 1)

            def body(e, par, turn, kind):
                for j in range(EHC):
                    dve.wait_ge(u_ready, e * EHC + j + 1)
                    dve.wait_ge(sg_ready, e * EHC + j + 1 + 2)
                    if kind != "first":
                        dve.wait_ge(ml_ready, e * EHC)
                    nc.vector.scalar_tensor_tensor(mf[:, j, :], up[:, j % 2, :], SA * UNSCALE, sg[:, j, :], ALU.mult,
                                                   ALU.mult).then_inc(mf_ready, 1)
                    if j:
                        low(e, par, j - 1)
                    if j == 2 and kind != "first":
                        add(e - 1)
                    if kind != "last":
                        split_next(e, par, j)
                low(e, par, EHC - 1)

            split_down(0, 0, 0)
            split_down(0, 0, 1)
            loop(dve, body)
            add(NX - 1)

        @block.tensor
        def _(pe):
            def down_proj(e, par):
                pe.wait_ge(dl_ready, e * 2 + 2)
                for t in range(TT):
                    tok = slice(t * P, (t + 1) * P)
                    pe.wait_ge(o_read, e * TT + t + 1)
                    for j in range(EHC):
                        if t == 0:
                            pe.wait_ge(ml_ready, e * EHC + j + 1)
                        last = product(nc, op[:, t, :], three(mh[par][:, j, tok], ml[par][:, j, tok],
                                                              dh[par][:, j, :], dl[par][:, j, :]),
                                       start=(j == 0), stop=(j == EHC - 1))
                    last.then_inc(o_ready, 1)

            def body(e, par, turn, kind):
                pe.wait_ge(gl_ready, e * DC + DC)
                for j in range(EHC):
                    for half, bank, free, ready in ((0, gp, sg_ready, g_ready), (1, up, mf_ready, u_ready)):
                        cols = slice(half * EH + j * P, half * EH + (j + 1) * P)
                        pe.wait_ge(free, e * EHC + j + 1)
                        product(nc, bank[:, j % 2, :], [p for c in range(DC) for p in
                                                        three(gh[par][:, c, cols], gl[par][:, c, cols],
                                                              keep.hh[:, c, :], keep.hl[:, c, :])]
                                ).then_inc(ready, 1)
                    if j == 1 and kind != "first":
                        down_proj(e - 1, 1 - par)

            loop(pe, body)
            down_proj(NX - 1, 1)


class Keep:
    pass


def program(nc, x, ctxT, wq, bq, wk, bk, wv, bv, bo, n1w, n2w, convw, convb, dtb, a_log, dskip, wpack, gate_up,
            down, out):
    def scratch(name, shape, dt=F32):
        return nc.dram_tensor(name, shape, dt).ap()

    q_dram = scratch("q_dram", [2, NH * DH, T], F16)
    kd = scratch("kd", [2, DH, NH, S], F16)
    vd = scratch("vd", [NH, P, S], F16)
    wsplit = scratch("wsplit", [2, P, WT, WC], F16)
    sums = scratch("sums", [4, NH * T])
    m_dram = scratch("m_dram", [NH * T], F16)
    r_dram = scratch("r_dram", [NH * T])
    xd_dram = scratch("xd_dram", [2 * DS, T])

    with ExitStack() as outer:
        m = Space(nc, outer, "first")
        keep = Keep()
        keep.wkh, keep.wkl, keep.wvh, keep.wvl = (m.sb(n, [P, DC, NH * DH], F16) for n in ("wkh", "wkl", "wvh", "wvl"))
        keep.qz = [m.sb(f"qz{i}", [P, PAIRS, T], F16) for i in range(2)]
        keep.cf = [m.sb(f"cf{i}", [P, DC, CK]) for i in range(2)]
        keep.ch, keep.cl = ([m.sb(f"{n}{i}", [P, DC, CK], F16) for i in range(2)] for n in ("ch", "cl"))
        keep.bkc, keep.bks = m.sb("bkc", [P, PAIRS]), m.sb("bks", [P, PAIRS])
        latent_queries(nc, keep, x, wq, bq, wk, wv, bk, ctxT, q_dram)
        context_keys_values(nc, keep, ctxT, kd, vd, m_dram, wpack, wsplit)
    with ExitStack() as outer:
        m = Space(nc, outer, "keep")
        keep = Keep()
        keep.big = [m.sb(f"big{i}", [P, 4 * WC], F16) for i in range(2)]
        keep.heads = [b[:, :].bitcast(F32).rearrange("p (j t) -> p j t", t=T) for b in keep.big]
        attention(nc, keep, q_dram, m_dram, kd, vd, sums)
        keep.big += [m.sb(f"big{i}", [P, 4 * WC], F16) for i in (2, 3)]
        keep.x1, keep.a = m.sb("x1", [P, TT, D]), m.sb("a", [P, TT, D])
        keep.hidden = m.sb("hidden", [P, 2 * DC, T], F16)
        keep.hh, keep.hl = keep.hidden[:, 0:DC, :], keep.hidden[:, DC:2 * DC, :]
        gates = m.sb("gates", [P, TT, NX])
        project_attention(nc, keep, x, sums, r_dram, bv, bo, n1w, wsplit)
        with ExitStack() as inner:
            m = Space(nc, inner, "mamba")
            keep.xin, keep.zs, keep.delta = (m.sb(n, [P, DIC, T]) for n in ("xin", "zs", "delta"))
            keep.yh, keep.yl = (m.sb(n, [P, DIC, T], F16) for n in ("yh", "yl"))
            mamba_inputs(nc, keep, convw, convb, dtb, xd_dram, wsplit)
            with ExitStack() as output:
                keep.outl = Space(nc, output, "output").sb("outl", [P, DIC, D], F16)
                mamba_scan(nc, keep, a_log, dskip, xd_dram, wsplit)
                second_norm(nc, keep, n2w, wsplit)
        gated_mlp(nc, keep, wsplit, gate_up, down)
        route(nc, keep, gates, wsplit)
        experts(nc, keep, gates, gate_up, down, out)


def columns(v):
    return v.reshape(-1, P).T


def layout(inputs):
    a = {k: np.asarray(v) for k, v in inputs.items()}
    g = lambda n: a["L0_xattn_" + n]
    b = lambda n: a["L0_attn_" + n]
    f = lambda n: a["L0_ffn_" + n]

    def rows(w):
        return w.reshape(-1, P, w.shape[1]).transpose(1, 0, 2).reshape(P, -1)

    dtw = np.concatenate([b("dt_proj_w").T, np.zeros((P - DR, DI), np.float32)])
    small = np.concatenate([rows(b("x_proj_w").T), rows(f("router_w").T), dtw], axis=1)
    small = np.concatenate([small, np.zeros((P, WC - small.shape[1]), np.float32)], axis=1)
    packed = np.concatenate([rows(g("Wo")), rows(b("in_proj_w").T), rows(b("w1").T), rows(b("w3").T),
                             rows(b("w2").T), rows(b("out_proj_w").T), small], axis=1)
    packed = np.concatenate([packed, np.zeros((P, WT * WC - packed.shape[1]), np.float32)], axis=1)
    sg, su, sd = f("shared_gate_w").T, f("shared_up_w").T, f("shared_down_w").T
    shared = [np.concatenate([sg[:, h * EH:(h + 1) * EH], su[:, h * EH:(h + 1) * EH]], axis=1) for h in range(2)]
    gate_up = np.concatenate([f("gate_up_w").reshape(NE * D, 2 * EH)] + shared)
    down = np.concatenate([f("down_w").reshape(NE * EH, D), sd])
    out = dict(
        x=a["x"][0], ctxT=a["ctx_1024"][0].T, wq=g("Wq"), bq=columns(g("bq")), wk=g("Wk"), bk=columns(g("bk")),
        wv=g("Wv"), bv=columns(g("bv")), bo=g("bo"), n1w=columns(b("norm1_w")), n2w=columns(b("norm2_w")),
        convw=b("conv_w").reshape(DIC, P, 4).transpose(1, 0, 2), convb=columns(b("conv_b")),
        dtb=columns(b("dt_proj_b")), a_log=b("A_log").reshape(DIC, P, DS).transpose(1, 0, 2), dskip=columns(b("D")),
        wpack=packed.reshape(P, WT, WC).transpose(1, 0, 2), gate_up=gate_up, down=down)
    return {k: np.ascontiguousarray(v) for k, v in out.items()}


def kernel(**inputs):
    import concourse.bacc as bacc
    from concourse.bass_utils import run_bass_kernel_spmd

    nc = bacc.Bacc("TRN2", target_bir_lowering=False, num_devices=1)
    arrays = layout(inputs)
    args = [nc.dram_tensor(k, v.shape, mybir.dt.from_np(v.dtype), kind="ExternalInput").ap()
            for k, v in arrays.items()]
    out = nc.dram_tensor("out", [T, D], F32, kind="ExternalOutput").ap()
    program(nc, *args, out)
    result = run_bass_kernel_spmd(nc, [arrays], core_ids=[0])
    return result.results[0]["out"].reshape(1, T, D)
```
